# Optimizing a Trainium2 kernel written in Bass

```python
import numpy as np
import jax
import jax.numpy as jnp

def _softmax(x, axis=-1):
    return jax.nn.softmax(x, axis=axis)

def _gelu(x):
    return jax.nn.gelu(x, approximate=True)

def _silu(x):
    return jax.nn.silu(x)

def _sigmoid(x):
    return jax.nn.sigmoid(x)

def _layernorm(x, axis=-1, eps=1e-05):
    m = jnp.mean(x, axis=axis, keepdims=True)
    v = jnp.var(x, axis=axis, keepdims=True)
    return (x - m) / jnp.sqrt(v + eps)

def _scatter_add(tgt, idx, src, axis=0):
    return tgt.at[idx].add(src)

def _segment_sum(src, seg, n):
    return jax.ops.segment_sum(src, seg, n)
kernel_name = 'mk_gps_d1_gnn_r8_c06a70'

def setup_inputs(seed: int=0):
    np.random.seed(seed)
    _w = jnp.asarray

    def _rec_inputs():
        import jax
        import jax.numpy as jnp
        _gk = jax.random.key(seed)
        x = -0.0002117 + 1 * jax.random.normal(jax.random.fold_in(_gk, 1), (6250, 512), jnp.float32)
        src = jax.random.randint(jax.random.fold_in(_gk, 2), (100000,), 0, 6250, jnp.int32)
        dst = jnp.minimum((6250 * jax.random.uniform(jax.random.fold_in(_gk, 3), (100000,)) ** 2.0).astype(jnp.int32), 49999)
        _o = jnp.argsort(dst, stable=True)
        src = src[_o]
        dst = dst[_o]
        return (x, src, dst)
    x, src, dst = _rec_inputs()

    def _L0_gnn_setup():
        import jax, jax.numpy as jnp
        import numpy as np
        N = 6250
        E = 50000
        IN_FEATS = 512
        HEADS = 8
        OUT_FEATS = 64
        NEG_SLOPE = 0.2
        key = jax.random.key(seed)
        ks = jax.random.split(key, 12)
        HF = HEADS * OUT_FEATS
        s = 1.0 / np.sqrt(IN_FEATS)
        inp = {'feat': jax.random.normal(ks[0], (N, IN_FEATS), dtype=jnp.float32), 'src': jax.random.randint(ks[1], (E,), 0, N, dtype=jnp.int32), 'dst': jax.random.randint(ks[2], (E,), 0, N, dtype=jnp.int32), 'W_src': jax.random.normal(ks[3], (IN_FEATS, HF), dtype=jnp.float32) * s, 'b_src': jax.random.normal(ks[4], (HF,), dtype=jnp.float32) * 0.01, 'W_dst': jax.random.normal(ks[5], (IN_FEATS, HF), dtype=jnp.float32) * s, 'b_dst': jax.random.normal(ks[6], (HF,), dtype=jnp.float32) * 0.01, 'W_val': jax.random.normal(ks[7], (IN_FEATS, HF), dtype=jnp.float32) * s, 'b_val': jax.random.normal(ks[8], (HF,), dtype=jnp.float32) * 0.01, 'attn_l': jax.random.normal(ks[9], (HEADS, OUT_FEATS), dtype=jnp.float32) * 0.1, 'attn_r': jax.random.normal(ks[10], (HEADS, OUT_FEATS), dtype=jnp.float32) * 0.1}
        return inp
    _L0_gnn_all = _L0_gnn_setup()
    _L0_gnn_in = {k: v for k, v in _L0_gnn_all.items() if k in ('W_src', 'b_src', 'W_dst', 'b_dst', 'W_val', 'b_val', 'attn_l', 'attn_r')}
    del _L0_gnn_all

    def _L0_mix_setup():
        import jax, jax.numpy as jnp
        import numpy as np
        B, S, H = (4, 1024, 512)
        NH, HD = (8, 64)
        FD = HD // 2
        key = jax.random.key(seed)
        k1, k2, k3, k4 = jax.random.split(key, 4)
        x = jax.random.normal(k1, (B, S, H), dtype=jnp.float32)
        W_qkv = jax.random.normal(k2, (H, 3 * H), dtype=jnp.float32) * (1.0 / np.sqrt(H))
        random_matrix = jax.random.normal(k3, (HD, FD), dtype=jnp.float32) * (1.0 / np.sqrt(HD))
        W_out = jax.random.normal(k4, (H, H), dtype=jnp.float32) * (1.0 / np.sqrt(H))
        b_out = jnp.zeros((H,), dtype=jnp.float32)
        return {'x': x, 'W_qkv': W_qkv, 'random_matrix': random_matrix, 'W_out': W_out, 'b_out': b_out}
    _L0_mix_all = _L0_mix_setup()
    _L0_mix_in = {k: v for k, v in _L0_mix_all.items() if k in ('W_qkv', 'random_matrix', 'W_out', 'b_out')}
    del _L0_mix_all

    def _L0_ffn_setup():
        import jax, jax.numpy as jnp
        import numpy as np
        B, T, D, F, E, TOP_K = (8, 512, 512, 256, 8, 2)

        def _moe_forward(x, Wr, W1, W2):
            b, t, d = x.shape
            e = Wr.shape[1]
            xf = x.reshape(-1, d)
            n = xf.shape[0]
            logits = xf @ Wr
            probs = jax.nn.softmax(logits, axis=-1)
            w, idx = jax.lax.top_k(probs, TOP_K)
            w = w.astype(xf.dtype)
            gates = jnp.zeros((n, e), xf.dtype).at[jnp.arange(n)[:, None], idx].add(w)

            def body(acc, expert):
                w1, w2, g = expert
                h = jax.nn.gelu(xf @ w1, approximate=False)
                return (acc + g[:, None] * (h @ w2), None)
            out, _ = jax.lax.scan(body, jnp.zeros_like(xf), (W1, W2, gates.T))
            return out.reshape(b, t, d)
        key = jax.random.key(seed)
        k1, k2, k3, k4 = jax.random.split(key, 4)
        x = jax.random.normal(k1, (B, T, D), jnp.float32)
        Wr = jax.random.normal(k2, (D, E), jnp.float32) * (1.0 / np.sqrt(D))
        W1 = jax.random.normal(k3, (E, D, F), jnp.float32) * (1.0 / np.sqrt(D))
        W2 = jax.random.normal(k4, (E, F, D), jnp.float32) * (1.0 / np.sqrt(F))
        return {'x': x, 'Wr': Wr, 'W1': W1, 'W2': W2}
    _L0_ffn_all = _L0_ffn_setup()
    _L0_ffn_in = {k: v for k, v in _L0_ffn_all.items() if k in ('Wr', 'W1', 'W2')}
    del _L0_ffn_all
    return {'x': x, 'src': src, 'dst': dst, 'L0_gnn_W_src': _L0_gnn_in['W_src'], 'L0_gnn_b_src': _L0_gnn_in['b_src'], 'L0_gnn_W_dst': _L0_gnn_in['W_dst'], 'L0_gnn_b_dst': _L0_gnn_in['b_dst'], 'L0_gnn_W_val': _L0_gnn_in['W_val'], 'L0_gnn_b_val': _L0_gnn_in['b_val'], 'L0_gnn_attn_l': _L0_gnn_in['attn_l'], 'L0_gnn_attn_r': _L0_gnn_in['attn_r'], 'L0_mix_W_qkv': _L0_mix_in['W_qkv'], 'L0_mix_random_matrix': _L0_mix_in['random_matrix'], 'L0_mix_W_out': _L0_mix_in['W_out'], 'L0_mix_b_out': _L0_mix_in['b_out'], 'L0_ffn_Wr': _L0_ffn_in['Wr'], 'L0_ffn_W1': _L0_ffn_in['W1'], 'L0_ffn_W2': _L0_ffn_in['W2']}

def reference(x, src, dst, L0_gnn_W_src, L0_gnn_b_src, L0_gnn_W_dst, L0_gnn_b_dst, L0_gnn_W_val, L0_gnn_b_val, L0_gnn_attn_l, L0_gnn_attn_r, L0_mix_W_qkv, L0_mix_random_matrix, L0_mix_W_out, L0_mix_b_out, L0_ffn_Wr, L0_ffn_W1, L0_ffn_W2):
    import jax
    import jax.numpy as jnp

    def _L0_gnn_ref(feat, src, dst, W_src, b_src, W_dst, b_dst, W_val, b_val, attn_l, attn_r):
        import jax, jax.numpy as jnp
        import numpy as np
        N = 6250
        E = 50000
        IN_FEATS = 512
        HEADS = 8
        OUT_FEATS = 64
        NEG_SLOPE = 0.2
        feat_src = (feat @ W_src + b_src).reshape(N, HEADS, OUT_FEATS)
        feat_dst = (feat @ W_dst + b_dst).reshape(N, HEADS, OUT_FEATS)
        feat_v = (feat @ W_val + b_val).reshape(N, HEADS, OUT_FEATS)
        el = jnp.einsum('nhf,hf->nh', feat_src, attn_l)
        er = jnp.einsum('nhf,hf->nh', feat_dst, attn_r)
        e = el[src] + er[dst]
        e = jnp.where(e >= 0, e, NEG_SLOPE * e)
        e_max = jax.ops.segment_max(e, dst, num_segments=N)
        e_max = jnp.where(jnp.isfinite(e_max), e_max, 0.0)
        exp_e = jnp.exp(e - e_max[dst])
        denom = jax.ops.segment_sum(exp_e, dst, num_segments=N)
        a = exp_e / jnp.maximum(denom[dst], 1e-16)
        msg = feat_v[src] * a[:, :, None]
        rst = jax.ops.segment_sum(msg, dst, num_segments=N)
        return rst.reshape(N, HEADS * OUT_FEATS)

    def _L0_mix_ref(x, W_qkv, random_matrix, W_out, b_out):
        import jax, jax.numpy as jnp
        import numpy as np
        B, S, H = (4, 1024, 512)
        NH, HD = (8, 64)
        FD = HD // 2
        b, s, h = x.shape
        qkv = (x @ W_qkv).reshape(b, s, 3, NH, HD)
        q, k, v = (qkv[:, :, 0], qkv[:, :, 1], qkv[:, :, 2])
        q_prime = jax.nn.elu(q @ random_matrix) + 1.0
        k_prime = jax.nn.elu(k @ random_matrix) + 1.0
        kv = jnp.einsum('bshd,bshf->bhdf', k_prime, v)
        z = jnp.einsum('bshd,bhdf->bshf', q_prime, kv)
        normalizer = jnp.einsum('bshd,bhd->bsh', q_prime, k_prime.sum(axis=1))
        z = z / (normalizer[..., None] + 1e-06)
        z = z.reshape(b, s, h)
        return z @ W_out + b_out

    def _L0_ffn_ref(x, Wr, W1, W2):
        import jax, jax.numpy as jnp
        import numpy as np
        B, T, D, F, E, TOP_K = (8, 512, 512, 256, 8, 2)

        def _moe_forward(x, Wr, W1, W2):
            b, t, d = x.shape
            e = Wr.shape[1]
            xf = x.reshape(-1, d)
            n = xf.shape[0]
            logits = xf @ Wr
            probs = jax.nn.softmax(logits, axis=-1)
            w, idx = jax.lax.top_k(probs, TOP_K)
            w = w.astype(xf.dtype)
            gates = jnp.zeros((n, e), xf.dtype).at[jnp.arange(n)[:, None], idx].add(w)

            def body(acc, expert):
                w1, w2, g = expert
                h = jax.nn.gelu(xf @ w1, approximate=False)
                return (acc + g[:, None] * (h @ w2), None)
            out, _ = jax.lax.scan(body, jnp.zeros_like(xf), (W1, W2, gates.T))
            return out.reshape(b, t, d)
        return _moe_forward(x, Wr, W1, W2)
    xn = _layernorm(x, axis=-1)
    x = x + _L0_gnn_ref(xn, src, dst, L0_gnn_W_src, L0_gnn_b_src, L0_gnn_W_dst, L0_gnn_b_dst, L0_gnn_W_val, L0_gnn_b_val, L0_gnn_attn_l, L0_gnn_attn_r) + _L0_mix_ref(xn[None], L0_mix_W_qkv, L0_mix_random_matrix, L0_mix_W_out, L0_mix_b_out)[0]
    x = x + _L0_ffn_ref(_layernorm(x, axis=-1)[None], L0_ffn_Wr, L0_ffn_W1, L0_ffn_W2)[0]
    return x

_drawn_inputs = setup_inputs


def setup_inputs(seed=0):
    import zlib

    import numpy as np

    out = dict(_drawn_inputs(seed))
    spreads = {'L0_mix_b_out': (0.0, 0.1)}
    factors = {'L0_gnn_b_src': 51.017,
     'L0_gnn_b_dst': 44.276,
     'L0_gnn_b_val': 3.458,
     'L0_mix_random_matrix': 4.055,
     'L0_mix_W_out': 2.674}
    for name, (base, spread) in spreads.items():
        noise = np.random.default_rng([zlib.crc32(name.encode()), seed]).standard_normal(out[name].shape)
        drawn = base * np.exp(spread * noise) if base else spread * noise
        out[name] = jnp.asarray(drawn.astype(out[name].dtype))
    for name, factor in factors.items():
        out[name] = (out[name] * factor).astype(out[name].dtype)
    return out
```

```python
from contextlib import ExitStack

import numpy as np

import concourse.bass as bass
from concourse import mybir

F32 = mybir.dt.float32
I32 = mybir.dt.int32
U16 = mybir.dt.uint16
U32 = mybir.dt.uint32
BF16 = mybir.dt.bfloat16
ALU = mybir.AluOpType
ACT = mybir.ActivationFunctionType
AX = mybir.AxisListType

P = 128
N, D, E = 6250, 512, 100000
H, HF = 8, 64
HD = 32
X, XF = 8, 256
KC = D // P
NT = -(-N // P)
NP = NT * P
CH = 16
CJ = -(-E // (P * CH))
ET = CH * CJ
EP = ET * P
CL = CJ * P
ST = ET + NT - 1
BIG = 1.0e30
ROUND = 1.5 * 2.0 ** 23
NEG_SLOPE = 0.2
LN_EPS = 1e-5
U = 16
SETUP_DMAS, WEIGHT_DMAS, EXPERT_DMAS = 9, 8, 6
assert ST % U == 0 and NT % 2 == 1

SEMAPHORES = (
    "dst_scan_in", "dst_stepped", "el_idx", "el_in0", "el_in1", "el_kept", "el_stored", "ends_tp",
    "er_add", "er_hot", "er_hot_t", "er_mm", "er_split", "er_tp", "ex_exp", "ex_g", "ex_gelu",
    "ex_hmm", "ex_hs", "ex_ht", "ex_htp", "ex_lg", "ex_nmax", "ex_out", "ex_st0", "ex_st1", "ex_tp",
    "ex_x0", "ex_x1", "ex_xn", "ex_xt", "ex_ymm", "experts_in", "fin_st0", "fin_st1", "fold_mm",
    "fold_out", "fold_v", "g_in", "g_mm", "g_out", "ident_ready", "jn_1", "jn_2", "jn_3", "jn_a0",
    "jn_a1", "jn_ag", "jn_aggr", "jn_b0", "jn_b1", "jn_bn", "jn_rstd", "jn_sqrt", "jn_st0",
    "jn_st1", "jn_var", "jn_x", "mx_mm", "mx_n1", "mx_n2", "mx_norm", "mx_out", "mx_qn", "mx_st0",
    "mx_st1", "mx_x0", "mx_x1", "mx_xb", "p_ready", "p_row", "p_set", "pj_k", "pj_kexp", "pj_kf",
    "pj_kmin", "pj_kv", "pj_kva", "pj_mv", "pj_mvs", "pj_q", "pj_qexp", "pj_qf", "pj_qmin",
    "pj_st0", "pj_st1", "pj_tp", "pj_v", "pj_vout", "pj_x0", "pj_x1", "pj_xn", "pj_xt", "r_zeroed",
    "row_back", "row_in", "row_v", "sc_mm", "sc_out", "sc_tp", "sc_x0", "sc_x1", "sc_xn", "sc_xt",
    "scan_done", "scan_ends", "scan_v", "setup_in", "sm", "sm_diff", "src_stepped", "st_agg",
    "st_kept", "st_rstd", "st_seen", "st_sqrt", "st_var", "st_x0", "st_x1", "step_idx", "step_mm",
    "step_pv", "tab_begun", "tab_d", "tab_k", "tab_mm", "tab_ready", "tile_out", "tile_sum",
    "tp_el", "tp_el_out", "tp_m", "tp_m_out", "v_set", "weights_in")


def turns(eng, body, n=NT, u=2):
    for j in range(u):
        body(j, j, 0)
    with eng.Fori(1, n // u) as i:
        for j in range(u):
            body(i * u + j, j, i)
    for t in range(n // u * u, n):
        body(t, t % u, t // u)


def wait_past(eng, sem, t, lag):
    if not isinstance(t, int) or t >= lag:
        eng.wait_ge(sem, t + (1 - lag))


def later(t, lag):
    return not isinstance(t, int) or t >= lag


def gps_layer(nc, x, src_cols, dst_cols, dst_rows, w_src, b_src, w_dst, b_dst, w_val, b_val, attn_l,
              attn_r, w_qk_t, w_v, r_mat, w_out, b_out, w_r, w_1, w_2, out):
    el_table = nc.dram_tensor("el_table", (NP, H), F32, kind="Internal").ap()
    v_table = nc.dram_tensor("v_table", (NP, D), F32, kind="Internal").ap()
    x_mix = nc.dram_tensor("x_mix", (NP, D), F32, kind="Internal").ap()
    agg = nc.dram_tensor("agg", (NP, D + H), F32, kind="Internal").ap()
    x_mid = nc.dram_tensor("x_mid", (NP, D), F32, kind="Internal").ap()

    def rows(dram, t):
        return dram[bass.ds(t * P, P), :]

    with ExitStack() as ctx:
        def sb(name, shape, dt=F32):
            return ctx.enter_context(nc.sbuf_tensor(name, shape, dt))

        def sem(name):
            return ctx.enter_context(nc.semaphore(name))

        ident = sb("ident", [P, P])
        ident_b = sb("ident_b", [P, P], BF16)
        col_no = sb("col_no", [P, P])
        ones = sb("ones", [P, P])
        zeros = sb("zeros", [1, D])
        src_of = sb("src_of", [P, ET], I32)
        dst_of = sb("dst_of", [P, ET], I32)
        dst_f = sb("dst_f", [P, ET])
        dst_local = sb("dst_local", [P, ST])
        src_step = sb("src_step", [P, ST], I32)
        el_er = sb("el_er", [P, NT, 2 * H])
        er_parts = sb("er_parts", [P, NT, 3, H], BF16)
        er_rest = sb("er_rest", [P, NT, H])
        k_tab = sb("k_tab", [1, ST], U16)
        d_tab = sb("d_tab", [1, ST], U16)
        turn_tab = sb("turn_tab", [1, ST], U16)
        real_row = sb("real_row", [P, NT])
        mean_var = sb("mean_var", [P, NT, 2])
        rstd = sb("rstd", [P, NT])
        small = sb("small", [P, 64])

        ARENA = 41400
        arena = sb("arena", [P, ARENA])

        def at(off, *shape, dt=None):
            n = int(np.prod(shape))
            assert off + n <= ARENA, (off, shape)
            v = arena[:, off:off + n]
            if dt is not None:
                v = v.bitcast(dt)
            if len(shape) == 2:
                v = v.rearrange("p (a b) -> p a b", a=shape[0])
            elif len(shape) == 3:
                v = v.rearrange("p (a b c) -> p a b c", a=shape[0], b=shape[1])
            return v

        t_el = at(0, CL)
        t_pen = at(CL, CL + 1)
        t_run = at(2 * CL + 2, CL)
        q_feat = at(0, 2, NP)
        e_el = at(3 * CL + 4, ET, H)
        o = 3 * CL + 4 + ET * H
        ph_a = o
        wv = at(o, KC, D); o += KC * D
        wmv = at(o, KC, D); o += KC * D
        wqk = at(o, KC, D); o += KC * D
        wo = at(o, KC, D); o += KC * D
        e_er = at(ph_a, ET, H)
        bv_all = at(o, D); o += D
        bo_all = at(o, D); o += D
        wlr = at(o, KC, 2 * H); o += KC * 2 * H
        blr = at(o, 2 * H); o += 2 * H
        at_acc = at(o, KC * HF + 2)
        kvt_acc = at(o, KC, HF); o += KC * HF
        ks_acc = at(o, 2); o += 2
        r_diag = at(o, HF); o += HF
        g_mat = at(o, 2, D); o += 2 * D
        kvt_diag = at(o, KC, P); o += KC * P
        ks_diag = at(o, 2, P); o += 2 * P
        xs = at(o, 2, D); o += 2 * D
        xn = at(o, D); o += D
        xt = at(o, 2, D); o += 2 * D
        vs = at(o, 2, D); o += 2 * D
        mv = at(o, D); o += D
        kf = at(o, 2 * P); o += 2 * P
        ex = at(o, 2, 2 * P); o += 4 * P
        assert o <= ARENA, o
        s_w = at(0, KC, D)
        s_w2 = at(2048, KC, D)
        s_al = at(4096, D)
        s_ar = at(4608, D)
        s_bs = at(5120, D)
        s_bd = at(5632, D)
        s_tmp = at(6144, KC, D)
        s_wqt = at(8192, 8, D)
        s_cnt = at(12288, ST)
        s_d = at(13200, ST)
        s_io = at(14200, ST)
        s_last = at(15200, ET)
        d128 = sb("d128", [P, ST])

        qn = [kf.rearrange("p (c t) -> p c t", c=2), ex[:, 1, :].rearrange("p (c t) -> p c t", c=2)]
        o = 0
        vg = at(o, U, D); o += U * D
        pv = at(o, 2, D + H); o += 2 * (D + H)
        hot = at(o, 2, P); o += 2 * P
        fin = at(o, 2, D + H); o += 2 * (D + H)
        assert o <= 2 * CL
        o = 0
        w1 = at(o, KC, X * XF); o += KC * X * XF
        w2 = at(o, 2 * X, D); o += 2 * X * D
        wr = at(o, KC, X); o += KC * X
        da = at(o, 2, D + H); o += 2 * (D + H)
        db = at(o, 2, D); o += 2 * D
        dx = at(o, 2, D); o += 2 * D
        dn = at(o, D); o += D
        dt_ = at(o, 2, D); o += 2 * D
        hs = at(o, 2, D); o += 2 * D
        ht = at(o, 2, D); o += 2 * D
        dy = at(o, 2, D); o += 2 * D
        assert o <= ARENA
        hot_b = sb("hot_b", [P, 2, P], BF16)
        hot_t = sb("hot_t", [P, 2, P], BF16)
        idx = sb("idx", [P, U], I32)
        idx_el = sb("idx_el", [P, 2, CH], I32)
        got_el = sb("got_el", [P, 2, CH, H])
        thr = sb("thr", [P, 1])
        bn = sb("bn", [P, 6])
        ag = sb("ag", [P, 2])
        den = sb("den", [P, H])
        row = at(ph_a + ET * H, 12, P)
        edge_first = sb("edge_first", [P, 4])
        col = sb("col", [P, 2])
        lg = sb("lg", [P, 8])
        top = sb("top", [P, 8])
        nmax = sb("nmax", [P, 1])
        pr = sb("pr", [P, 8])
        psum_ = sb("psum_", [P, 1])
        ptop = sb("ptop", [P, 8])
        pidx = sb("pidx", [P, 8], U32)
        pidf = sb("pidf", [P, 8])
        ga = sb("ga", [P, 8])
        gb = sb("gb", [P, 8])
        gate = sb("gate", [P, 2, 8])
        e_m = at(2 * CL + 2, ET, H)
        dst_scan = at(2 * CL + 2, CL, dt=I32)
        mv_flat = mean_var[:].rearrange("p t a -> p (t a)")
        el_er_flat = el_er[:].rearrange("p t a -> p (t a)")
        er_flat = er_parts[:].rearrange("p t i h -> p (t i h)")
        e_er_flat = e_er.rearrange("p k h -> p (k h)")
        e_el_flat = e_el.rearrange("p k h -> p (k h)")

        bank = [ctx.enter_context(nc.psum_tensor(f"bank{i}", [P, D], F32)) for i in range(7)]
        bank_b = ctx.enter_context(nc.psum_tensor("bank_b", [P, 2 * D], BF16))
        sems = {}

        def s(name):
            if name not in sems:
                sems[name] = sem(name)
            return sems[name]

        gathered = [sem(f"rows_gathered{j}") for j in range(U)]
        for name in SEMAPHORES:
            s(name)
        block = ctx.enter_context(nc.Block())

        def apart(eng, sem_, value):
            if not isinstance(value, int):
                value = eng.to_reg(value)
                eng.wait_ge(s("p_set"), 1)
            eng.wait_ge(sem_, value)

        def by_chunk(w):
            return w.rearrange("(c p) n -> p c n", p=P)

        def bcast(row_ap):
            return row_ap.broadcast_to([P, row_ap.shape[-1]])

        @block.sync
        def _(sp):
            for dst, src in ((src_of[:], src_cols), (dst_of[:], dst_cols), (s_w, by_chunk(w_src)),
                             (s_w2, by_chunk(w_dst)), (s_al, bcast(attn_l)), (s_ar, bcast(attn_r)),
                             (s_bs, bcast(b_src)), (s_bd, bcast(b_dst)),
                             (s_last[0:NT - 1, :].bitcast(I32), dst_cols[P - 1:P, :].broadcast_to([NT - 1, ET]))):
                sp.dma_start(dst, src).then_inc(s("setup_in"), 16)

            def stats(t, slot, r):
                wait_past(sp, s("st_seen"), t, 2)
                sp.dma_start(xs[:, slot, :], rows(x, t)).then_inc(s(f"st_x{slot}"), 16)
            turns(sp, stats)
            sp.wait_ge(s("r_zeroed"), 1)
            for dst, src in ((r_diag[0:HF, 0:HD], r_mat), (r_diag[HF:P, HD:2 * HD], r_mat),
                             (s_wqt, by_chunk(w_qk_t)), (wv, by_chunk(w_val)), (wmv, by_chunk(w_v)),
                             (wo, by_chunk(w_out)), (bv_all, bcast(b_val)), (bo_all, bcast(b_out))):
                sp.dma_start(dst, src).then_inc(s("weights_in"), 16)

            sp.wait_ge(s("st_seen"), NT)

            def scores(t, slot, r):
                wait_past(sp, s("sc_xn"), t, 2)
                sp.dma_start(xs[:, slot, :], rows(x, t)).then_inc(s(f"sc_x{slot}"), 16)
            turns(sp, scores)
            sp.wait_ge(s("sc_out"), NT)
            sp.dma_start(el_table.rearrange("(t p) h -> p t h", p=P), el_er[:, :, 0:H]).then_inc(s("el_stored"), 16)

            def proj(t, slot, r):
                wait_past(sp, s("pj_xn"), t, 2)
                sp.dma_start(xs[:, slot, :], rows(x, t)).then_inc(s(f"pj_x{slot}"), 16)
                if later(t, 1):
                    sp.wait_ge(s("pj_vout"), t)
                    sp.dma_start(rows(v_table, t - 1), vs[:, 1 - slot, :]).then_inc(s(f"pj_st{1 - slot}"), 16)
            turns(sp, proj)
            sp.wait_ge(s("pj_vout"), NT)
            sp.dma_start(rows(v_table, NT - 1), vs[:, (NT - 1) % 2, :]).then_inc(s("pj_st0"), 16)

            sp.wait_ge(s("pj_xn"), NT)

            def mix(t, slot, r):
                wait_past(sp, s("mx_xb"), t, 2)
                sp.dma_start(xs[:, slot, :], rows(x, t)).then_inc(s(f"mx_x{slot}"), 16)
                if later(t, 1):
                    sp.wait_ge(s("mx_out"), t)
                    sp.dma_start(rows(x_mix, t - 1), vs[:, 1 - slot, :]).then_inc(s(f"mx_st{1 - slot}"), 16)
            turns(sp, mix)
            sp.wait_ge(s("mx_out"), NT)
            sp.dma_start(rows(x_mix, NT - 1), vs[:, (NT - 1) % 2, :]).then_inc(s("mx_st0"), 16)

            for c in range(CH):
                sp.dma_start(dst_scan[c * H:(c + 1) * H, :], dst_rows[c:c + 1, :].broadcast_to([H, CL]))\
                  .then_inc(s("dst_scan_in"), 16)

            sp.wait_ge(s("fin_st0"), 16 * (NT // 2 + 1))
            sp.wait_ge(s("fin_st1"), 16 * (NT // 2))
            sp.wait_ge(s("mx_st0"), 16 * (NT // 2 + 1))
            sp.wait_ge(s("mx_st1"), 16 * (NT // 2))
            sp.wait_ge(s("step_mm"), ST)
            for dst, src in ((wr, by_chunk(w_r)), (w1.rearrange("p c (e f) -> p c e f", e=X)[:, 0], w_1[:, 0:P, :].rearrange("e p f -> p e f")),
                             (w1.rearrange("p c (e f) -> p c e f", e=X)[:, 1], w_1[:, P:2 * P, :].rearrange("e p f -> p e f")),
                             (w1.rearrange("p c (e f) -> p c e f", e=X)[:, 2], w_1[:, 2 * P:3 * P, :].rearrange("e p f -> p e f")),
                             (w1.rearrange("p c (e f) -> p c e f", e=X)[:, 3], w_1[:, 3 * P:4 * P, :].rearrange("e p f -> p e f")),
                             (w2, w_2.rearrange("e (c p) n -> p (e c) n", p=P))):
                sp.dma_start(dst, src).then_inc(s("experts_in"), 16)

            def join(t, slot, r):
                wait_past(sp, s("jn_x"), t, 2)
                sp.dma_start(da[:, slot, :], rows(agg, t)).then_inc(s(f"jn_a{slot}"), 16)
                sp.dma_start(db[:, slot, :], rows(x_mix, t)).then_inc(s(f"jn_b{slot}"), 16)
                if later(t, 1):
                    sp.wait_ge(s("jn_x"), t)
                    sp.dma_start(rows(x_mid, t - 1), dx[:, 1 - slot, :]).then_inc(s(f"jn_st{1 - slot}"), 16)
            turns(sp, join)
            sp.wait_ge(s("jn_x"), NT)
            sp.dma_start(rows(x_mid, NT - 1), dx[:, 0, :]).then_inc(s("jn_st0"), 16)
            sp.wait_ge(s("jn_st0"), 16 * (NT // 2 + 1))
            sp.wait_ge(s("jn_st1"), 16 * (NT // 2))
            sp.wait_ge(s("jn_aggr"), NT)

            def moe(t, slot, r):
                wait_past(sp, s("ex_out"), t, 2)
                sp.dma_start(dx[:, slot, :], rows(x_mid, t)).then_inc(s(f"ex_x{slot}"), 16)
                if later(t, 1):
                    sp.wait_ge(s("ex_out"), t)
                    sp.dma_start(rows(out, t - 1), dy[:, 1 - slot, :]).then_inc(s(f"ex_st{1 - slot}"), 16)
            turns(sp, moe)
            sp.wait_ge(s("ex_out"), NT)
            sp.dma_start(rows(out, NT - 1), dy[:, 0, :]).then_inc(s("ex_st0"), 16)
            sp.wait_ge(s("ex_st0"), 16 * (NT // 2 + 1))
            sp.wait_ge(s("ex_st1"), 16 * (NT // 2))

        @block.gpsimd
        def _(pool):
            kw = dict(allow_small_or_imprecise_dtypes=True)
            pool.memset(ident[:], 0.0).then_inc(s("p_set"), 1)
            pool.memset(ones[:], 1.0).then_inc(s("p_set"), 1)
            pool.memset(zeros[:], 0.0).then_inc(s("p_set"), 1)
            pool.wait_ge(s("p_set"), 1)
            pool.affine_select(out=ident[:], in_=ident[:], compare_op=ALU.not_equal, fill=1.0, base=0,
                               pattern=[[-1, P]], channel_multiplier=1).then_inc(s("p_set"), 1)
            pool.iota(col_no[:], [[1, P]], base=0, channel_multiplier=0, **kw).then_inc(s("p_set"), 1)
            pool.iota(thr[:], [[0, 1]], base=P, channel_multiplier=P, **kw).then_inc(s("p_set"), 1)
            pool.iota(s_io, [[1, ST]], base=0, channel_multiplier=0, **kw).then_inc(s("p_set"), 1)
            pool.iota(real_row[:], [[P, NT]], base=0, channel_multiplier=1, **kw).then_inc(s("p_row"), 1)
            pool.wait_ge(s("p_row"), 1)
            pool.tensor_scalar(real_row[:], real_row[:], float(N), None, ALU.is_lt).then_inc(s("p_set"), 1)
            pool.memset(r_diag, 0.0).then_inc(s("r_zeroed"), 1)
            pool.memset(kvt_diag, 0.0).then_inc(s("p_set"), 1)
            pool.memset(ks_diag, 0.0).then_inc(s("p_set"), 1)
            pool.memset(at_acc, 0.0).then_inc(s("p_set"), 1)
            pool.wait_ge(s("setup_in"), SETUP_DMAS * 16)
            pool.wait_ge(s("el_stored"), 16)

            def keep(t, slot, r):
                pool.wait_ge(s(f"el_in{slot}"), (r + 1) * (16 * CH))
                pool.tensor_copy(e_el_flat[:, bass.ds(t * P, P)], got_el[:, slot].rearrange("p c h -> p (c h)"))\
                    .then_inc(s("el_kept"), 1)

            def gather(t, slot, r):
                wait_past(pool, s("el_kept"), t, 2)
                pool.tensor_copy(idx_el[:, slot, :], src_of[:, bass.ds(t * CH, CH)])\
                    .then_inc(s("el_idx"), 1)
                apart(pool, s("el_idx"), t + 1)
                for c in range(CH):
                    pool.indirect_dma_start(got_el[:, slot, c, :], None, el_table,
                                            bass.IndirectOffsetOnAxis(ap=idx_el[:, slot, c:c + 1], axis=0))\
                        .then_inc(s(f"el_in{slot}"), 16)
                if later(t, 1):
                    keep(t - 1, 1 - slot, (r - 1 if slot == 0 else r))
            turns(pool, gather, CJ)
            keep(CJ - 1, (CJ - 1) % 2, (CJ - 1) // 2)

            for name, n in (("pj_st0", NT // 2 + 1), ("pj_st1", NT // 2), ("mx_st0", NT // 2 + 1), ("mx_st1", NT // 2)):
                pool.wait_ge(s(name), 16 * n)
            pool.wait_ge(s("src_stepped"), ST)
            pool.wait_ge(s("p_ready"), 1)

            def values(t, j, r):
                if j % 8 == 0:
                    wait_past(pool, s("step_pv"), t, 9)
                    pool.tensor_copy(idx[:, j:j + 8], src_step[:, bass.ds(t, 8)]).then_inc(s("step_idx"), 1)
                    apart(pool, s("step_idx"), r * (U // 8) + (j // 8 + 1))
                if later(t, U):
                    apart(pool, s("step_pv"), t + (1 - U))
                pool.indirect_dma_start(vg[:, j, :], None, v_table,
                                        bass.IndirectOffsetOnAxis(ap=idx[:, j:j + 1], axis=0))\
                    .then_inc(gathered[j], 16)
            turns(pool, values, ST, U)

        @block.scalar
        def _(act):
            act.wait_ge(s("fold_mm"), KC)
            for c in range(KC):
                act.activation(wqk[:, c, :], bank[c][:], ACT.Copy).then_inc(s("fold_out"), 1)
            act.wait_ge(s("st_var"), 1)
            act.activation(rstd[:], rstd[:], ACT.Sqrt).then_inc(s("st_sqrt"), 1)

            def scores(t, slot, r):
                act.wait_ge(s("sc_tp"), t + 1)
                wait_past(act, s("sc_mm"), t, 2)
                act.activation(xt[:, slot, :], bank[slot][:], ACT.Copy).then_inc(s("sc_xt"), 1)
            turns(act, scores)
            act.wait_ge(s("sc_mm"), NT)

            def proj(t, slot, r):
                act.wait_ge(s("pj_tp"), t + 1)
                wait_past(act, s("pj_q"), t, 2)
                act.activation(xt[:, slot, :], bank[slot][:], ACT.Copy).then_inc(s("pj_xt"), 1)
                act.wait_ge(s("pj_mv"), t + 1)
                act.activation(mv, bank[3][:], ACT.Copy).then_inc(s("pj_mvs"), 1)
                act.wait_ge(s("pj_kmin"), t + 1)
                act.activation(ex[:, 0, :], ex[:, 0, :], ACT.Exp).then_inc(s("pj_kexp"), 1)
                act.wait_ge(s("pj_qmin"), t + 1)
                act.activation(ex[:, 1, :], ex[:, 1, :], ACT.Exp).then_inc(s("pj_qexp"), 1)
            turns(act, proj)
            act.wait_ge(s("g_mm"), 1)
            for c in range(2):
                act.activation(g_mat[:, c, :], bank[c][:], ACT.Copy).then_inc(s("g_out"), 1)

            def expand(t, slot, r):
                k = act.value_load(k_tab[0:1, bass.ds(t, 1)], min_val=0, max_val=ET - 1)
                act.activation(src_step[:, bass.ds(t, 1)], src_of[:, bass.ds(k, 1)], ACT.Copy).then_inc(s("src_stepped"), 1)
                act.wait_ge(s("er_tp"), t + 1)
                wait_past(act, s("er_mm"), t, 2)
                act.activation(hot_t[:, slot, :], bank_b[:, slot * D:slot * D + P], ACT.Copy).then_inc(s("er_hot_t"), 1)
            turns(act, expand, ST)

            for g in range(-(-CJ // 4)):
                n = min(4, CJ - 4 * g)
                act.wait_ge(s("tp_el"), g + 1)
                act.activation(t_el[:, g * D:g * D + n * P], bank[g % 4][:, 0:n * P], ACT.Copy).then_inc(s("tp_el_out"), 1)
            m_flat = e_m.rearrange("p k h -> p (k h)")
            for g in range(-(-CJ // 4)):
                n = min(4, CJ - 4 * g)
                act.wait_ge(s("tp_m"), g + 1)
                act.activation(m_flat[:, 4 * g * P:(4 * g + n) * P], bank[g % 4][:, 0:n * P], ACT.Copy).then_inc(s("tp_m_out"), 1)
            act.wait_ge(s("sm_diff"), 1)
            act.activation(e_el, e_el, ACT.Exp).then_inc(s("p_ready"), 1)

            def finish(t, slot, r):
                act.wait_ge(s("tile_sum"), t + 1)
                if later(t, 2):
                    act.wait_ge(s(f"fin_st{slot}"), r * 16)
                act.activation(fin[:, slot, 0:D], bank[0][:], ACT.Copy)
                act.activation(fin[:, slot, D:D + H], bank[1][:, 0:H], ACT.Copy).then_inc(s("tile_out"), 1)
                act.wait_ge(s("tile_out"), t + 1)
                act.dma_start(rows(agg, t), fin[:, slot, :]).then_inc(s(f"fin_st{slot}"), 16)
            turns(act, finish)

            act.wait_ge(s("jn_var"), 1)
            act.activation(rstd[:], rstd[:], ACT.Sqrt).then_inc(s("jn_sqrt"), 1)

            def moe(t, slot, r):
                act.wait_ge(s("ex_tp"), t + 1)
                if later(t, 2):
                    act.wait_ge(s("ex_hmm"), 4 * t - 4)
                act.activation(dt_[:, slot, :], bank[slot][:], ACT.Copy).then_inc(s("ex_xt"), 1)
                act.wait_ge(s("ex_nmax"), t + 1)
                act.activation(pr[:], lg[:], ACT.Exp, bias=nmax[:], accum_out=psum_[:]).then_inc(s("ex_exp"), 1)
                for q in range(4):
                    act.wait_ge(s("ex_hmm"), 4 * t + (q + 1))
                    if q >= 2 or later(t, 1):
                        act.wait_ge(s("ex_htp"), 4 * t + (q - 1))
                    act.activation(hs[:, q % 2, :], bank[2 + q % 2][:], ACT.Gelu).then_inc(s("ex_gelu"), 1)
            turns(act, moe)

        @block.vector
        def _(dve):
            dve.wait_ge(s("p_set"), 11)
            dve.tensor_copy(ident_b[:], ident[:]).then_inc(s("ident_ready"), 1)
            dve.memset(mean_var[:], 0.0).then_inc(s("v_set"), 1)
            dve.wait_ge(s("setup_in"), SETUP_DMAS * 16)
            dve.tensor_copy(dst_f[:], dst_of[:]).then_inc(s("v_set"), 1)
            R_ = NT - 1
            dve.tensor_copy(s_last[0:R_, :], s_last[0:R_, :].bitcast(I32)).then_inc(s("v_set"), 1)
            dve.wait_ge(s("v_set"), 3)
            dve.tensor_scalar(s_d[0:R_, 0:ET], s_last[0:R_, :], thr[0:R_, :], None, ALU.is_lt).then_inc(s("v_set"), 1)
            dve.wait_ge(s("v_set"), 4)
            dve.tensor_reduce(small[0:R_, 0:1], s_d[0:R_, 0:ET], AX.X, ALU.add).then_inc(s("v_set"), 1)
            dve.wait_ge(s("v_set"), 5)
            dve.scalar_tensor_tensor(small[0:R_, 1:2], thr[0:R_, :], 1.0 / P, small[0:R_, 0:1], ALU.mult, ALU.add)\
                .then_inc(s("v_set"), 1)
            dve.wait_ge(s("v_set"), 6)
            dve.tensor_scalar(s_cnt[0:R_, :], s_io[0:R_, :], small[0:R_, 1:2], None, ALU.is_ge).then_inc(s("tab_begun"), 1)
            n = 0
            for w, a, b, lo in ((s_w, s_al, s_bs, 0), (s_w2, s_ar, s_bd, H)):
                for c in range(KC):
                    dve.tensor_tensor(s_tmp[:, c, :], w[:, c, :], a, ALU.mult).then_inc(s("fold_v"), 1)
                n += KC
                dve.wait_ge(s("fold_v"), n)
                dve.tensor_reduce(wlr[:, :, lo:lo + H], s_tmp.rearrange("p c (h f) -> p c h f", f=HF), AX.X, ALU.add)\
                    .then_inc(s("fold_v"), 1)
                n += 1
                dve.wait_ge(s("fold_v"), n)
                dve.tensor_tensor(s_tmp[:, 0, :], b, a, ALU.mult).then_inc(s("fold_v"), 1)
                n += 1
                dve.wait_ge(s("fold_v"), n)
                dve.tensor_reduce(blr[:, lo:lo + H], s_tmp[:, 0, :].rearrange("p (h f) -> p h f", f=HF), AX.X, ALU.add)\
                    .then_inc(s("fold_v"), 1)
                n += 1
                dve.wait_ge(s("fold_v"), n)
            dve.wait_ge(s("tab_mm"), 1)
            dve.tensor_scalar(d128[:, 0:ST // 2], bank[4][:, 0:ST // 2], float(P), None, ALU.mult)
            dve.tensor_scalar(d128[:, ST // 2:], bank[5][:, 0:ST // 2], float(P), None, ALU.mult)
            dve.tensor_copy(s_d[0:1, 0:ST // 2], bank[4][0:1, 0:ST // 2])
            dve.tensor_copy(s_d[0:1, ST // 2:ST], bank[5][0:1, 0:ST // 2]).then_inc(s("tab_d"), 1)
            dve.wait_ge(s("tab_d"), 1)
            dve.tensor_copy(d_tab[:], s_d[0:1, 0:ST])
            dve.tensor_tensor(s_tmp[0:1, 0:2, :].rearrange("o a b -> o (a b)")[:, 0:ST], s_io[0:1, :], s_d[0:1, 0:ST],
                              ALU.subtract).then_inc(s("tab_k"), 1)
            k_row = s_tmp[0:1, 0:2, :].rearrange("o a b -> o (a b)")[:, 0:ST]
            c_row = s_tmp[0:1, 2:4, :].rearrange("o a b -> o (a b)")[:, 0:ST]
            dve.wait_ge(s("tab_k"), 1)
            dve.tensor_scalar(c_row, k_row, 1.0 / CJ, 0.5 / CJ - 0.5, ALU.mult, ALU.add).then_inc(s("tab_k"), 1)
            dve.wait_ge(s("tab_k"), 2)
            dve.tensor_scalar(c_row, c_row, ROUND, -ROUND, ALU.add, ALU.add).then_inc(s("tab_k"), 1)
            dve.tensor_scalar(k_row, k_row, float(CH), None, ALU.mult).then_inc(s("tab_k"), 1)
            dve.wait_ge(s("tab_k"), 4)
            dve.scalar_tensor_tensor(k_tab[:], c_row, float(1 - CH * CJ), k_row, ALU.mult, ALU.add)
            dve.tensor_tensor(s_cnt[0:1, 0:ST - 1], s_d[0:1, 1:ST], s_d[0:1, 0:ST - 1], ALU.subtract)
            dve.memset(s_cnt[0:1, ST - 1:ST], 1.0).then_inc(s("tab_d"), 1)
            dve.wait_ge(s("tab_d"), 2)
            dve.scalar_tensor_tensor(turn_tab[:], s_d[0:1, 0:ST], 1.0, s_cnt[0:1, :], ALU.add, ALU.mult)\
                .then_inc(s("tab_ready"), 1)

            def stats(t, slot, r):
                dve.wait_ge(s(f"st_x{slot}"), (r + 1) * 16)
                wait_past(dve, s("st_agg"), t, 1)
                dve.bn_stats(bn[:], xs[:, slot, :]).then_inc(s("st_seen"), 1)
                wait_past(dve, s("st_kept"), t, 1)
                apart(dve, s("st_seen"), t + 1)
                dve.bn_aggr(ag[:], bn[:]).then_inc(s("st_agg"), 1)
                dve.wait_ge(s("st_agg"), t + 1)
                dve.tensor_copy(mv_flat[:, bass.ds(t * 2, 2)], ag[:]).then_inc(s("st_kept"), 1)
            turns(dve, stats)
            dve.wait_ge(s("st_kept"), NT)
            dve.tensor_scalar(rstd[:], mean_var[:, :, 1], LN_EPS, None, ALU.add).then_inc(s("st_var"), 1)
            dve.wait_ge(s("st_sqrt"), 1)
            dve.reciprocal(rstd[:], rstd[:]).then_inc(s("st_rstd"), 1)
            dve.wait_ge(s("st_rstd"), 1)

            def normed(out_, in_, t):
                return dve.tensor_scalar(out_, in_, mv_flat[:, bass.ds(t * 2, 1)], rstd[:, bass.ds(t, 1)],
                                         ALU.subtract, ALU.mult)

            def score_out(t, slot):
                dve.wait_ge(s("sc_mm"), t + 1)
                dve.tensor_tensor(el_er_flat[:, bass.ds(t * 2 * H, 2 * H)], bank[2 + slot][:, 0:2 * H], blr, ALU.add).then_inc(s("sc_out"), 1)

            def scores(t, slot, r):
                dve.wait_ge(s(f"sc_x{slot}"), (r + 1) * 16)
                wait_past(dve, s("sc_tp"), t, 1)
                normed(xn, xs[:, slot, :], t).then_inc(s("sc_xn"), 1)
                if later(t, 1):
                    score_out(t - 1, 1 - slot)
            turns(dve, scores)
            score_out(NT - 1, (NT - 1) % 2)
            dve.wait_ge(s("sc_out"), NT)
            for i in range(3):
                rest = el_er[:, :, H:2 * H] if i == 0 else er_rest[:]
                dve.tensor_copy(er_parts[:, :, i, :], rest).then_inc(s("er_split"), 1)
                dve.wait_ge(s("er_split"), 2 * i + 1)
                if i < 2:
                    dve.tensor_tensor(er_rest[:], rest, er_parts[:, :, i, :], ALU.subtract).then_inc(s("er_split"), 1)
                    dve.wait_ge(s("er_split"), 2 * i + 2)

            dve.wait_ge(s("weights_in"), WEIGHT_DMAS * 16)

            def kv_add(t):
                dve.wait_ge(s("pj_kv"), t + 1)
                wait_past(dve, s("pj_kva"), t, 1)
                dve.tensor_tensor(at_acc, at_acc, bank[6][:, 0:KC * HF + 2], ALU.add).then_inc(s("pj_kva"), 1)

            def proj(t, slot, r):
                if isinstance(t, int) and t == 0:
                    dve.wait_ge(s("pj_x0"), 16)
                    normed(xn, xs[:, 0, :], 0).then_inc(s("pj_xn"), 1)
                if not (isinstance(t, int) and t == NT - 1):
                    dve.wait_ge(s(f"pj_x{1 - slot}"), (r + (1 if slot == 0 else 2)) * 16)
                    dve.wait_ge(s("pj_tp"), t + 1)
                    normed(xn, xs[:, 1 - slot, :], t + 1).then_inc(s("pj_xn"), 1)
                dve.wait_ge(s("pj_v"), t + 1)
                if later(t, 2):
                    dve.wait_ge(s(f"pj_st{slot}"), r * 16)
                dve.tensor_tensor(vs[:, slot, :], bank[2][:], bv_all, ALU.add).then_inc(s("pj_vout"), 1)
                if later(t, 1):
                    kv_add(t - 1)
                dve.wait_ge(s("pj_k"), t + 1)
                wait_past(dve, s("pj_kf"), t, 1)
                dve.tensor_scalar_min(ex[:, 0, :], bank[4][:, 0:2 * P], 0.0).then_inc(s("pj_kmin"), 1)
                dve.wait_ge(s("pj_kexp"), t + 1)
                wait_past(dve, s("pj_kv"), t, 1)
                dve.scalar_tensor_tensor(kf, bank[4][:, 0:2 * P], 0.0, ex[:, 0, :], ALU.max, ALU.add)\
                    .then_inc(s("pj_kf"), 1)
                dve.wait_ge(s("pj_q"), t + 1)
                wait_past(dve, s("pj_qf"), t, 1)
                dve.tensor_scalar_min(ex[:, 1, :], bank[5][:, 0:2 * P], 0.0).then_inc(s("pj_qmin"), 1)
                dve.wait_ge(s("pj_qexp"), t + 1)
                dve.scalar_tensor_tensor(q_feat[:, :, bass.ds(t * P, P)],
                                         bank[5][:, 0:2 * P].rearrange("p (c t) -> p c t", c=2), 0.0,
                                         ex[:, 1, :].rearrange("p (c t) -> p c t", c=2), ALU.max, ALU.add)\
                    .then_inc(s("pj_qf"), 1)
            turns(dve, proj)
            kv_add(NT - 1)
            dve.wait_ge(s("pj_kva"), NT)
            for j in range(KC):
                for i in range(2):
                    b = (2 * j + i) % 4
                    dve.tensor_copy(kvt_diag[i * HF:(i + 1) * HF, j, b * HD:(b + 1) * HD],
                                    kvt_acc[i * HF:(i + 1) * HF, j, i * HD:(i + 1) * HD])
            for c in range(2):
                for b in range(4):
                    r_ = slice(b * HD, (b + 1) * HD)
                    last = dve.tensor_scalar(ks_diag[r_, c, r_], ones[r_, r_], ks_acc[r_, c:c + 1], None, ALU.mult)
            last.then_inc(s("g_in"), 1)

            def mix(t, slot, r):
                dve.wait_ge(s(f"mx_x{slot}"), (r + 1) * 16)
                if later(t, 2):
                    dve.wait_ge(s(f"mx_st{slot}"), r * 16)
                elif t == 0:
                    dve.wait_ge(s("pj_st0"), 16 * (NT // 2 + 1))
                    dve.wait_ge(s("pj_st1"), 16 * (NT // 2))
                dve.tensor_tensor(vs[:, slot, :], xs[:, slot, :], bo_all, ALU.add).then_inc(s("mx_xb"), 1)
                dve.wait_ge(s("mx_norm"), t + 1)
                dve.tensor_scalar(ex[:, 0, :], bank[slot][:, 0:2 * P], 1e-6, None, ALU.add).then_inc(s("mx_n1"), 1)
                dve.wait_ge(s("mx_n1"), t + 1)
                dve.reciprocal(ex[:, 0, :], ex[:, 0, :]).then_inc(s("mx_n2"), 1)
                dve.wait_ge(s("mx_n2"), t + 1)
                wait_past(dve, s("mx_mm"), t, 2)
                dve.tensor_tensor(qn[slot], q_feat[:, :, bass.ds(t * P, P)],
                                  ex[:, 0, :].rearrange("p (c t) -> p c t", c=2), ALU.mult).then_inc(s("mx_qn"), 1)
                dve.wait_ge(s("mx_mm"), t + 1)
                dve.wait_ge(s("mx_xb"), t + 1)
                dve.tensor_tensor(vs[:, slot, :], vs[:, slot, :], bank[2 + slot][:], ALU.add).then_inc(s("mx_out"), 1)
            turns(dve, mix)

            dve.memset(e_er, 0.0).then_inc(s("er_add"), 1)

            def er_add(t, slot):
                k = dve.value_load(k_tab[0:1, bass.ds(t, 1)], min_val=0, max_val=ET - 1)
                dve.wait_ge(s("er_mm"), t + 1)
                dve.wait_ge(s("er_add"), t + 1)
                dve.tensor_tensor(e_er_flat[:, bass.ds(k * H, H)], e_er_flat[:, bass.ds(k * H, H)], bank[slot][:, 0:H],
                                  ALU.add).then_inc(s("er_add"), 1)

            def expand(t, slot, r):
                k = dve.value_load(k_tab[0:1, bass.ds(t, 1)], min_val=0, max_val=ET - 1)
                dve.tensor_tensor(dst_local[:, bass.ds(t, 1)], dst_f[:, bass.ds(k, 1)], d128[:, bass.ds(t, 1)],
                                  ALU.subtract).then_inc(s("dst_stepped"), 1)
                dve.wait_ge(s("dst_stepped"), t + 1)
                wait_past(dve, s("er_tp"), t, 2)
                dve.tensor_scalar(hot_b[:, slot, :], col_no[:], dst_local[:, bass.ds(t, 1)], None, ALU.is_equal)\
                    .then_inc(s("er_hot"), 1)
                if later(t, 1):
                    er_add(t - 1, 1 - slot)
            turns(dve, expand, ST)
            er_add(ST - 1, (ST - 1) % 2)

            dve.wait_ge(s("dst_scan_in"), 16 * CH)
            dve.tensor_tensor(t_pen[:, 1:CL], dst_scan[:, 1:CL], dst_scan[:, 0:CL - 1], ALU.not_equal).then_inc(s("scan_v"), 1)
            dve.tensor_copy(edge_first[:, 0:1], dst_scan[:, 0:1])
            dve.tensor_copy(edge_first[:, 1:2], dst_scan[:, CL - 1:CL])
            dve.memset(t_pen[:, 0:1], 0.0)
            dve.memset(t_pen[:, CL:CL + 1], 0.0).then_inc(s("scan_v"), 1)
            dve.wait_ge(s("scan_v"), 2)
            dve.tensor_scalar(t_pen[:, 1:CL], t_pen[:, 1:CL], -BIG, None, ALU.mult).then_inc(s("scan_v"), 1)
            dve.wait_ge(s("scan_v"), 3)
            dve.wait_ge(s("tp_el_out"), -(-CJ // 4))
            dve.tensor_tensor_scan(t_run, t_pen[:, 0:CL], t_el, -BIG, ALU.add, ALU.max).then_inc(s("scan_v"), 1)
            dve.wait_ge(s("scan_v"), 4)
            dve.tensor_copy(edge_first[:, 2:3], t_run[:, CL - 1:CL]).then_inc(s("scan_ends"), 1)

            def R(i):
                return row[0:1, i, :]
            FIRST, LAST, RUN, CONN, WHOLE, PEN_IN, PEN_W, OUT_, IN_, PEN_INB, PEN_WB = range(11)
            hc = lambda a: a.rearrange("o (h c) -> o h c", c=CH)
            n = 0

            def link(ins):
                nonlocal n
                n += 1
                ins.then_inc(s("row_v"), 1)
                dve.wait_ge(s("row_v"), n)
            dve.wait_ge(s("ends_tp"), 1)
            for i in range(3):
                link(dve.tensor_copy(hc(R(i)), bank[5][0:1, i * P:(i + 1) * P].rearrange("o (c h) -> o h c", h=H)))
            link(dve.memset(R(CONN), 0.0))
            link(dve.tensor_tensor(hc(R(CONN))[:, :, 1:CH], hc(R(FIRST))[:, :, 1:CH], hc(R(LAST))[:, :, 0:CH - 1], ALU.is_equal))
            link(dve.tensor_tensor(R(WHOLE), R(FIRST), R(LAST), ALU.is_equal))
            link(dve.tensor_scalar(R(PEN_IN), R(CONN), BIG, -BIG, ALU.mult, ALU.add))
            link(dve.tensor_tensor(R(PEN_W), R(CONN), R(WHOLE), ALU.mult))
            link(dve.tensor_scalar(R(PEN_W), R(PEN_W), BIG, -BIG, ALU.mult, ALU.add))
            link(dve.memset(R(PEN_INB), -BIG))
            link(dve.tensor_copy(hc(R(PEN_INB))[:, :, 0:CH - 1], hc(R(PEN_IN))[:, :, 1:CH]))
            link(dve.tensor_scalar(R(PEN_WB), R(WHOLE), BIG, -BIG, ALU.mult, ALU.add))
            link(dve.tensor_tensor(R(PEN_WB), R(PEN_WB), R(PEN_INB), ALU.min))
            link(dve.tensor_tensor_scan(R(OUT_), R(PEN_W), R(RUN), -BIG, ALU.add, ALU.max))
            link(dve.memset(R(IN_), -BIG))
            link(dve.tensor_tensor(hc(R(IN_))[:, :, 1:CH], hc(R(OUT_))[:, :, 0:CH - 1], hc(R(PEN_IN))[:, :, 1:CH], ALU.add))
            dve.tensor_scalar_max(R(11).rearrange("o (c h) -> o h c", h=H), hc(R(IN_)), -BIG).then_inc(s("row_in"), 1)
            dve.wait_ge(s("row_back"), 1)
            dve.tensor_copy(col[:, 0:1], bank[6][:, 0:1]).then_inc(s("scan_v"), 1)
            dve.wait_ge(s("scan_v"), 5)
            dve.tensor_tensor_scan(t_run, t_pen[:, 0:CL], t_el, col[:, 0:1], ALU.add, ALU.max).then_inc(s("scan_v"), 1)
            dve.wait_ge(s("scan_v"), 6)
            dve.tensor_tensor_scan(t_el[:, ::-1], t_pen[:, 1:CL + 1][:, ::-1], t_run[:, ::-1], -BIG, ALU.add, ALU.max)\
                .then_inc(s("scan_v"), 1)
            dve.wait_ge(s("scan_v"), 7)
            dve.tensor_copy(edge_first[:, 3:4], t_el[:, 0:1]).then_inc(s("scan_ends"), 1)
            dve.wait_ge(s("ends_tp"), 2)
            link(dve.tensor_copy(hc(R(RUN)), bank[5][0:1, 0:P].rearrange("o (c h) -> o h c", h=H)))
            link(dve.tensor_tensor_scan(R(OUT_)[:, ::-1], R(PEN_WB)[:, ::-1], R(RUN)[:, ::-1], -BIG, ALU.add, ALU.max))
            link(dve.memset(R(IN_), -BIG))
            link(dve.tensor_tensor(hc(R(IN_))[:, :, 0:CH - 1], hc(R(OUT_))[:, :, 1:CH], hc(R(PEN_INB))[:, :, 0:CH - 1], ALU.add))
            dve.tensor_scalar_max(R(11).rearrange("o (c h) -> o h c", h=H), hc(R(IN_)), -BIG).then_inc(s("row_in"), 1)
            dve.wait_ge(s("row_back"), 2)
            dve.tensor_copy(col[:, 1:2], bank[6][:, 0:1]).then_inc(s("scan_v"), 1)
            dve.wait_ge(s("scan_v"), 8)
            dve.tensor_tensor_scan(t_el[:, ::-1], t_pen[:, 1:CL + 1][:, ::-1], t_run[:, ::-1], col[:, 1:2], ALU.add, ALU.max)\
                .then_inc(s("scan_done"), 1)

            dve.wait_ge(s("er_add"), ST + 1)
            dve.wait_ge(s("el_kept"), CJ)
            dve.tensor_tensor(e_el, e_el, e_er, ALU.add).then_inc(s("sm"), 1)
            dve.wait_ge(s("sm"), 1)
            dve.scalar_tensor_tensor(e_el, e_el, NEG_SLOPE, e_el, ALU.mult, ALU.max).then_inc(s("sm"), 1)
            dve.wait_ge(s("tp_m_out"), -(-CJ // 4))
            dve.tensor_tensor(e_m, e_m, e_er, ALU.add).then_inc(s("sm"), 1)
            dve.wait_ge(s("sm"), 3)
            dve.scalar_tensor_tensor(e_m, e_m, NEG_SLOPE, e_m, ALU.mult, ALU.max).then_inc(s("sm"), 1)
            dve.wait_ge(s("sm"), 4)
            dve.tensor_tensor(e_el, e_el, e_m, ALU.subtract).then_inc(s("sm_diff"), 1)
            dve.wait_ge(s("p_ready"), 1)

            def step(t, j, r):
                k = dve.value_load(k_tab[0:1, bass.ds(t, 1)], min_val=0, max_val=ET - 1)
                b = j % 2
                wait_past(dve, s("step_mm"), t, 2)
                dve.tensor_scalar(hot[:, b, :], col_no[:], dst_local[:, bass.ds(t, 1)], None, ALU.is_equal)
                dve.tensor_copy(pv[:, b, D:D + H], e_el_flat[:, bass.ds(k * H, H)])
                dve.wait_ge(gathered[j], (r + 1) * 16)
                dve.tensor_tensor(pv[:, b, 0:D].rearrange("p (h f) -> p h f", h=H),
                                  vg[:, j, :].rearrange("p (h f) -> p h f", h=H),
                                  e_el_flat[:, bass.ds(k * H, H)].unsqueeze(2).broadcast_to([P, H, HF]),
                                  ALU.mult).then_inc(s("step_pv"), 1)
            turns(dve, step, ST, U)

            def join(t, slot, r):
                dve.wait_ge(s(f"jn_a{slot}"), (r + 1) * 16)
                dve.tensor_scalar_max(den[:], da[:, slot, D:D + H], 1e-16).then_inc(s("jn_1"), 1)
                dve.wait_ge(s("jn_1"), t + 1)
                dve.reciprocal(den[:], den[:]).then_inc(s("jn_2"), 1)
                dve.wait_ge(s("jn_2"), t + 1)
                dve.tensor_tensor(dn.rearrange("p (h f) -> p h f", h=H), da[:, slot, 0:D].rearrange("p (h f) -> p h f", h=H),
                                  den[:].unsqueeze(2).broadcast_to([P, H, HF]), ALU.mult).then_inc(s("jn_3"), 1)
                dve.wait_ge(s("jn_3"), t + 1)
                dve.wait_ge(s(f"jn_b{slot}"), (r + 1) * 16)
                if later(t, 2):
                    dve.wait_ge(s(f"jn_st{slot}"), r * 16)
                dve.tensor_tensor(dx[:, slot, :], dn, db[:, slot, :], ALU.add).then_inc(s("jn_x"), 1)
                dve.wait_ge(s("jn_x"), t + 1)
                dve.bn_stats(bn[:], dx[:, slot, :]).then_inc(s("jn_bn"), 1)
                apart(dve, s("jn_bn"), t + 1)
                dve.bn_aggr(ag[:], bn[:]).then_inc(s("jn_ag"), 1)
                dve.wait_ge(s("jn_ag"), t + 1)
                dve.tensor_copy(mv_flat[:, bass.ds(t * 2, 2)], ag[:]).then_inc(s("jn_aggr"), 1)
            turns(dve, join)
            dve.wait_ge(s("jn_aggr"), NT)
            dve.tensor_scalar(rstd[:], mean_var[:, :, 1], LN_EPS, None, ALU.add).then_inc(s("jn_var"), 1)
            dve.wait_ge(s("jn_sqrt"), 1)
            dve.reciprocal(rstd[:], rstd[:]).then_inc(s("jn_rstd"), 1)
            dve.wait_ge(s("jn_rstd"), 1)

            def moe(t, slot, r):
                dve.wait_ge(s(f"ex_x{slot}"), (r + 1) * 16)
                wait_past(dve, s("ex_tp"), t, 1)
                normed(dn, dx[:, slot, :], t).then_inc(s("ex_xn"), 1)
                n = 0

                def link(ins):
                    nonlocal n
                    n += 1
                    ins.then_inc(s("ex_g"), 1)
                    apart(dve, s("ex_g"), t * 10 + n)
                dve.wait_ge(s("ex_lg"), t + 1)
                link(dve.tensor_copy(lg[:], bank[6][:, 0:X]))
                link(dve.max(top[:], lg[:]))
                dve.tensor_scalar(nmax[:], top[:, 0:1], -1.0, None, ALU.mult).then_inc(s("ex_nmax"), 1)
                dve.wait_ge(s("ex_exp"), t + 1)
                link(dve.reciprocal(psum_[:], psum_[:]))
                link(dve.tensor_scalar(pr[:], pr[:], psum_[:], None, ALU.mult))
                link(dve.max(ptop[:], pr[:]))
                link(dve.max_index(pidx[:], ptop[:], pr[:]))
                link(dve.tensor_copy(pidf[:], pidx[:]))
                link(dve.scalar_tensor_tensor(ga[:], col_no[:, 0:X], pidf[:, 0:1], pr[:], ALU.is_equal, ALU.mult))
                link(dve.scalar_tensor_tensor(gb[:], col_no[:, 0:X], pidf[:, 1:2], pr[:], ALU.is_equal, ALU.mult))
                link(dve.tensor_tensor(gate[:, slot, :], ga[:], gb[:], ALU.add))
                for q in range(4):
                    dve.wait_ge(s("ex_gelu"), 4 * t + (q + 1))
                    for i in range(2):
                        last = dve.tensor_scalar(hs[:, q % 2, i * XF:(i + 1) * XF], hs[:, q % 2, i * XF:(i + 1) * XF],
                                                 gate[:, slot, 2 * q + i:2 * q + i + 1], None, ALU.mult)
                    last.then_inc(s("ex_hs"), 1)
                    dve.wait_ge(s("ex_htp"), 4 * t + (q + 1))
                    if q >= 2 or later(t, 1):
                        dve.wait_ge(s("ex_ymm"), 4 * t + (q - 1))
                    dve.tensor_copy(ht[:, q % 2, :], bank[4][:]).then_inc(s("ex_ht"), 1)
                dve.wait_ge(s("ex_ymm"), 4 * t + 4)
                if later(t, 2):
                    dve.wait_ge(s(f"ex_st{slot}"), r * 16)
                dve.tensor_tensor(dy[:, slot, :], dx[:, slot, :], bank[5][:], ALU.add).then_inc(s("ex_out"), 1)
            turns(dve, moe)

        @block.tensor
        def _(pe):
            def product(dst, pairs, opened=True, closed=True):
                n = len(pairs)
                for i, (a, b) in enumerate(pairs):
                    last = pe.matmul(dst, a, b, start=(opened and i == 0), stop=(closed and i == n - 1))
                return last

            def transposed(dst, src, n=KC):
                for c in range(n):
                    last = pe.transpose(dst[:, c * P:(c + 1) * P], src[:, c * P:(c + 1) * P], ident[:])
                return last

            pe.wait_ge(s("ident_ready"), 1)
            pe.wait_ge(s("tab_begun"), 1)
            for i in range(2):
                last = product(bank[4 + i][:, 0:ST // 2], [(ones[0:NT - 1, :], s_cnt[0:NT - 1, i * (ST // 2):(i + 1) * (ST // 2)])])
            last.then_inc(s("tab_mm"), 1)
            pe.wait_ge(s("weights_in"), WEIGHT_DMAS * 16)
            for c in range(KC):
                for j in range(8):
                    last = product(bank[c][:, j * HF:(j + 1) * HF], [(s_wqt[:, j, c * P:(c + 1) * P], r_diag)])
                last.then_inc(s("fold_mm"), 1)
            pe.wait_ge(s("fold_out"), KC)
            pe.wait_ge(s("fold_v"), 14)

            def scores(t, slot, r):
                pe.wait_ge(s("sc_xn"), t + 1)
                wait_past(pe, s("sc_xt"), t, 2)
                transposed(bank[slot], xn).then_inc(s("sc_tp"), 1)
                pe.wait_ge(s("sc_xt"), t + 1)
                wait_past(pe, s("sc_out"), t, 2)
                product(bank[2 + slot][:, 0:2 * H], [(xt[:, slot, c * P:(c + 1) * P], wlr[:, c, :]) for c in range(KC)])\
                    .then_inc(s("sc_mm"), 1)
            turns(pe, scores)
            pe.wait_ge(s("sc_out"), NT)

            def chunks(slot):
                return [xt[:, slot, c * P:(c + 1) * P] for c in range(KC)]

            def kv(t):
                pe.wait_ge(s("pj_mvs"), t + 1)
                pe.wait_ge(s("pj_kf"), t + 1)
                wait_past(pe, s("pj_kva"), t, 1)
                for j in range(KC):
                    product(bank[6][:, j * HF:(j + 1) * HF], [(mv[:, j * P:(j + 1) * P], kf[:, j * HF:(j + 1) * HF])])
                for c in range(2):
                    last = product(bank[6][:, KC * HF + c:KC * HF + c + 1],
                                   [(kf[:, c * P:(c + 1) * P], real_row[:, bass.ds(t, 1)])])
                last.then_inc(s("pj_kv"), 1)

            def turn_over(t, slot):
                pe.wait_ge(s("pj_xn"), t + 1)
                wait_past(pe, s("pj_xt"), t, 2)
                transposed(bank[slot], xn).then_inc(s("pj_tp"), 1)

            def proj(t, slot, r):
                if isinstance(t, int) and t == 0:
                    turn_over(0, 0)
                pe.wait_ge(s("pj_xt"), t + 1)
                wait_past(pe, s("pj_vout"), t, 1)
                product(bank[2][:], [(a, wv[:, c, :]) for c, a in enumerate(chunks(slot))]).then_inc(s("pj_v"), 1)
                if later(t, 1):
                    kv(t - 1)
                    pe.wait_ge(s("pj_mvs"), t)
                product(bank[3][:], [(a, wmv[:, c, :]) for c, a in enumerate(chunks(slot))]).then_inc(s("pj_mv"), 1)
                wait_past(pe, s("pj_kf"), t, 1)
                product(bank[4][:, 0:2 * P], [(a, wqk[:, c, 2 * P:4 * P]) for c, a in enumerate(chunks(slot))])\
                    .then_inc(s("pj_k"), 1)
                if not (isinstance(t, int) and t == NT - 1):
                    turn_over(t + 1, 1 - slot)
                wait_past(pe, s("pj_qf"), t, 1)
                for i in range(2):
                    last = product(bank[5][:, i * P:(i + 1) * P],
                                   [(wqk[:, c, i * P:(i + 1) * P], a) for c, a in enumerate(chunks(slot))])
                last.then_inc(s("pj_q"), 1)
            turns(pe, proj)
            kv(NT - 1)

            pe.wait_ge(s("g_in"), 1)
            for c in range(2):
                last = product(bank[c][:], [(kvt_diag[:, j, :], wo[:, j, :]) for j in (2 * c, 2 * c + 1)])
            last.then_inc(s("g_mm"), 1)
            pe.wait_ge(s("g_out"), 2)

            def mix(t, slot, r):
                wait_past(pe, s("mx_n1"), t, 2)
                for c in range(2):
                    last = product(bank[slot][:, c * P:(c + 1) * P], [(ks_diag[:, c, :], q_feat[:, c, bass.ds(t * P, P)])])
                last.then_inc(s("mx_norm"), 1)
                pe.wait_ge(s("mx_qn"), t + 1)
                wait_past(pe, s("mx_out"), t, 2)
                product(bank[2 + slot][:], [(qn[slot][:, c, :], g_mat[:, c, :]) for c in range(2)]).then_inc(s("mx_mm"), 1)
            turns(pe, mix)

            def turn_hot(t, slot):
                pe.wait_ge(s("er_hot"), t + 1)
                wait_past(pe, s("er_hot_t"), t, 2)
                pe.transpose(bank_b[:, slot * D:slot * D + P], hot_b[:, slot, :], ident_b[:]).then_inc(s("er_tp"), 1)

            def expand(t, slot, r):
                d = pe.value_load(d_tab[0:1, bass.ds(t, 1)], min_val=0, max_val=NT - 1)
                turn_hot(t, slot)
                pe.wait_ge(s("er_hot_t"), t + 1)
                if later(t, 2):
                    pe.wait_ge(s("er_add"), t)
                product(bank[slot][:, 0:H], [(hot_t[:, slot, :], er_flat[:, bass.ds(d * 3 * H + i * H, H)])
                                             for i in range(3)]).then_inc(s("er_mm"), 1)
            pe.wait_ge(s("mx_out"), NT)
            turns(pe, expand, ST)
            pe.wait_ge(s("er_add"), ST + 1)

            pe.wait_ge(s("el_kept"), CJ)
            for g in range(-(-CJ // 4)):
                if g >= 4:
                    pe.wait_ge(s("tp_el_out"), g - 3)
                for i in range(min(4, CJ - 4 * g)):
                    last = pe.transpose(bank[g % 4][:, i * P:(i + 1) * P], e_el_flat[:, (4 * g + i) * P:(4 * g + i + 1) * P], ident[:])
                last.then_inc(s("tp_el"), 1)
            pe.wait_ge(s("scan_ends"), 1)
            for i in range(3):
                last = pe.transpose(bank[5][0:1, i * P:(i + 1) * P], edge_first[:, i:i + 1], ident[:])
            last.then_inc(s("ends_tp"), 1)
            in_row = row[0:1, 11, :]
            pe.wait_ge(s("row_in"), 1)
            product(bank[6][:, 0:1], [(in_row, ones[0:1, 0:1])]).then_inc(s("row_back"), 1)
            pe.wait_ge(s("scan_ends"), 2)
            pe.transpose(bank[5][0:1, 0:P], edge_first[:, 3:4], ident[:]).then_inc(s("ends_tp"), 1)
            pe.wait_ge(s("row_in"), 2)
            product(bank[6][:, 0:1], [(in_row, ones[0:1, 0:1])]).then_inc(s("row_back"), 1)
            pe.wait_ge(s("scan_done"), 1)
            pe.wait_ge(s("tp_el_out"), -(-CJ // 4))
            for g in range(-(-CJ // 4)):
                if g >= 4:
                    pe.wait_ge(s("tp_m_out"), g - 3)
                for i in range(min(4, CJ - 4 * g)):
                    last = pe.transpose(bank[g % 4][:, i * P:(i + 1) * P], t_el[:, (4 * g + i) * P:(4 * g + i + 1) * P], ident[:])
                last.then_inc(s("tp_m"), 1)
            pe.wait_ge(s("tp_m_out"), -(-CJ // 4))

            def empty(opened, closed):
                pe.matmul(bank[0][:], zeros[0:1, 0:P], zeros[0:1, :], start=opened, stop=closed)
                return pe.matmul(bank[1][:, 0:H], zeros[0:1, 0:P], zeros[0:1, 0:H], start=opened, stop=closed)

            def step(t, j, r):
                turn = pe.value_load(turn_tab[0:1, bass.ds(t, 1)], min_val=0, max_val=NT)
                pe.wait_ge(s("step_pv"), t + 1)
                pe.matmul(bank[0][:], hot[:, j % 2, :], pv[:, j % 2, 0:D], start=False, stop=False)
                pe.matmul(bank[1][:, 0:H], hot[:, j % 2, :], pv[:, j % 2, D:D + H], start=False, stop=False)\
                    .then_inc(s("step_mm"), 1)
                with pe.If(turn):
                    empty(False, True).then_inc(s("tile_sum"), 1)
                    pe.wait_ge(s("tile_out"), turn)
                    empty(True, False)
            empty(True, False)
            turns(pe, step, ST, U)
            empty(False, True)

            pe.wait_ge(s("experts_in"), EXPERT_DMAS * 16)

            def moe(t, slot, r):
                pe.wait_ge(s("ex_xn"), t + 1)
                wait_past(pe, s("ex_xt"), t, 2)
                transposed(bank[slot], dn).then_inc(s("ex_tp"), 1)
                pe.wait_ge(s("ex_xt"), t + 1)
                xc = [dt_[:, slot, c * P:(c + 1) * P] for c in range(KC)]
                if later(t, 1):
                    pe.wait_ge(s("ex_g"), t * 10)
                product(bank[6][:, 0:X], [(a, wr[:, c, :]) for c, a in enumerate(xc)]).then_inc(s("ex_lg"), 1)

                def hidden(q):
                    if q >= 2 or later(t, 1):
                        pe.wait_ge(s("ex_gelu"), 4 * t + (q - 1))
                    product(bank[2 + q % 2][:], [(a, w1[:, c, q * D:(q + 1) * D]) for c, a in enumerate(xc)])\
                        .then_inc(s("ex_hmm"), 1)

                def turned(q):
                    pe.wait_ge(s("ex_hs"), 4 * t + (q + 1))
                    if q >= 1 or later(t, 1):
                        pe.wait_ge(s("ex_ht"), 4 * t + q)
                    transposed(bank[4], hs[:, q % 2, :]).then_inc(s("ex_htp"), 1)

                def summed(q):
                    pe.wait_ge(s("ex_ht"), 4 * t + (q + 1))
                    if q == 0:
                        wait_past(pe, s("ex_out"), t, 1)
                    product(bank[5][:], [(ht[:, q % 2, c * P:(c + 1) * P], w2[:, 4 * q + c, :]) for c in range(KC)],
                            opened=(q == 0), closed=(q == 3)).then_inc(s("ex_ymm"), 1)
                hidden(0)
                hidden(1)
                turned(0)
                for q in range(4):
                    if q < 2:
                        hidden(q + 2)
                    summed(q)
                    if q < 3:
                        turned(q + 1)
            turns(pe, moe)


_OUT = (NP, D)


def kernel(**inputs):
    import numpy as _np
    import concourse.bacc as _bacc
    from concourse import mybir as _mybir
    from concourse.bass_utils import run_bass_kernel_spmd as _run

    def padded(a, n):
        b = _np.zeros((n,) + a.shape[1:], a.dtype)
        b[:a.shape[0]] = a
        return b

    a = {k: _np.ascontiguousarray(v) for k, v in inputs.items()}
    def columns(edges):
        return edges.reshape(CH, CJ, P).transpose(2, 1, 0).reshape(P, ET)

    src = padded(a["src"], EP)
    dst = _np.full((EP,), 2 * NP, a["dst"].dtype)
    dst[:E] = a["dst"]
    w_qkv = a["L0_mix_W_qkv"]
    laid = {
        "x": padded(a["x"], NP),
        "src_cols": columns(src), "dst_cols": columns(dst), "dst_rows": dst.reshape(CH, CL),
        "w_src": a["L0_gnn_W_src"], "b_src": a["L0_gnn_b_src"].reshape(1, D),
        "w_dst": a["L0_gnn_W_dst"], "b_dst": a["L0_gnn_b_dst"].reshape(1, D),
        "w_val": a["L0_gnn_W_val"], "b_val": a["L0_gnn_b_val"].reshape(1, D),
        "attn_l": a["L0_gnn_attn_l"].reshape(1, D), "attn_r": a["L0_gnn_attn_r"].reshape(1, D),
        "w_qk_t": w_qkv[:, :2 * D].T, "w_v": w_qkv[:, 2 * D:],
        "r_mat": a["L0_mix_random_matrix"], "w_out": a["L0_mix_W_out"],
        "b_out": a["L0_mix_b_out"].reshape(1, D), "w_r": a["L0_ffn_Wr"],
        "w_1": a["L0_ffn_W1"], "w_2": a["L0_ffn_W2"],
    }
    nc = _bacc.Bacc("TRN2", target_bir_lowering=False, num_devices=1)
    arrays, args = {}, {}
    for name, v in laid.items():
        v = _np.ascontiguousarray(v)
        arrays[f"in_{name}"] = v
        args[name] = nc.dram_tensor(f"in_{name}", v.shape, _mybir.dt.from_np(v.dtype), kind="ExternalInput").ap()
    args["out"] = nc.dram_tensor("out_0", _OUT, _mybir.dt.float32, kind="ExternalOutput").ap()
    gps_layer(nc, **args)
    r = _run(nc, [arrays], core_ids=[0])
    return r.results[0]["out_0"][:N]
```

```python
from contextlib import ExitStack

import numpy as np

import concourse.bass as bass
from concourse import mybir

F32 = mybir.dt.float32
F32R = mybir.dt.float32r
I32 = mybir.dt.int32
U16 = mybir.dt.uint16
U32 = mybir.dt.uint32
BF16 = mybir.dt.bfloat16
ALU = mybir.AluOpType
ACT = mybir.ActivationFunctionType
AX = mybir.AxisListType
ENGINE = mybir.EngineType

P = 128
N, D, E = 6250, 512, 100000
H, HF = 8, 64
HD = 32
X, XF = 8, 256
KC = D // P
NT = -(-N // P)
NP = NT * P
CH = 16
CJ = -(-E // (P * CH))
ET = CH * CJ
EP = ET * P
CL = CJ * P
ST = ET + NT - 1
BIG = 1.0e30
ROUND = 1.5 * 2.0 ** 23
NEG_SLOPE = 0.2
LN_EPS = 1e-5
U = 16
G = 8
V = 4
SG = ST // G
SETUP_DMAS, WEIGHT_DMAS, EXPERT_DMAS = 9, 8, 5
assert NT % 4 == 1 and ST % U == 0 and SG % 2 == 0 and U % (2 * V) == 0 and NT % 2 == 1

SEMAPHORES = (
    "dst_scan_in", "dst_stepped", "el_idx", "el_in0", "el_in1", "el_kept", "el_stored",
    "ends_stepped", "ends_tp", "er_carried", "er_got", "er_hot", "er_hot_t", "er_kept", "er_mm",
    "er_split", "er_summed", "er_tp", "ex_exp", "ex_g", "ex_gelu", "ex_hhi", "ex_hmm", "ex_hs",
    "ex_ht", "ex_htp", "ex_lg", "ex_nmax", "ex_out", "ex_st0", "ex_st1", "ex_st2", "ex_st3",
    "ex_tp", "ex_xhi", "ex_xn", "ex_xt", "ex_ymm", "experts_in", "fin_st0", "fin_st1",
    "fold_mm", "fold_out", "fold_v", "g_in", "g_mm", "g_out", "ident_ready", "jn_a0", "jn_a1",
    "jn_ag", "jn_b0", "jn_b1", "jn_b2", "jn_b3", "jn_bn", "jn_inv", "jn_eps", "jn_power", "jn_n", "jn_x", "mx_mm",
    "mx_n1", "mx_n2", "mx_norm", "mx_out", "mx_qn", "mx_st0", "mx_st1", "mx_x0", "mx_x1",
    "mx_xb", "p_ready", "p_row", "p_set", "pj_k", "pj_kexp", "pj_kf", "pj_kmin", "pj_kv",
    "pj_kva", "pj_mv", "pj_mvs", "pj_q", "pj_qexp", "pj_qf", "pj_qmin", "pj_st0", "pj_st1",
    "pj_tp", "pj_v", "pj_vout", "pj_x0", "pj_x1", "pj_xn", "pj_xt", "r_zeroed", "router_in",
    "row_back", "row_in", "row_v", "same_set", "sc_mm", "sc_out", "sc_tp", "sc_x0", "sc_x1",
    "sc_xn", "sc_xt", "scan_done", "scan_ends", "scan_v", "setup_in", "sm", "sm_diff", "st_agg",
    "st_kept", "st_rstd", "st_seen", "st_sqrt", "st_var", "st_x0", "st_x1", "step_idx",
    "step_mm", "step_pv", "tab_begun", "tab_d", "tab_k", "tab_mm", "tab_ready", "tile_out",
    "tile_sum", "tp_el", "tp_el_out", "tp_m", "tp_m_out", "v_set", "w_hi", "w_lo", "weights_in")


def turns(eng, body, n=NT, u=2, peeled=1):
    for t in range(u * peeled):
        body(t, t % u, t // u)
    with eng.Fori(peeled, n // u) as i:
        for j in range(u):
            body(i * u + j, j, i)
    for t in range(n // u * u, n):
        body(t, t % u, t // u)


def wait_past(eng, sem, t, lag):
    if not isinstance(t, int) or t >= lag:
        eng.wait_ge(sem, t + (1 - lag))


def not_last(t):
    return not (isinstance(t, int) and t == NT - 1)


def later(t, lag):
    return not isinstance(t, int) or t >= lag


def gps_layer(nc, x, src_cols, dst_cols, dst_rows, w_src, b_src, w_dst, b_dst, w_val, b_val, attn_l,
              attn_r, w_qk_t, w_v, r_mat, w_out, b_out, w_r, w_1, w_2, out):
    el_table = nc.dram_tensor("el_table", (NP, H), F32, kind="Internal").ap()
    v_table = nc.dram_tensor("v_table", (NP, D), F32, kind="Internal").ap()
    x_mix = nc.dram_tensor("x_mix", (NP, D), F32, kind="Internal").ap()
    agg = nc.dram_tensor("agg", (NP, D + H), F32, kind="Internal").ap()
    x_mid = nc.dram_tensor("x_mid", (NP, D), F32, kind="Internal").ap()

    def rows(dram, t):
        return dram[bass.ds(t * P, P), :]

    with ExitStack() as ctx:
        def sb(name, shape, dt=F32):
            return ctx.enter_context(nc.sbuf_tensor(name, shape, dt))

        def sem(name):
            return ctx.enter_context(nc.semaphore(name))

        ident = sb("ident", [P, P])
        ident_b = sb("ident_b", [P, P], BF16)
        col_no = sb("col_no", [P, P])
        ones = sb("ones", [P, P])
        zeros = sb("zeros", [1, D], BF16)
        ends_of = sb("ends_of", [P, 2, ET], I32)
        ends_step = sb("ends_step", [P, 2, ST], I32)
        dst_local = sb("dst_local", [P, ST])
        el_er = sb("el_er", [P, NT, 2 * H])
        er_parts = sb("er_parts", [P, NT, 3, H], BF16)
        er_rest = sb("er_rest", [P, NT, H])
        k_tab = sb("k_tab", [1, ST], U16)
        d_tab = sb("d_tab", [1, ST], U16)
        keep_tab = sb("keep_tab", [1, ST], U16)
        turn_tab = sb("turn_tab", [1, ST], U16)
        real_row = sb("real_row", [P, NT])
        mean_var = sb("mean_var", [P, NT, 2])
        rstd = sb("rstd", [P, NT])
        small = sb("small", [P, 64])

        ARENA = 41480
        with nc.sbuf_tensor("arena", [P, ARENA], F32) as arena:
            pass
        w1_hi = [sb(f"w1_hi{c}", [P, X * XF], F32R) for c in range(KC)]
        w2_hi = [sb(f"w2_hi{c}", [P, KC, D], F32R) for c in range(4)]
        wr_at = 2 * KC * X * XF
        sb("wr_room", [P, KC * X])
        wr_hi = sb("wr_hi", [P, KC, X], F32R)
        wr_lo = sb("wr_lo", [P, KC, X], F32R)
        xt_hi = sb("xt_hi", [P, 2, D], F32R)
        xt_lo = sb("xt_lo", [P, 2, D], F32R)
        ht_hi = sb("ht_hi", [P, 2, D], F32R)
        ht_lo = sb("ht_lo", [P, 2, D], F32R)
        rows_at = wr_at + 3 * KC * X + 8 * D
        w1_at, w2_at = ARENA - 2 * KC * X * XF, ARENA - KC * X * XF
        sb("rows_room", [P, w1_at - rows_at])
        w1_lo = [sb(f"w1_lo{c}", [P, X * XF], F32R) for c in range(KC)]
        w2_lo = [sb(f"w2_lo{c}", [P, KC, D], F32R) for c in range(4)]

        def at(off, *shape, dt=None):
            n = int(np.prod(shape))
            assert off + n <= ARENA, (off, shape)
            v = arena[:, off:off + n]
            if dt is not None:
                v = v.bitcast(dt)
            if len(shape) == 2:
                v = v.rearrange("p (a b) -> p a b", a=shape[0])
            elif len(shape) == 3:
                v = v.rearrange("p (a b c) -> p a b c", a=shape[0], b=shape[1])
            return v

        t_el = at(0, CL)
        t_pen = at(CL, CL + 1)
        t_run = at(2 * CL + 2, CL)
        q_feat = at(0, 2, NP)
        e_el = at(3 * CL + 4, ET, H)
        o = 3 * CL + 4 + ET * H
        ph_a = o
        wv = at(o, KC, D); o += KC * D
        wmv = at(o, KC, D); o += KC * D
        wqk = at(o, KC, D); o += KC * D
        wo = at(o, KC, D); o += KC * D
        e_er = at(ph_a, ET, H)
        bv_all = at(o, D); o += D
        bo_all = at(o, D); o += D
        wlr = at(o, KC, 2 * H); o += KC * 2 * H
        blr = at(o, 2 * H); o += 2 * H
        at_acc = at(o, KC * HF + 2)
        kvt_acc = at(o, KC, HF); o += KC * HF
        ks_acc = at(o, 2); o += 2
        r_diag = at(o, HF); o += HF
        g_mat = at(o, 2, D); o += 2 * D
        kvt_diag = at(o, KC, P); o += KC * P
        ks_diag = at(o, 2, P); o += 2 * P
        xs_at = o
        xs = at(o, 2, D); o += 2 * D
        xn = at(o, D); o += D
        xt = at(o, 2, D); o += 2 * D
        vs = at(o, 2, D); o += 2 * D
        mv = at(o, D); o += D
        kf = at(o, 2 * P); o += 2 * P
        ex = at(o, 2, 2 * P); o += 4 * P
        assert o <= ARENA, o
        s_w = at(0, KC, D)
        s_w2 = at(2048, KC, D)
        s_al = at(4096, D)
        s_ar = at(4608, D)
        s_bs = at(5120, D)
        s_bd = at(5632, D)
        s_tmp = at(6144, KC, D)
        s_wqt = at(8192, 8, D)
        s_cnt = at(12288, ST)
        s_d = at(13200, ST)
        s_io = at(14200, ST)
        s_last = at(15200, ET)
        d128 = sb("d128", [P, ST])

        qn = [kf.rearrange("p (c t) -> p c t", c=2), ex[:, 1, :].rearrange("p (c t) -> p c t", c=2)]
        o = 0
        vg = at(o, U, D); o += U * D
        pv = at(o, V, D + H); o += V * (D + H)
        hot = at(o, 2, V, P); o += 2 * V * P
        fin = at(o, 2, D + H); o += 2 * (D + H)
        assert o <= 2 * CL
        wr = at(wr_at, KC, X)
        w1 = at(w1_at, KC, X * XF)
        w2 = at(w2_at, 2 * X, D)
        o = rows_at
        da = at(o, 2, D + H); o += 2 * (D + H)
        dx = at(o, 4, D); o += 4 * D
        hs = at(o, 2, D); o += 2 * D
        assert o <= w1_at
        idx = sb("idx", [P, U], I32)
        idx_el = sb("idx_el", [P, 2, CH], I32)
        got_el = sb("got_el", [P, 2, CH, H])
        thr = sb("thr", [P, 1])
        inv = sb("inv", [P, 1])
        power = sb("power", [P, 1])
        bn = sb("bn", [P, 6])
        ag = sb("ag", [P, 2])
        den = sb("den", [P, H])
        row = at(ph_a + (ET + NT) * H, 12, P)
        o = ph_a + (ET + NT) * H + 12 * P
        hot_b = at(o, G * P, dt=BF16).rearrange("p (s g n) -> p s g n", s=2, g=G); o += G * P
        hot_t = at(o, G * P, dt=BF16).rearrange("p (s n) -> p s n", s=2); o += G * P
        same = at(0, SG, H * (1 + G)).rearrange("p g (h i) -> p g h i", h=H)
        er_got = at(o, 2, H, 1 + G); o += 2 * H * (1 + G)
        er_run = at(o, 2, H, 1 + G); o += 2 * H * (1 + G)
        assert o <= xs_at
        edge_first = sb("edge_first", [P, 4])
        col = sb("col", [P, 2])
        lg = sb("lg", [P, 8])
        top = sb("top", [P, 8])
        nmax = sb("nmax", [P, 1])
        pr = sb("pr", [P, 8])
        psum_ = sb("psum_", [P, 1])
        ptop = sb("ptop", [P, 8])
        pidx = sb("pidx", [P, 8], U32)
        pidf = sb("pidf", [P, 8])
        ga = sb("ga", [P, 8])
        gb = sb("gb", [P, 8])
        gate = sb("gate", [P, 2, 8])
        e_m = at(2 * CL + 2, ET, H)
        dst_scan = at(2 * CL + 2, CL, dt=I32)
        mv_flat = mean_var[:].rearrange("p t a -> p (t a)")
        el_er_flat = el_er[:].rearrange("p t a -> p (t a)")
        er_flat = er_parts[:].rearrange("p t i h -> p (t i h)")
        e_er_flat = at(ph_a, (ET + NT) * H)
        e_el_flat = e_el.rearrange("p k h -> p (k h)")

        bank = [ctx.enter_context(nc.psum_tensor(f"bank{i}", [P, D], F32)) for i in range(7)]
        bank_b = ctx.enter_context(nc.psum_tensor("bank_b", [P, 2 * D], BF16))
        turned_hot = [bank_b, bank[6][:].bitcast(BF16)]
        sems = {}

        def s(name):
            if name not in sems:
                sems[name] = sem(name)
            return sems[name]

        gathered = [sem(f"rows_gathered{j}") for j in range(U)]
        for name in SEMAPHORES:
            s(name)
        block = ctx.enter_context(nc.Block())

        def apart(eng, sem_, value):
            if not isinstance(value, int):
                value = eng.to_reg(value)
                eng.wait_ge(s("p_set"), 1)
            eng.wait_ge(sem_, value)

        def by_chunk(w):
            return w.rearrange("(c p) n -> p c n", p=P)

        def bcast(row_ap):
            return row_ap.broadcast_to([P, row_ap.shape[-1]])

        def by_part(w, n):
            return w[:].unsqueeze(1) if n == 1 else w[:]

        def looked_up(engine, table, t, n, top):
            return nc.values_load_multi_w_load_instructions(
                table[0:1, bass.ds(t, n)], engines=(engine,), min_val=0, max_val=top,
                skip_runtime_bounds_check_because="the tables count edge tiles and node tiles, whatever dst holds")[1]

        @block.sync
        def _(sp):
            for dst, src in ((ends_of[:, 0, :], src_cols), (ends_of[:, 1, :], dst_cols), (s_w, by_chunk(w_src)),
                             (s_w2, by_chunk(w_dst)), (s_al, bcast(attn_l)), (s_ar, bcast(attn_r)),
                             (s_bs, bcast(b_src)), (s_bd, bcast(b_dst)),
                             (s_last[0:NT - 1, :].bitcast(I32), dst_cols[P - 1:P, :].broadcast_to([NT - 1, ET]))):
                sp.dma_start(dst, src).then_inc(s("setup_in"), 16)

            def stats(t, slot, r):
                wait_past(sp, s("st_seen"), t, 2)
                sp.dma_start(xs[:, slot, :], rows(x, t)).then_inc(s(f"st_x{slot}"), 16)
            turns(sp, stats)
            sp.wait_ge(s("r_zeroed"), 1)
            for dst, src in ((r_diag[0:HF, 0:HD], r_mat), (r_diag[HF:P, HD:2 * HD], r_mat),
                             (s_wqt, by_chunk(w_qk_t)), (wv, by_chunk(w_val)), (wmv, by_chunk(w_v)),
                             (wo, by_chunk(w_out)), (bv_all, bcast(b_val)), (bo_all, bcast(b_out))):
                sp.dma_start(dst, src).then_inc(s("weights_in"), 16)

            sp.wait_ge(s("st_seen"), NT)

            def scores(t, slot, r):
                wait_past(sp, s("sc_xn"), t, 2)
                sp.dma_start(xs[:, slot, :], rows(x, t)).then_inc(s(f"sc_x{slot}"), 16)
            turns(sp, scores)
            sp.wait_ge(s("sc_out"), NT)
            sp.dma_start(el_table.rearrange("(t p) h -> p t h", p=P), el_er[:, :, 0:H]).then_inc(s("el_stored"), 16)

            def proj(t, slot, r):
                wait_past(sp, s("pj_xn"), t, 2)
                sp.dma_start(xs[:, slot, :], rows(x, t)).then_inc(s(f"pj_x{slot}"), 16)
                if later(t, 1):
                    sp.wait_ge(s("pj_vout"), t)
                    sp.dma_start(rows(v_table, t - 1), vs[:, 1 - slot, :]).then_inc(s(f"pj_st{1 - slot}"), 16)
            turns(sp, proj)
            sp.wait_ge(s("pj_vout"), NT)
            sp.dma_start(rows(v_table, NT - 1), vs[:, (NT - 1) % 2, :]).then_inc(s("pj_st0"), 16)

            sp.wait_ge(s("pj_xn"), NT)

            def mix(t, slot, r):
                wait_past(sp, s("mx_xb"), t, 2)
                sp.dma_start(xs[:, slot, :], rows(x, t)).then_inc(s(f"mx_x{slot}"), 16)
                if later(t, 1):
                    sp.wait_ge(s("mx_out"), t)
                    sp.dma_start(rows(x_mix, t - 1), vs[:, 1 - slot, :]).then_inc(s(f"mx_st{1 - slot}"), 16)
            turns(sp, mix)
            sp.wait_ge(s("mx_out"), NT)
            sp.dma_start(rows(x_mix, NT - 1), vs[:, (NT - 1) % 2, :]).then_inc(s("mx_st0"), 16)

            for c in range(CH):
                sp.dma_start(dst_scan[c * H:(c + 1) * H, :], dst_rows[c:c + 1, :].broadcast_to([H, CL]))\
                  .then_inc(s("dst_scan_in"), 16)

            sp.wait_ge(s("mx_st0"), 16 * (NT // 2 + 1))
            sp.wait_ge(s("mx_st1"), 16 * (NT // 2))
            sp.wait_ge(s("p_ready"), 1)
            w1_by = w1.rearrange("p c (e f) -> p c e f", e=X)
            for c in range(KC):
                sp.dma_start(w1_by[:, c], w_1[:, c * P:(c + 1) * P, :].rearrange("e p f -> p e f")).then_inc(s("experts_in"), 16)
            sp.dma_start(w2, w_2.rearrange("e (c p) n -> p (e c) n", p=P)).then_inc(s("experts_in"), 16)
            sp.wait_ge(s("fin_st0"), 16 * (NT // 2 + 1))
            sp.wait_ge(s("fin_st1"), 16 * (NT // 2))
            sp.wait_ge(s("step_mm"), ST)
            sp.dma_start(wr, by_chunk(w_r)).then_inc(s("router_in"), 16)

            def store(t, j, r):
                sp.wait_ge(s("ex_out"), t + 1)
                sp.dma_start(rows(out, t), dx[:, j, :]).then_inc(s(f"ex_st{j}"), 16)

            def moe(t, j, r):
                wait_past(sp, s("ex_tp"), t, 2)
                sp.dma_start(da[:, j % 2, :], rows(agg, t)).then_inc(s(f"jn_a{j % 2}"), 16)
                if later(t, 4):
                    sp.wait_ge(s(f"ex_st{j}"), r * 16)
                sp.dma_start(dx[:, j, :], rows(x_mix, t)).then_inc(s(f"jn_b{j}"), 16)
                if later(t, 3):
                    store(t - 3, (j + 1) % 4, r)
            turns(sp, moe, NT, 4)
            for t in range(NT - 3, NT):
                store(t, t % 4, t // 4)
            for j in range(4):
                sp.wait_ge(s(f"ex_st{j}"), 16 * ((NT - 1 - j) // 4 + 1))

        @block.gpsimd
        def _(pool):
            kw = dict(allow_small_or_imprecise_dtypes=True)
            pool.memset(ident[:], 0.0).then_inc(s("p_set"), 1)
            pool.memset(ones[:], 1.0).then_inc(s("p_set"), 1)
            pool.memset(zeros[:], 0.0).then_inc(s("p_set"), 1)
            pool.wait_ge(s("p_set"), 1)
            pool.affine_select(out=ident[:], in_=ident[:], compare_op=ALU.not_equal, fill=1.0, base=0,
                               pattern=[[-1, P]], channel_multiplier=1).then_inc(s("p_set"), 1)
            pool.iota(col_no[:], [[1, P]], base=0, channel_multiplier=0, **kw).then_inc(s("p_set"), 1)
            pool.iota(thr[:], [[0, 1]], base=P, channel_multiplier=P, **kw).then_inc(s("p_set"), 1)
            pool.iota(s_io, [[1, ST]], base=0, channel_multiplier=0, **kw).then_inc(s("p_set"), 1)
            pool.iota(real_row[:], [[P, NT]], base=0, channel_multiplier=1, **kw).then_inc(s("p_row"), 1)
            pool.wait_ge(s("p_row"), 1)
            pool.tensor_scalar(real_row[:], real_row[:], float(N), None, ALU.is_lt).then_inc(s("p_set"), 1)
            pool.memset(r_diag, 0.0).then_inc(s("r_zeroed"), 1)
            pool.memset(kvt_diag, 0.0).then_inc(s("p_set"), 1)
            pool.memset(ks_diag, 0.0).then_inc(s("p_set"), 1)
            pool.memset(at_acc, 0.0).then_inc(s("p_set"), 1)
            pool.wait_ge(s("setup_in"), SETUP_DMAS * 16)
            pool.wait_ge(s("el_stored"), 16)

            def keep(t, slot, r):
                pool.wait_ge(s(f"el_in{slot}"), (r + 1) * (16 * CH))
                pool.tensor_copy(e_el_flat[:, bass.ds(t * P, P)], got_el[:, slot].rearrange("p c h -> p (c h)"))\
                    .then_inc(s("el_kept"), 1)

            def gather(t, slot, r):
                wait_past(pool, s("el_kept"), t, 2)
                pool.tensor_copy(idx_el[:, slot, :], ends_of[:, 0, bass.ds(t * CH, CH)])\
                    .then_inc(s("el_idx"), 1)
                apart(pool, s("el_idx"), t + 1)
                for c in range(CH):
                    pool.indirect_dma_start(got_el[:, slot, c, :], None, el_table,
                                            bass.IndirectOffsetOnAxis(ap=idx_el[:, slot, c:c + 1], axis=0))\
                        .then_inc(s(f"el_in{slot}"), 16)
                if later(t, 1):
                    keep(t - 1, 1 - slot, (r - 1 if slot == 0 else r))
            turns(pool, gather, CJ)
            keep(CJ - 1, (CJ - 1) % 2, (CJ - 1) // 2)

            for name, n in (("pj_st0", NT // 2 + 1), ("pj_st1", NT // 2), ("mx_st0", NT // 2 + 1), ("mx_st1", NT // 2)):
                pool.wait_ge(s(name), 16 * n)
            pool.wait_ge(s("ends_stepped"), SG)
            pool.wait_ge(s("p_ready"), 1)

            def values(t, j, r):
                if j % 8 == 0:
                    wait_past(pool, s("step_pv"), t, 9)
                    pool.tensor_copy(idx[:, j:j + 8], ends_step[:, 0, bass.ds(t, 8)]).then_inc(s("step_idx"), 1)
                    apart(pool, s("step_idx"), r * (U // 8) + (j // 8 + 1))
                if later(t, U):
                    apart(pool, s("step_pv"), t + (1 - U))
                pool.indirect_dma_start(vg[:, j, :], None, v_table,
                                        bass.IndirectOffsetOnAxis(ap=idx[:, j:j + 1], axis=0))\
                    .then_inc(gathered[j], 16)
            turns(pool, values, ST, U)

            def inverse(t, slot, r):
                apart(pool, s("jn_ag"), t + 1)
                wait_past(pool, s("ex_xn"), t, 1)
                pool.tensor_scalar(inv[:], ag[:, 1:2], LN_EPS, None, ALU.add).then_inc(s("jn_eps"), 1)
                pool.wait_ge(s("jn_eps"), t + 1)
                pool.tensor_tensor(inv[:], inv[:], power[:], ALU.pow).then_inc(s("jn_inv"), 1)
            pool.memset(power[:], -0.5).then_inc(s("jn_power"), 1)
            pool.wait_ge(s("jn_power"), 1)
            turns(pool, inverse)

        @block.scalar
        def _(act):
            act.wait_ge(s("fold_mm"), KC)
            for c in range(KC):
                act.activation(wqk[:, c, :], bank[c][:], ACT.Copy).then_inc(s("fold_out"), 1)
            act.wait_ge(s("st_var"), 1)
            act.activation(rstd[:], rstd[:], ACT.Sqrt).then_inc(s("st_sqrt"), 1)

            def scores(t, slot, r):
                act.wait_ge(s("sc_tp"), t + 1)
                wait_past(act, s("sc_mm"), t, 2)
                act.activation(xt[:, slot, :], bank[slot][:], ACT.Copy).then_inc(s("sc_xt"), 1)
            turns(act, scores)
            act.wait_ge(s("sc_mm"), NT)

            def proj(t, slot, r):
                act.wait_ge(s("pj_tp"), t + 1)
                wait_past(act, s("pj_q"), t, 2)
                act.activation(xt[:, slot, :], bank[slot][:], ACT.Copy).then_inc(s("pj_xt"), 1)
                act.wait_ge(s("pj_mv"), t + 1)
                act.activation(mv, bank[3][:], ACT.Copy).then_inc(s("pj_mvs"), 1)
                act.wait_ge(s("pj_kmin"), t + 1)
                act.activation(ex[:, 0, :], ex[:, 0, :], ACT.Exp).then_inc(s("pj_kexp"), 1)
                act.wait_ge(s("pj_qmin"), t + 1)
                act.activation(ex[:, 1, :], ex[:, 1, :], ACT.Exp).then_inc(s("pj_qexp"), 1)
            turns(act, proj)
            act.wait_ge(s("g_mm"), 1)
            for c in range(2):
                act.activation(g_mat[:, c, :], bank[c][:], ACT.Copy).then_inc(s("g_out"), 1)

            def keep_hot(g, slot):
                act.wait_ge(s("er_tp"), g + 1)
                wait_past(act, s("er_mm"), g, 2)
                act.activation(hot_t[:, slot, :], turned_hot[slot][:, 0:G * P], ACT.Copy).then_inc(s("er_hot_t"), 1)

            def keep_er(g, slot, places):
                act.wait_ge(s("er_summed"), g + 1)
                for i, k in enumerate(places):
                    last = act.activation(e_er_flat[:, bass.ds(k * H, H)], er_run[:, slot, :, 1 + i], ACT.Copy)
                last.then_inc(s("er_kept"), 1)

            def places_of(g):
                return looked_up(ENGINE.Activation, keep_tab, g * G, G, ET + NT - 1)

            def expand(g, slot, r):
                for i, k in enumerate(looked_up(ENGINE.Activation, k_tab, g * G, G, ET - 1)):
                    last = act.activation(ends_step[:, :, bass.ds(g * G + i, 1)], ends_of[:, :, bass.ds(k, 1)], ACT.Copy)
                last.then_inc(s("ends_stepped"), 1)
                if later(g, 1):
                    keep_hot(g - 1, 1 - slot)
                if later(g, 3):
                    keep_er(g - 3, 1 - slot, places_of(g - 3))
            turns(act, expand, SG, peeled=2)
            keep_hot(SG - 1, 1)
            for g in range(SG - 3, SG):
                keep_er(g, g % 2, places_of(g))

            for g in range(-(-CJ // 4)):
                n = min(4, CJ - 4 * g)
                act.wait_ge(s("tp_el"), g + 1)
                act.activation(t_el[:, g * D:g * D + n * P], bank[g % 4][:, 0:n * P], ACT.Copy).then_inc(s("tp_el_out"), 1)
            m_flat = e_m.rearrange("p k h -> p (k h)")
            for g in range(-(-CJ // 4)):
                n = min(4, CJ - 4 * g)
                act.wait_ge(s("tp_m"), g + 1)
                act.activation(m_flat[:, 4 * g * P:(4 * g + n) * P], bank[g % 4][:, 0:n * P], ACT.Copy).then_inc(s("tp_m_out"), 1)
            act.wait_ge(s("sm_diff"), 1)
            act.activation(e_el, e_el, ACT.Exp).then_inc(s("p_ready"), 1)

            def finish(t, slot, r):
                act.wait_ge(s("tile_sum"), t + 1)
                if later(t, 2):
                    act.wait_ge(s(f"fin_st{slot}"), r * 16)
                act.activation(fin[:, slot, 0:D], bank[0][:], ACT.Copy)
                act.activation(fin[:, slot, D:D + H], bank[1][:, 0:H], ACT.Copy).then_inc(s("tile_out"), 1)
                act.wait_ge(s("tile_out"), t + 1)
                act.dma_start(rows(agg, t), fin[:, slot, :]).then_inc(s(f"fin_st{slot}"), 16)
            turns(act, finish)

            act.wait_ge(s("step_mm"), ST)
            act.wait_ge(s("fin_st0"), 16 * (NT // 2 + 1))
            act.wait_ge(s("fin_st1"), 16 * (NT // 2))
            act.wait_ge(s("experts_in"), EXPERT_DMAS * 16)
            act.wait_ge(s("router_in"), 16)
            act.activation(wr_hi[:], wr, ACT.Copy).then_inc(s("w_hi"), 1)
            for hi, w in ((w1_hi, w1), (w2_hi, w2)):
                for c in range(4):
                    n = w.shape[1] // 4
                    act.activation(by_part(hi[c], n), w[:, c * n:(c + 1) * n], ACT.Copy).then_inc(s("w_hi"), 1)

            def x_hi(t, slot):
                act.wait_ge(s("ex_tp"), t + 1)
                if later(t, 2):
                    act.wait_ge(s("ex_hmm"), 4 * t - 4)
                act.activation(xt_hi[:, slot, :], bank[slot][:], ACT.Copy).then_inc(s("ex_xhi"), 1)

            def exps(t):
                act.wait_ge(s("ex_nmax"), t + 1)
                act.activation(pr[:], lg[:], ACT.Exp, bias=nmax[:], accum_out=psum_[:]).then_inc(s("ex_exp"), 1)

            def gelu(n, q):
                act.wait_ge(s("ex_hmm"), n + 1)
                wait_past(act, s("ex_htp"), n, 2)
                act.activation(hs[:, q % 2, :], bank[2 + q % 2][:], ACT.Gelu).then_inc(s("ex_gelu"), 1)

            def h_hi(n, q):
                act.wait_ge(s("ex_htp"), n + 1)
                wait_past(act, s("ex_ymm"), n, 2)
                act.activation(ht_hi[:, q % 2, :], bank[4][:], ACT.Copy).then_inc(s("ex_hhi"), 1)
            x_hi(0, 0)
            exps(0)
            gelu(0, 0)
            gelu(1, 1)

            def moe(t, j, r):
                more = not_last(t)
                for q in range(4):
                    h_hi(t * 4 + q, q)
                    if q == 1 and more:
                        x_hi(t + 1, (j + 1) % 2)
                    if q < 2 or more:
                        gelu(t * 4 + (q + 2), q)
                    if q == 2 and more:
                        exps(t + 1)
            turns(act, moe, NT, 4)

        @block.vector
        def _(dve):
            dve.wait_ge(s("p_set"), 11)
            dve.tensor_copy(ident_b[:], ident[:]).then_inc(s("ident_ready"), 1)
            dve.memset(mean_var[:], 0.0).then_inc(s("v_set"), 1)
            dve.wait_ge(s("setup_in"), SETUP_DMAS * 16)
            R_ = NT - 1
            dve.tensor_copy(s_last[0:R_, :], s_last[0:R_, :].bitcast(I32)).then_inc(s("v_set"), 1)
            dve.wait_ge(s("v_set"), 2)
            dve.tensor_scalar(s_d[0:R_, 0:ET], s_last[0:R_, :], thr[0:R_, :], None, ALU.is_lt).then_inc(s("v_set"), 1)
            dve.wait_ge(s("v_set"), 3)
            dve.tensor_reduce(small[0:R_, 0:1], s_d[0:R_, 0:ET], AX.X, ALU.add).then_inc(s("v_set"), 1)
            dve.wait_ge(s("v_set"), 4)
            dve.scalar_tensor_tensor(small[0:R_, 1:2], thr[0:R_, :], 1.0 / P, small[0:R_, 0:1], ALU.mult, ALU.add)\
                .then_inc(s("v_set"), 1)
            dve.wait_ge(s("v_set"), 5)
            dve.tensor_scalar(s_cnt[0:R_, :], s_io[0:R_, :], small[0:R_, 1:2], None, ALU.is_ge).then_inc(s("tab_begun"), 1)
            n = 0
            for w, a, b, lo in ((s_w, s_al, s_bs, 0), (s_w2, s_ar, s_bd, H)):
                for c in range(KC):
                    dve.tensor_tensor(s_tmp[:, c, :], w[:, c, :], a, ALU.mult).then_inc(s("fold_v"), 1)
                n += KC
                dve.wait_ge(s("fold_v"), n)
                dve.tensor_reduce(wlr[:, :, lo:lo + H], s_tmp.rearrange("p c (h f) -> p c h f", f=HF), AX.X, ALU.add)\
                    .then_inc(s("fold_v"), 1)
                n += 1
                dve.wait_ge(s("fold_v"), n)
                dve.tensor_tensor(s_tmp[:, 0, :], b, a, ALU.mult).then_inc(s("fold_v"), 1)
                n += 1
                dve.wait_ge(s("fold_v"), n)
                dve.tensor_reduce(blr[:, lo:lo + H], s_tmp[:, 0, :].rearrange("p (h f) -> p h f", f=HF), AX.X, ALU.add)\
                    .then_inc(s("fold_v"), 1)
                n += 1
                dve.wait_ge(s("fold_v"), n)
            dve.wait_ge(s("tab_mm"), 1)
            dve.tensor_scalar(d128[:, 0:ST // 2], bank[4][:, 0:ST // 2], float(P), None, ALU.mult)
            dve.tensor_scalar(d128[:, ST // 2:], bank[5][:, 0:ST // 2], float(P), None, ALU.mult)
            dve.tensor_copy(s_d[0:1, 0:ST // 2], bank[4][0:1, 0:ST // 2])
            dve.tensor_copy(s_d[0:1, ST // 2:ST], bank[5][0:1, 0:ST // 2]).then_inc(s("tab_d"), 1)
            dve.wait_ge(s("tab_d"), 1)
            dve.tensor_copy(d_tab[:], s_d[0:1, 0:ST])
            dve.tensor_tensor(s_tmp[0:1, 0:2, :].rearrange("o a b -> o (a b)")[:, 0:ST], s_io[0:1, :], s_d[0:1, 0:ST],
                              ALU.subtract).then_inc(s("tab_k"), 1)
            k_row = s_tmp[0:1, 0:2, :].rearrange("o a b -> o (a b)")[:, 0:ST]
            c_row = s_tmp[0:1, 2:4, :].rearrange("o a b -> o (a b)")[:, 0:ST]
            dve.wait_ge(s("tab_k"), 1)
            dve.tensor_scalar(c_row, k_row, 1.0 / CJ, 0.5 / CJ - 0.5, ALU.mult, ALU.add).then_inc(s("tab_k"), 1)
            dve.wait_ge(s("tab_k"), 2)
            dve.tensor_scalar(c_row, c_row, ROUND, -ROUND, ALU.add, ALU.add).then_inc(s("tab_k"), 1)
            dve.tensor_scalar(k_row, k_row, float(CH), None, ALU.mult).then_inc(s("tab_k"), 1)
            dve.wait_ge(s("tab_k"), 4)
            dve.scalar_tensor_tensor(k_row, c_row, float(1 - CH * CJ), k_row, ALU.mult, ALU.add).then_inc(s("tab_k"), 1)
            dve.tensor_tensor(s_cnt[0:1, 0:ST - 1], s_d[0:1, 1:ST], s_d[0:1, 0:ST - 1], ALU.subtract)
            dve.memset(s_cnt[0:1, ST - 1:ST], 0.0).then_inc(s("tab_d"), 1)
            dve.wait_ge(s("tab_k"), 5)
            dve.wait_ge(s("tab_d"), 2)
            dve.tensor_copy(k_tab[:], k_row)
            dve.scalar_tensor_tensor(c_row, s_d[0:1, 0:ST], float(ET), k_row, ALU.add, ALU.subtract).then_inc(s("tab_k"), 1)
            dve.wait_ge(s("tab_k"), 6)
            dve.tensor_tensor(c_row, c_row, s_cnt[0:1, :], ALU.mult).then_inc(s("tab_k"), 1)
            dve.wait_ge(s("tab_k"), 7)
            dve.tensor_tensor(keep_tab[:], c_row, k_row, ALU.add)
            dve.memset(s_cnt[0:1, ST - 1:ST], 1.0).then_inc(s("tab_d"), 1)
            dve.wait_ge(s("tab_d"), 3)
            dve.scalar_tensor_tensor(turn_tab[:], s_d[0:1, 0:ST], 1.0, s_cnt[0:1, :], ALU.add, ALU.mult)\
                .then_inc(s("tab_ready"), 1)

            def stats(t, slot, r):
                dve.wait_ge(s(f"st_x{slot}"), (r + 1) * 16)
                wait_past(dve, s("st_agg"), t, 1)
                dve.bn_stats(bn[:], xs[:, slot, :]).then_inc(s("st_seen"), 1)
                wait_past(dve, s("st_kept"), t, 1)
                apart(dve, s("st_seen"), t + 1)
                dve.bn_aggr(ag[:], bn[:]).then_inc(s("st_agg"), 1)
                dve.wait_ge(s("st_agg"), t + 1)
                dve.tensor_copy(mv_flat[:, bass.ds(t * 2, 2)], ag[:]).then_inc(s("st_kept"), 1)
            turns(dve, stats)
            dve.wait_ge(s("st_kept"), NT)
            dve.tensor_scalar(rstd[:], mean_var[:, :, 1], LN_EPS, None, ALU.add).then_inc(s("st_var"), 1)
            dve.wait_ge(s("st_sqrt"), 1)
            dve.reciprocal(rstd[:], rstd[:]).then_inc(s("st_rstd"), 1)
            dve.wait_ge(s("st_rstd"), 1)

            def normed(out_, in_, t):
                return dve.tensor_scalar(out_, in_, mv_flat[:, bass.ds(t * 2, 1)], rstd[:, bass.ds(t, 1)],
                                         ALU.subtract, ALU.mult)

            def score_out(t, slot):
                dve.wait_ge(s("sc_mm"), t + 1)
                dve.tensor_tensor(el_er_flat[:, bass.ds(t * 2 * H, 2 * H)], bank[2 + slot][:, 0:2 * H], blr, ALU.add).then_inc(s("sc_out"), 1)

            def scores(t, slot, r):
                dve.wait_ge(s(f"sc_x{slot}"), (r + 1) * 16)
                wait_past(dve, s("sc_tp"), t, 1)
                normed(xn, xs[:, slot, :], t).then_inc(s("sc_xn"), 1)
                if later(t, 1):
                    score_out(t - 1, 1 - slot)
            turns(dve, scores)
            score_out(NT - 1, (NT - 1) % 2)
            dve.wait_ge(s("sc_out"), NT)
            for i in range(3):
                rest = el_er[:, :, H:2 * H] if i == 0 else er_rest[:]
                dve.tensor_copy(er_parts[:, :, i, :], rest).then_inc(s("er_split"), 1)
                dve.wait_ge(s("er_split"), 2 * i + 1)
                if i < 2:
                    dve.tensor_tensor(er_rest[:], rest, er_parts[:, :, i, :], ALU.subtract).then_inc(s("er_split"), 1)
                    dve.wait_ge(s("er_split"), 2 * i + 2)

            dve.wait_ge(s("weights_in"), WEIGHT_DMAS * 16)

            def kv_add(t):
                dve.wait_ge(s("pj_kv"), t + 1)
                wait_past(dve, s("pj_kva"), t, 1)
                dve.tensor_tensor(at_acc, at_acc, bank[6][:, 0:KC * HF + 2], ALU.add).then_inc(s("pj_kva"), 1)

            def proj(t, slot, r):
                if isinstance(t, int) and t == 0:
                    dve.wait_ge(s("pj_x0"), 16)
                    normed(xn, xs[:, 0, :], 0).then_inc(s("pj_xn"), 1)
                if not (isinstance(t, int) and t == NT - 1):
                    dve.wait_ge(s(f"pj_x{1 - slot}"), (r + (1 if slot == 0 else 2)) * 16)
                    dve.wait_ge(s("pj_tp"), t + 1)
                    normed(xn, xs[:, 1 - slot, :], t + 1).then_inc(s("pj_xn"), 1)
                dve.wait_ge(s("pj_v"), t + 1)
                if later(t, 2):
                    dve.wait_ge(s(f"pj_st{slot}"), r * 16)
                dve.tensor_tensor(vs[:, slot, :], bank[2][:], bv_all, ALU.add).then_inc(s("pj_vout"), 1)
                if later(t, 1):
                    kv_add(t - 1)
                dve.wait_ge(s("pj_k"), t + 1)
                wait_past(dve, s("pj_kf"), t, 1)
                dve.tensor_scalar_min(ex[:, 0, :], bank[4][:, 0:2 * P], 0.0).then_inc(s("pj_kmin"), 1)
                dve.wait_ge(s("pj_kexp"), t + 1)
                wait_past(dve, s("pj_kv"), t, 1)
                dve.scalar_tensor_tensor(kf, bank[4][:, 0:2 * P], 0.0, ex[:, 0, :], ALU.max, ALU.add)\
                    .then_inc(s("pj_kf"), 1)
                dve.wait_ge(s("pj_q"), t + 1)
                wait_past(dve, s("pj_qf"), t, 1)
                dve.tensor_scalar_min(ex[:, 1, :], bank[5][:, 0:2 * P], 0.0).then_inc(s("pj_qmin"), 1)
                dve.wait_ge(s("pj_qexp"), t + 1)
                dve.scalar_tensor_tensor(q_feat[:, :, bass.ds(t * P, P)],
                                         bank[5][:, 0:2 * P].rearrange("p (c t) -> p c t", c=2), 0.0,
                                         ex[:, 1, :].rearrange("p (c t) -> p c t", c=2), ALU.max, ALU.add)\
                    .then_inc(s("pj_qf"), 1)
            turns(dve, proj)
            kv_add(NT - 1)
            dve.wait_ge(s("pj_kva"), NT)
            for j in range(KC):
                for i in range(2):
                    b = (2 * j + i) % 4
                    dve.tensor_copy(kvt_diag[i * HF:(i + 1) * HF, j, b * HD:(b + 1) * HD],
                                    kvt_acc[i * HF:(i + 1) * HF, j, i * HD:(i + 1) * HD])
            for c in range(2):
                for b in range(4):
                    r_ = slice(b * HD, (b + 1) * HD)
                    last = dve.tensor_scalar(ks_diag[r_, c, r_], ones[r_, r_], ks_acc[r_, c:c + 1], None, ALU.mult)
            last.then_inc(s("g_in"), 1)

            def mix(t, slot, r):
                dve.wait_ge(s(f"mx_x{slot}"), (r + 1) * 16)
                if later(t, 2):
                    dve.wait_ge(s(f"mx_st{slot}"), r * 16)
                elif t == 0:
                    dve.wait_ge(s("pj_st0"), 16 * (NT // 2 + 1))
                    dve.wait_ge(s("pj_st1"), 16 * (NT // 2))
                dve.tensor_tensor(vs[:, slot, :], xs[:, slot, :], bo_all, ALU.add).then_inc(s("mx_xb"), 1)
                dve.wait_ge(s("mx_norm"), t + 1)
                dve.tensor_scalar(ex[:, 0, :], bank[slot][:, 0:2 * P], 1e-6, None, ALU.add).then_inc(s("mx_n1"), 1)
                dve.wait_ge(s("mx_n1"), t + 1)
                dve.reciprocal(ex[:, 0, :], ex[:, 0, :]).then_inc(s("mx_n2"), 1)
                dve.wait_ge(s("mx_n2"), t + 1)
                wait_past(dve, s("mx_mm"), t, 2)
                dve.tensor_tensor(qn[slot], q_feat[:, :, bass.ds(t * P, P)],
                                  ex[:, 0, :].rearrange("p (c t) -> p c t", c=2), ALU.mult).then_inc(s("mx_qn"), 1)
                dve.wait_ge(s("mx_mm"), t + 1)
                dve.wait_ge(s("mx_xb"), t + 1)
                dve.tensor_tensor(vs[:, slot, :], vs[:, slot, :], bank[2 + slot][:], ALU.add).then_inc(s("mx_out"), 1)
            turns(dve, mix)

            dve.memset(same, 0.0)
            dve.memset(er_got, 0.0).then_inc(s("same_set"), 1)
            dve.wait_ge(s("same_set"), 1)
            by_group = d128[:].rearrange("p (g i) -> p g i", i=G)
            dve.tensor_tensor(same[:, :, 0, 2:], by_group[:, :, 1:], by_group[:, :, :G - 1], ALU.subtract)
            dve.tensor_tensor(same[:, 1:, 0, 1], by_group[:, 1:, 0], by_group[:, :SG - 1, G - 1], ALU.subtract)\
                .then_inc(s("same_set"), 1)
            dve.wait_ge(s("same_set"), 2)
            dve.tensor_scalar(same[:, :, 0, :], same[:, :, 0, :], 1.0 / P, None, ALU.mult).then_inc(s("same_set"), 1)
            dve.wait_ge(s("same_set"), 3)
            dve.tensor_copy(same[:, :, 1:, :], same[:, :, 0:1, :].broadcast_to([P, SG, H - 1, 1 + G])).then_inc(s("same_set"), 1)
            dve.wait_ge(s("same_set"), 4)
            same_flat = same.rearrange("p g h i -> p (g h i)")

            def er_sum(g, slot):
                dve.wait_ge(s("er_mm"), g + 1)
                dve.tensor_reduce(er_got[:, slot, :, 1:], bank[slot][:, 0:G * 3 * H].rearrange("p (g i h) -> p h g i", g=G, i=3),
                                  AX.X, ALU.add).then_inc(s("er_got"), 1)
                if later(g, 1):
                    dve.wait_ge(s("er_summed"), g)
                    dve.tensor_copy(er_got[:, slot, :, 0], er_run[:, 1 - slot, :, G]).then_inc(s("er_carried"), 1)
                    dve.wait_ge(s("er_carried"), g)
                dve.wait_ge(s("er_got"), g + 1)
                wait_past(dve, s("er_kept"), g, 2)
                n = H * (1 + G)
                dve.tensor_tensor_scan(er_run[:, slot].rearrange("p h i -> p (h i)"), same_flat[:, bass.ds(g * n, n)],
                                       er_got[:, slot].rearrange("p h i -> p (h i)"), 0.0, ALU.mult, ALU.add).then_inc(s("er_summed"), 1)

            def expand(g, slot, r):
                dve.wait_ge(s("ends_stepped"), g + 1)
                dve.tensor_tensor(dst_local[:, bass.ds(g * G, G)], ends_step[:, 1, bass.ds(g * G, G)],
                                  d128[:, bass.ds(g * G, G)], ALU.subtract).then_inc(s("dst_stepped"), 1)
                dve.wait_ge(s("dst_stepped"), g + 1)
                wait_past(dve, s("er_tp"), g, 2)
                dve.tensor_tensor(hot_b[:, slot], col_no[:].unsqueeze(1).broadcast_to([P, G, P]),
                                  dst_local[:, bass.ds(g * G, G)].unsqueeze(2).broadcast_to([P, G, P]), ALU.is_equal)\
                    .then_inc(s("er_hot"), 1)
                if later(g, 2):
                    er_sum(g - 2, slot)
            turns(dve, expand, SG, peeled=2)
            for g in (SG - 2, SG - 1):
                er_sum(g, g % 2)

            dve.wait_ge(s("dst_scan_in"), 16 * CH)
            dve.wait_ge(s("er_summed"), SG)
            dve.tensor_tensor(t_pen[:, 1:CL], dst_scan[:, 1:CL], dst_scan[:, 0:CL - 1], ALU.not_equal).then_inc(s("scan_v"), 1)
            dve.tensor_copy(edge_first[:, 0:1], dst_scan[:, 0:1])
            dve.tensor_copy(edge_first[:, 1:2], dst_scan[:, CL - 1:CL])
            dve.memset(t_pen[:, 0:1], 0.0)
            dve.memset(t_pen[:, CL:CL + 1], 0.0).then_inc(s("scan_v"), 1)
            dve.wait_ge(s("scan_v"), 2)
            dve.tensor_scalar(t_pen[:, 1:CL], t_pen[:, 1:CL], -BIG, None, ALU.mult).then_inc(s("scan_v"), 1)
            dve.wait_ge(s("scan_v"), 3)
            dve.wait_ge(s("tp_el_out"), -(-CJ // 4))
            dve.tensor_tensor_scan(t_run, t_pen[:, 0:CL], t_el, -BIG, ALU.add, ALU.max).then_inc(s("scan_v"), 1)
            dve.wait_ge(s("scan_v"), 4)
            dve.tensor_copy(edge_first[:, 2:3], t_run[:, CL - 1:CL]).then_inc(s("scan_ends"), 1)

            def R(i):
                return row[0:1, i, :]
            FIRST, LAST, RUN, CONN, WHOLE, PEN_IN, PEN_W, OUT_, IN_, PEN_INB, PEN_WB = range(11)
            hc = lambda a: a.rearrange("o (h c) -> o h c", c=CH)
            n = 0

            def link(ins):
                nonlocal n
                n += 1
                ins.then_inc(s("row_v"), 1)
                dve.wait_ge(s("row_v"), n)
            dve.wait_ge(s("ends_tp"), 1)
            for i in range(3):
                link(dve.tensor_copy(hc(R(i)), bank[5][0:1, i * P:(i + 1) * P].rearrange("o (c h) -> o h c", h=H)))
            link(dve.memset(R(CONN), 0.0))
            link(dve.tensor_tensor(hc(R(CONN))[:, :, 1:CH], hc(R(FIRST))[:, :, 1:CH], hc(R(LAST))[:, :, 0:CH - 1], ALU.is_equal))
            link(dve.tensor_tensor(R(WHOLE), R(FIRST), R(LAST), ALU.is_equal))
            link(dve.tensor_scalar(R(PEN_IN), R(CONN), BIG, -BIG, ALU.mult, ALU.add))
            link(dve.tensor_tensor(R(PEN_W), R(CONN), R(WHOLE), ALU.mult))
            link(dve.tensor_scalar(R(PEN_W), R(PEN_W), BIG, -BIG, ALU.mult, ALU.add))
            link(dve.memset(R(PEN_INB), -BIG))
            link(dve.tensor_copy(hc(R(PEN_INB))[:, :, 0:CH - 1], hc(R(PEN_IN))[:, :, 1:CH]))
            link(dve.tensor_scalar(R(PEN_WB), R(WHOLE), BIG, -BIG, ALU.mult, ALU.add))
            link(dve.tensor_tensor(R(PEN_WB), R(PEN_WB), R(PEN_INB), ALU.min))
            link(dve.tensor_tensor_scan(R(OUT_), R(PEN_W), R(RUN), -BIG, ALU.add, ALU.max))
            link(dve.memset(R(IN_), -BIG))
            link(dve.tensor_tensor(hc(R(IN_))[:, :, 1:CH], hc(R(OUT_))[:, :, 0:CH - 1], hc(R(PEN_IN))[:, :, 1:CH], ALU.add))
            dve.tensor_scalar_max(R(11).rearrange("o (c h) -> o h c", h=H), hc(R(IN_)), -BIG).then_inc(s("row_in"), 1)
            dve.wait_ge(s("row_back"), 1)
            dve.tensor_copy(col[:, 0:1], bank[6][:, 0:1]).then_inc(s("scan_v"), 1)
            dve.wait_ge(s("scan_v"), 5)
            dve.tensor_tensor_scan(t_run, t_pen[:, 0:CL], t_el, col[:, 0:1], ALU.add, ALU.max).then_inc(s("scan_v"), 1)
            dve.wait_ge(s("scan_v"), 6)
            dve.tensor_tensor_scan(t_el[:, ::-1], t_pen[:, 1:CL + 1][:, ::-1], t_run[:, ::-1], -BIG, ALU.add, ALU.max)\
                .then_inc(s("scan_v"), 1)
            dve.wait_ge(s("scan_v"), 7)
            dve.tensor_copy(edge_first[:, 3:4], t_el[:, 0:1]).then_inc(s("scan_ends"), 1)
            dve.wait_ge(s("ends_tp"), 2)
            link(dve.tensor_copy(hc(R(RUN)), bank[5][0:1, 0:P].rearrange("o (c h) -> o h c", h=H)))
            link(dve.tensor_tensor_scan(R(OUT_)[:, ::-1], R(PEN_WB)[:, ::-1], R(RUN)[:, ::-1], -BIG, ALU.add, ALU.max))
            link(dve.memset(R(IN_), -BIG))
            link(dve.tensor_tensor(hc(R(IN_))[:, :, 0:CH - 1], hc(R(OUT_))[:, :, 1:CH], hc(R(PEN_INB))[:, :, 0:CH - 1], ALU.add))
            dve.tensor_scalar_max(R(11).rearrange("o (c h) -> o h c", h=H), hc(R(IN_)), -BIG).then_inc(s("row_in"), 1)
            dve.wait_ge(s("row_back"), 2)
            dve.tensor_copy(col[:, 1:2], bank[6][:, 0:1]).then_inc(s("scan_v"), 1)
            dve.wait_ge(s("scan_v"), 8)
            dve.tensor_tensor_scan(t_el[:, ::-1], t_pen[:, 1:CL + 1][:, ::-1], t_run[:, ::-1], col[:, 1:2], ALU.add, ALU.max)\
                .then_inc(s("scan_done"), 1)

            dve.wait_ge(s("er_kept"), SG)
            dve.wait_ge(s("el_kept"), CJ)
            dve.tensor_tensor(e_el, e_el, e_er, ALU.add).then_inc(s("sm"), 1)
            dve.wait_ge(s("sm"), 1)
            dve.scalar_tensor_tensor(e_el, e_el, NEG_SLOPE, e_el, ALU.mult, ALU.max).then_inc(s("sm"), 1)
            dve.wait_ge(s("tp_m_out"), -(-CJ // 4))
            dve.tensor_tensor(e_m, e_m, e_er, ALU.add).then_inc(s("sm"), 1)
            dve.wait_ge(s("sm"), 3)
            dve.scalar_tensor_tensor(e_m, e_m, NEG_SLOPE, e_m, ALU.mult, ALU.max).then_inc(s("sm"), 1)
            dve.wait_ge(s("sm"), 4)
            dve.tensor_tensor(e_el, e_el, e_m, ALU.subtract).then_inc(s("sm_diff"), 1)
            dve.wait_ge(s("p_ready"), 1)

            places = []
            def step(t, j, r):
                if j % V == 0:
                    wait_past(dve, s("step_mm"), t, V + 1)
                    dve.tensor_tensor(hot[:, j // V % 2], col_no[:].unsqueeze(1).broadcast_to([P, V, P]),
                                      dst_local[:, bass.ds(t, V)].unsqueeze(2).broadcast_to([P, V, P]), ALU.is_equal)
                if j % V == 0:
                    places[:] = looked_up(ENGINE.DVE, k_tab, t, V, ET - 1)
                k, b = places[j % V], j % V
                wait_past(dve, s("step_mm"), t, V)
                dve.tensor_copy(pv[:, b, D:D + H], e_el_flat[:, bass.ds(k * H, H)])
                dve.wait_ge(gathered[j], (r + 1) * 16)
                dve.tensor_tensor(pv[:, b, 0:D].rearrange("p (h f) -> p h f", h=H),
                                  vg[:, j, :].rearrange("p (h f) -> p h f", h=H),
                                  e_el_flat[:, bass.ds(k * H, H)].unsqueeze(2).broadcast_to([P, H, HF]),
                                  ALU.mult).then_inc(s("step_pv"), 1)
            turns(dve, step, ST, U)

            def w_lo(lo, w, hi, c, n):
                dve.wait_ge(s("w_hi"), n)
                m = w.shape[1] // 4
                dve.tensor_tensor(by_part(lo[c], m), w[:, c * m:(c + 1) * m], by_part(hi[c], m).bitcast(F32), ALU.subtract)\
                    .then_inc(s("w_lo"), 1)

            def join(t, j, r):
                slot = j % 2
                dve.wait_ge(s(f"jn_a{slot}"), r * 32 + 16 * (j // 2 + 1))
                if later(t, 1):
                    dve.wait_ge(s("jn_n"), t * 3)
                dve.tensor_scalar_max(den[:], da[:, slot, D:D + H], 1e-16).then_inc(s("jn_n"), 1)
                dve.wait_ge(s("jn_n"), t * 3 + 1)
                dve.reciprocal(den[:], den[:]).then_inc(s("jn_n"), 1)
                dve.wait_ge(s("jn_n"), t * 3 + 2)
                by_head = da[:, slot, 0:D].rearrange("p (h f) -> p h f", h=H)
                dve.tensor_tensor(by_head, by_head, den[:].unsqueeze(2).broadcast_to([P, H, HF]), ALU.mult).then_inc(s("jn_n"), 1)
                dve.wait_ge(s("jn_n"), t * 3 + 3)
                dve.wait_ge(s(f"jn_b{j}"), (r + 1) * 16)
                dve.tensor_tensor(dx[:, j, :], da[:, slot, 0:D], dx[:, j, :], ALU.add).then_inc(s("jn_x"), 1)
                wait_past(dve, s("jn_ag"), t, 1)
                dve.wait_ge(s("jn_x"), t + 1)
                dve.bn_stats(bn[:], dx[:, j, :]).then_inc(s("jn_bn"), 1)
                apart(dve, s("jn_bn"), t + 1)
                wait_past(dve, s("ex_xn"), t, 1)
                dve.bn_aggr(ag[:], bn[:]).then_inc(s("jn_ag"), 1)
                dve.wait_ge(s("jn_inv"), t + 1)
                dve.tensor_scalar(da[:, slot, 0:D], dx[:, j, :], ag[:, 0:1], inv[:], ALU.subtract, ALU.mult)\
                    .then_inc(s("ex_xn"), 1)

            def x_lo(t, slot):
                dve.wait_ge(s("ex_xhi"), t + 1)
                dve.tensor_tensor(xt_lo[:, slot, :], bank[slot][:], xt_hi[:, slot, :].bitcast(F32), ALU.subtract)\
                    .then_inc(s("ex_xt"), 1)

            def gates(t, slot):
                n = 0

                def link(ins):
                    nonlocal n
                    n += 1
                    ins.then_inc(s("ex_g"), 1)
                    apart(dve, s("ex_g"), t * 9 + n)
                dve.wait_ge(s("ex_lg"), t + 1)
                link(dve.tensor_copy(lg[:], bank[6][:, 0:X]))
                link(dve.max(top[:], lg[:]))
                dve.tensor_scalar(nmax[:], top[:, 0:1], -1.0, None, ALU.mult).then_inc(s("ex_nmax"), 1)
                dve.wait_ge(s("ex_exp"), t + 1)
                link(dve.reciprocal(psum_[:], psum_[:]))
                link(dve.tensor_scalar(pr[:], pr[:], psum_[:], None, ALU.mult))
                link(dve.max(ptop[:], pr[:]))
                link(dve.max_index(pidx[:], ptop[:], pr[:]))
                link(dve.tensor_copy(pidf[:], pidx[:]))
                dve.scalar_tensor_tensor(ga[:], col_no[:, 0:X], pidf[:, 0:1], pr[:], ALU.is_equal, ALU.mult)
                link(dve.scalar_tensor_tensor(gb[:], col_no[:, 0:X], pidf[:, 1:2], pr[:], ALU.is_equal, ALU.mult))
                link(dve.tensor_tensor(gate[:, slot, :], ga[:], gb[:], ALU.add))

            def gated(n, q, slot):
                dve.wait_ge(s("ex_gelu"), n + 1)
                by_expert = hs[:, q % 2, :].rearrange("p (e f) -> p e f", e=2)
                dve.tensor_tensor(by_expert, by_expert, gate[:, slot, 2 * q:2 * q + 2].unsqueeze(2).broadcast_to([P, 2, XF]),
                                  ALU.mult).then_inc(s("ex_hs"), 1)

            def h_lo(n, q):
                dve.wait_ge(s("ex_hhi"), n + 1)
                dve.tensor_tensor(ht_lo[:, q % 2, :], bank[4][:], ht_hi[:, q % 2, :].bitcast(F32), ALU.subtract)\
                    .then_inc(s("ex_ht"), 1)

            def output(t, j):
                dve.wait_ge(s("ex_ymm"), 4 * t + 4)
                dve.tensor_tensor(dx[:, j, :], dx[:, j, :], bank[5][:], ALU.add).then_inc(s("ex_out"), 1)
            dve.wait_ge(s("experts_in"), EXPERT_DMAS * 16)
            dve.wait_ge(s("router_in"), 16)
            dve.wait_ge(s("w_hi"), 1)
            dve.tensor_tensor(wr_lo[:], wr, wr_hi[:].bitcast(F32), ALU.subtract).then_inc(s("w_lo"), 1)
            for c in range(4):
                w_lo(w1_lo, w1, w1_hi, c, 2 + c)
            join(0, 0, 0)
            x_lo(0, 0)
            for c in range(4):
                w_lo(w2_lo, w2, w2_hi, c, 6 + c)
            gates(0, 0)
            gated(0, 0, 0)

            def moe(t, j, r):
                more = not_last(t)
                slot, nslot = j % 2, (j + 1) % 2
                for q in range(4):
                    h_lo(t * 4 + q, q)
                    if q == 0:
                        if later(t, 1):
                            output(t - 1, (j - 1) % 4)
                    if q == 1 and more:
                        x_lo(t + 1, nslot)
                    if q < 3:
                        gated(t * 4 + (q + 1), q + 1, slot)
                    elif more:
                        gated(t * 4 + 4, 0, nslot)
                    if q == 0 and more:
                        join(t + 1, (j + 1) % 4, (r if j < 3 else r + 1))
                    if q == 2 and more:
                        gates(t + 1, nslot)
            turns(dve, moe, NT, 4)
            output(NT - 1, (NT - 1) % 4)

        @block.tensor
        def _(pe):
            def product(dst, pairs, opened=True, closed=True):
                n = len(pairs)
                for i, (a, b) in enumerate(pairs):
                    last = pe.matmul(dst, a, b, start=(opened and i == 0), stop=(closed and i == n - 1))
                return last

            def transposed(dst, src, n=KC):
                for c in range(n):
                    last = pe.transpose(dst[:, c * P:(c + 1) * P], src[:, c * P:(c + 1) * P], ident[:])
                return last

            pe.wait_ge(s("ident_ready"), 1)
            pe.wait_ge(s("tab_begun"), 1)
            for i in range(2):
                last = product(bank[4 + i][:, 0:ST // 2], [(ones[0:NT - 1, :], s_cnt[0:NT - 1, i * (ST // 2):(i + 1) * (ST // 2)])])
            last.then_inc(s("tab_mm"), 1)
            pe.wait_ge(s("weights_in"), WEIGHT_DMAS * 16)
            for c in range(KC):
                for j in range(8):
                    last = product(bank[c][:, j * HF:(j + 1) * HF], [(s_wqt[:, j, c * P:(c + 1) * P], r_diag)])
                last.then_inc(s("fold_mm"), 1)
            pe.wait_ge(s("fold_out"), KC)
            pe.wait_ge(s("fold_v"), 14)

            def scores(t, slot, r):
                pe.wait_ge(s("sc_xn"), t + 1)
                wait_past(pe, s("sc_xt"), t, 2)
                transposed(bank[slot], xn).then_inc(s("sc_tp"), 1)
                pe.wait_ge(s("sc_xt"), t + 1)
                wait_past(pe, s("sc_out"), t, 2)
                product(bank[2 + slot][:, 0:2 * H], [(xt[:, slot, c * P:(c + 1) * P], wlr[:, c, :]) for c in range(KC)])\
                    .then_inc(s("sc_mm"), 1)
            turns(pe, scores)
            pe.wait_ge(s("sc_out"), NT)

            def chunks(slot):
                return [xt[:, slot, c * P:(c + 1) * P] for c in range(KC)]

            def kv(t):
                pe.wait_ge(s("pj_mvs"), t + 1)
                pe.wait_ge(s("pj_kf"), t + 1)
                wait_past(pe, s("pj_kva"), t, 1)
                for j in range(KC):
                    product(bank[6][:, j * HF:(j + 1) * HF], [(mv[:, j * P:(j + 1) * P], kf[:, j * HF:(j + 1) * HF])])
                for c in range(2):
                    last = product(bank[6][:, KC * HF + c:KC * HF + c + 1],
                                   [(kf[:, c * P:(c + 1) * P], real_row[:, bass.ds(t, 1)])])
                last.then_inc(s("pj_kv"), 1)

            def turn_over(t, slot):
                pe.wait_ge(s("pj_xn"), t + 1)
                wait_past(pe, s("pj_xt"), t, 2)
                transposed(bank[slot], xn).then_inc(s("pj_tp"), 1)

            def proj(t, slot, r):
                if isinstance(t, int) and t == 0:
                    turn_over(0, 0)
                pe.wait_ge(s("pj_xt"), t + 1)
                wait_past(pe, s("pj_vout"), t, 1)
                product(bank[2][:], [(a, wv[:, c, :]) for c, a in enumerate(chunks(slot))]).then_inc(s("pj_v"), 1)
                if later(t, 1):
                    kv(t - 1)
                    pe.wait_ge(s("pj_mvs"), t)
                product(bank[3][:], [(a, wmv[:, c, :]) for c, a in enumerate(chunks(slot))]).then_inc(s("pj_mv"), 1)
                wait_past(pe, s("pj_kf"), t, 1)
                product(bank[4][:, 0:2 * P], [(a, wqk[:, c, 2 * P:4 * P]) for c, a in enumerate(chunks(slot))])\
                    .then_inc(s("pj_k"), 1)
                if not (isinstance(t, int) and t == NT - 1):
                    turn_over(t + 1, 1 - slot)
                wait_past(pe, s("pj_qf"), t, 1)
                for i in range(2):
                    last = product(bank[5][:, i * P:(i + 1) * P],
                                   [(wqk[:, c, i * P:(i + 1) * P], a) for c, a in enumerate(chunks(slot))])
                last.then_inc(s("pj_q"), 1)
            turns(pe, proj)
            kv(NT - 1)

            pe.wait_ge(s("g_in"), 1)
            for c in range(2):
                last = product(bank[c][:], [(kvt_diag[:, j, :], wo[:, j, :]) for j in (2 * c, 2 * c + 1)])
            last.then_inc(s("g_mm"), 1)
            pe.wait_ge(s("g_out"), 2)

            def mix(t, slot, r):
                wait_past(pe, s("mx_n1"), t, 2)
                for c in range(2):
                    last = product(bank[slot][:, c * P:(c + 1) * P], [(ks_diag[:, c, :], q_feat[:, c, bass.ds(t * P, P)])])
                last.then_inc(s("mx_norm"), 1)
                pe.wait_ge(s("mx_qn"), t + 1)
                wait_past(pe, s("mx_out"), t, 2)
                product(bank[2 + slot][:], [(qn[slot][:, c, :], g_mat[:, c, :]) for c in range(2)]).then_inc(s("mx_mm"), 1)
            turns(pe, mix)

            def er_of(g, slot):
                pe.wait_ge(s("er_hot_t"), g + 1)
                wait_past(pe, s("er_got"), g, 2)
                for i, d in enumerate(looked_up(ENGINE.PE, d_tab, g * G, G, NT - 1)):
                    last = product(bank[slot][:, i * 3 * H:(i + 1) * 3 * H],
                                   [(hot_t[:, slot, i * P:(i + 1) * P], er_flat[:, bass.ds(d * 3 * H, 3 * H)])])
                last.then_inc(s("er_mm"), 1)

            def expand(g, slot, r):
                pe.wait_ge(s("er_hot"), g + 1)
                wait_past(pe, s("er_hot_t"), g, 2)
                for i in range(G):
                    last = pe.transpose(turned_hot[slot][:, i * P:(i + 1) * P], hot_b[:, slot, i, :], ident_b[:])
                last.then_inc(s("er_tp"), 1)
                if later(g, 1):
                    er_of(g - 1, 1 - slot)
            pe.wait_ge(s("mx_out"), NT)
            turns(pe, expand, SG, peeled=2)
            er_of(SG - 1, 1)
            pe.wait_ge(s("er_summed"), SG)

            pe.wait_ge(s("el_kept"), CJ)
            for g in range(-(-CJ // 4)):
                if g >= 4:
                    pe.wait_ge(s("tp_el_out"), g - 3)
                for i in range(min(4, CJ - 4 * g)):
                    last = pe.transpose(bank[g % 4][:, i * P:(i + 1) * P], e_el_flat[:, (4 * g + i) * P:(4 * g + i + 1) * P], ident[:])
                last.then_inc(s("tp_el"), 1)
            pe.wait_ge(s("scan_ends"), 1)
            for i in range(3):
                last = pe.transpose(bank[5][0:1, i * P:(i + 1) * P], edge_first[:, i:i + 1], ident[:])
            last.then_inc(s("ends_tp"), 1)
            in_row = row[0:1, 11, :]
            pe.wait_ge(s("row_in"), 1)
            product(bank[6][:, 0:1], [(in_row, ones[0:1, 0:1])]).then_inc(s("row_back"), 1)
            pe.wait_ge(s("scan_ends"), 2)
            pe.transpose(bank[5][0:1, 0:P], edge_first[:, 3:4], ident[:]).then_inc(s("ends_tp"), 1)
            pe.wait_ge(s("row_in"), 2)
            product(bank[6][:, 0:1], [(in_row, ones[0:1, 0:1])]).then_inc(s("row_back"), 1)
            pe.wait_ge(s("scan_done"), 1)
            pe.wait_ge(s("tp_el_out"), -(-CJ // 4))
            for g in range(-(-CJ // 4)):
                if g >= 4:
                    pe.wait_ge(s("tp_m_out"), g - 3)
                for i in range(min(4, CJ - 4 * g)):
                    last = pe.transpose(bank[g % 4][:, i * P:(i + 1) * P], t_el[:, (4 * g + i) * P:(4 * g + i + 1) * P], ident[:])
                last.then_inc(s("tp_m"), 1)
            pe.wait_ge(s("tp_m_out"), -(-CJ // 4))

            def empty(opened, closed):
                pe.matmul(bank[0][:], zeros[0:1, 0:P], zeros[0:1, :], start=opened, stop=closed)
                return pe.matmul(bank[1][:, 0:H], zeros[0:1, 0:P], zeros[0:1, 0:H], start=opened, stop=closed)

            ends = []

            def step(t, j, r):
                if j % V == 0:
                    ends[:] = looked_up(ENGINE.PE, turn_tab, t, V, NT)
                turn = ends[j % V]
                pe.wait_ge(s("step_pv"), t + 1)
                pe.matmul(bank[0][:], hot[:, j // V % 2, j % V, :], pv[:, j % V, 0:D], start=False, stop=False)
                pe.matmul(bank[1][:, 0:H], hot[:, j // V % 2, j % V, :], pv[:, j % V, D:D + H], start=False, stop=False)\
                    .then_inc(s("step_mm"), 1)
                with pe.If(turn):
                    empty(False, True).then_inc(s("tile_sum"), 1)
                    pe.wait_ge(s("tile_out"), turn)
                    empty(True, False)
            empty(True, False)
            turns(pe, step, ST, U)
            empty(False, True)

            def split_product(dst, parts, opened=True, closed=True):
                return product(dst, [pair for a, a_lo, b, b_lo in parts for pair in ((a, b), (a, b_lo), (a_lo, b))],
                               opened, closed)

            def turn_x(t, slot):
                pe.wait_ge(s("ex_xn"), t + 1)
                wait_past(pe, s("ex_xt"), t, 2)
                transposed(bank[slot], da[:, slot, 0:D]).then_inc(s("ex_tp"), 1)

            def x_parts(slot, c):
                return xt_hi[:, slot, c * P:(c + 1) * P], xt_lo[:, slot, c * P:(c + 1) * P]

            def logits(t, slot):
                if later(t, 1):
                    pe.wait_ge(s("ex_g"), (t - 1) * 9 + 1)
                split_product(bank[6][:, 0:X], [(*x_parts(slot, c), wr_hi[:, c, :], wr_lo[:, c, :]) for c in range(KC)])\
                    .then_inc(s("ex_lg"), 1)

            def hidden(n, q, slot):
                wait_past(pe, s("ex_gelu"), n, 2)
                cols = slice(q * D, (q + 1) * D)
                split_product(bank[2 + q % 2][:], [(*x_parts(slot, c), w1_hi[c][:, cols], w1_lo[c][:, cols]) for c in range(KC)])\
                    .then_inc(s("ex_hmm"), 1)

            def turned(n, q):
                pe.wait_ge(s("ex_hs"), n + 1)
                wait_past(pe, s("ex_ht"), n, 1)
                transposed(bank[4], hs[:, q % 2, :]).then_inc(s("ex_htp"), 1)

            def summed(n, q, t):
                pe.wait_ge(s("ex_ht"), n + 1)
                if q == 0:
                    wait_past(pe, s("ex_out"), t, 1)
                split_product(bank[5][:], [(ht_hi[:, q % 2, c * P:(c + 1) * P], ht_lo[:, q % 2, c * P:(c + 1) * P],
                                            w2_hi[q][:, c, :], w2_lo[q][:, c, :]) for c in range(KC)],
                              opened=(q == 0), closed=(q == 3)).then_inc(s("ex_ymm"), 1)
            turn_x(0, 0)
            pe.wait_ge(s("ex_xt"), 1)
            pe.wait_ge(s("w_lo"), 5)
            logits(0, 0)
            hidden(0, 0, 0)
            hidden(1, 1, 0)
            pe.wait_ge(s("w_lo"), 9)
            turned(0, 0)

            def moe(t, j, r):
                more = not_last(t)
                slot, nslot = j % 2, (j + 1) % 2
                for q in range(4):
                    n = t * 4 + q
                    if q == 2 and more:
                        pe.wait_ge(s("ex_xt"), t + 2)
                    if q < 2 or more:
                        hidden(t * 4 + (q + 2), (q + 2) % 4, slot if q < 2 else nslot)
                    if q == 1 and more:
                        turn_x(t + 1, nslot)
                    if q == 2 and more:
                        logits(t + 1, nslot)
                    summed(n, q, t)
                    if q < 3 or more:
                        turned(t * 4 + (q + 1), (q + 1) % 4)
            turns(pe, moe, NT, 4)


_OUT = (NP, D)


def kernel(**inputs):
    import numpy as _np
    import concourse.bacc as _bacc
    from concourse import mybir as _mybir
    from concourse.bass_utils import run_bass_kernel_spmd as _run

    def padded(a, n):
        b = _np.zeros((n,) + a.shape[1:], a.dtype)
        b[:a.shape[0]] = a
        return b

    a = {k: _np.ascontiguousarray(v) for k, v in inputs.items()}
    def columns(edges):
        return edges.reshape(CH, CJ, P).transpose(2, 1, 0).reshape(P, ET)

    src = padded(a["src"], EP)
    dst = _np.full((EP,), 2 * NP, a["dst"].dtype)
    dst[:E] = a["dst"]
    w_qkv = a["L0_mix_W_qkv"]
    laid = {
        "x": padded(a["x"], NP),
        "src_cols": columns(src), "dst_cols": columns(dst), "dst_rows": dst.reshape(CH, CL),
        "w_src": a["L0_gnn_W_src"], "b_src": a["L0_gnn_b_src"].reshape(1, D),
        "w_dst": a["L0_gnn_W_dst"], "b_dst": a["L0_gnn_b_dst"].reshape(1, D),
        "w_val": a["L0_gnn_W_val"], "b_val": a["L0_gnn_b_val"].reshape(1, D),
        "attn_l": a["L0_gnn_attn_l"].reshape(1, D), "attn_r": a["L0_gnn_attn_r"].reshape(1, D),
        "w_qk_t": w_qkv[:, :2 * D].T, "w_v": w_qkv[:, 2 * D:],
        "r_mat": a["L0_mix_random_matrix"], "w_out": a["L0_mix_W_out"],
        "b_out": a["L0_mix_b_out"].reshape(1, D), "w_r": a["L0_ffn_Wr"],
        "w_1": a["L0_ffn_W1"], "w_2": a["L0_ffn_W2"],
    }
    nc = _bacc.Bacc("TRN2", target_bir_lowering=False, num_devices=1)
    arrays, args = {}, {}
    for name, v in laid.items():
        v = _np.ascontiguousarray(v)
        arrays[f"in_{name}"] = v
        args[name] = nc.dram_tensor(f"in_{name}", v.shape, _mybir.dt.from_np(v.dtype), kind="ExternalInput").ap()
    args["out"] = nc.dram_tensor("out_0", _OUT, _mybir.dt.float32, kind="ExternalOutput").ap()
    gps_layer(nc, **args)
    r = _run(nc, [arrays], core_ids=[0])
    return r.results[0]["out_0"][:N]
```

```python
from contextlib import ExitStack

import numpy as np

import concourse.bass as bass
from concourse import mybir

F32 = mybir.dt.float32
F32R = mybir.dt.float32r
I32 = mybir.dt.int32
U16 = mybir.dt.uint16
U32 = mybir.dt.uint32
BF16 = mybir.dt.bfloat16
ALU = mybir.AluOpType
ACT = mybir.ActivationFunctionType
AX = mybir.AxisListType
ENGINE = mybir.EngineType

P = 128
N, D, E = 6250, 512, 100000
H, HF = 8, 64
HD = 32
X, XF = 8, 256
KC = D // P
NT = -(-N // P)
NP = NT * P
CH = 16
CJ = -(-E // (P * CH))
ET = CH * CJ
EP = ET * P
CL = CJ * P
ST = ET + NT - 1
BIG = 1.0e30
ROUND = 1.5 * 2.0 ** 23
NEG_SLOPE = 0.2
LN_EPS = 1e-5
U = 16
G = 8
HALF = (D + H) // 2
V = 4
SG = ST // G
SETUP_DMAS, WEIGHT_DMAS, EXPERT_DMAS = 9, 7, 6
assert NT % 4 == 1 and ST % U == 0 and SG % 2 == 0 and U % (2 * V) == 0 and NT % 2 == 1

SEMAPHORES = (
    "dst_scan_in", "dst_stepped", "el_idx", "el_in0", "el_in1", "el_kept", "el_stored",
    "ends_stepped", "ends_tp", "er_carried", "er_got", "er_hot", "er_hot_t", "er_kept", "er_mm",
    "er_split", "er_summed", "er_tp", "ex_exp", "ex_g", "ex_gelu", "ex_hhi", "ex_hmm", "ex_hs",
    "ex_ht", "ex_htp", "ex_lg", "ex_nmax", "ex_out", "ex_st0", "ex_st1", "ex_st2", "ex_st3",
    "ex_tp", "ex_xhi", "ex_xn", "ex_xt", "ex_ymm", "experts_in", "fin_st0", "fin_st1",
    "fold_mm", "fold_out", "fold_v", "g_in", "g_mm", "g_out", "ident_ready", "jn_a0", "jn_a1",
    "jn_ag", "jn_b0", "jn_b1", "jn_b2", "jn_b3", "jn_bn", "jn_eps", "jn_inv", "jn_n", "jn_x",
    "mx_mm", "mx_n1", "mx_n2", "mx_norm", "mx_out", "mx_qn", "mx_st0", "mx_st1", "mx_st2",
    "mx_st3", "mx_x0", "mx_x1", "mx_x2", "mx_x3", "p_ready", "p_row", "p_set", "pen_ready",
    "pj_kexp", "pj_kf", "pj_kmin", "pj_kv", "pj_kva", "pj_mv", "pj_mvs", "pj_q", "pj_qf",
    "pj_st0", "pj_st1", "pj_tp", "pj_v", "pj_vout", "pj_x0", "pj_x1", "pj_xhi", "pj_xn",
    "pj_xt", "pw_hi", "pw_lo", "r_zeroed", "row_back", "row_in", "row_v", "sc_mm", "sc_out",
    "sc_tp", "sc_xn", "sc_xt", "scan_done", "scan_ends", "scan_v", "setup_in", "sm", "sm_diff",
    "st_agg", "st_eps", "st_inv", "st_seen", "st_x0", "st_x1", "st_x2", "st_x3", "step_idx",
    "step_mm", "step_pv", "tab_begun", "tab_d", "tab_k", "tab_mm", "tile_out", "tile_sum",
    "tp_el", "tp_el_out", "tp_m", "tp_m_out", "v_set", "w_hi", "w_lo", "weights_in", "wo_in")


def turns(eng, body, n=NT, u=2, peeled=1):
    for t in range(u * peeled):
        body(t, t % u, t // u)
    with eng.Fori(peeled, n // u) as i:
        for j in range(u):
            body(i * u + j, j, i)
    for t in range(n // u * u, n):
        body(t, t % u, t // u)


def wait_past(eng, sem, t, lag):
    if not isinstance(t, int) or t >= lag:
        eng.wait_ge(sem, t + (1 - lag))


def not_last(t):
    return not (isinstance(t, int) and t == NT - 1)


def later(t, lag):
    return not isinstance(t, int) or t >= lag


def gps_layer(nc, x, src_cols, dst_cols, dst_rows, w_src, b_src, w_dst, b_dst, w_val, b_val, attn_l,
              attn_r, w_qk_t, w_v, r_mat, w_out, b_out, w_r, w_1, w_2, out):
    el_table = nc.dram_tensor("el_table", (NP, H), F32, kind="Internal").ap()
    v_table = nc.dram_tensor("v_table", (NP, D), F32, kind="Internal").ap()
    x_mix = nc.dram_tensor("x_mix", (NP, D), F32, kind="Internal").ap()
    agg = nc.dram_tensor("agg", (NP, D + H), F32, kind="Internal").ap()
    x_mid = nc.dram_tensor("x_mid", (NP, D), F32, kind="Internal").ap()

    def rows(dram, t):
        return dram[bass.ds(t * P, P), :]

    with ExitStack() as ctx:
        def sb(name, shape, dt=F32):
            return ctx.enter_context(nc.sbuf_tensor(name, shape, dt))

        def sem(name):
            return ctx.enter_context(nc.semaphore(name))

        ident = sb("ident", [P, P])
        ident_b = sb("ident_b", [P, P], BF16)
        col_no = sb("col_no", [P, P])
        ones = sb("ones", [P, P])
        zeros = sb("zeros", [1, D], BF16)
        ends_of = sb("ends_of", [P, 2, ET], I32)
        ends_step = sb("ends_step", [P, 2, ST], I32)
        dst_local = sb("dst_local", [P, ST])
        el_er = sb("el_er", [P, NT, 2 * H])
        er_parts = sb("er_parts", [P, NT, 3, H], BF16)
        er_rest = sb("er_rest", [P, NT, H])
        k_tab = sb("k_tab", [1, ST], U16)
        d_tab = sb("d_tab", [1, ST], U16)
        keep_tab = sb("keep_tab", [1, ST], U16)
        turn_tab = sb("turn_tab", [1, ST], U16)
        real_row = sb("real_row", [P, NT])
        mean_rstd = sb("mean_rstd", [P, NT * 2])
        small = sb("small", [P, 2])
        bo_all = sb("bo_all", [P, D])

        ARENA = 41480
        with nc.sbuf_tensor("arena", [P, ARENA], F32) as arena:
            pass
        hi_at, ph_a = (-(-at_ // 8) * 8 for at_ in (2 * CL + 2, 3 * CL + 4 + ET * H))
        with ExitStack() as early:
            def sb_early(name, shape, dt=F32R):
                return early.enter_context(nc.sbuf_tensor(name, shape, dt))
            sb_early("low_room", [P, hi_at])
            wv_hi, wmv_hi, wqk_hi = (sb_early(f"{n}_hi", [P, KC, D]) for n in ("wv", "wmv", "wqk"))
            sb_early("edges_room", [P, ph_a - hi_at - 3 * KC * D])
            wv_lo, wmv_lo, wqk_lo = (sb_early(f"{n}_lo", [P, KC, D]) for n in ("wv", "wmv", "wqk"))
            xp_hi, xp_lo = (sb_early(f"xp_{n}", [P, 2, D]) for n in ("hi", "lo"))
        w1_hi = [sb(f"w1_hi{c}", [P, X * XF], F32R) for c in range(KC)]
        w2_hi = [sb(f"w2_hi{c}", [P, KC, D], F32R) for c in range(4)]
        wr_at = 2 * KC * X * XF
        sb("wr_room", [P, KC * X])
        wr_r = sb("wr_r", [P, KC, 2 * X], F32R)
        xt_hi = sb("xt_hi", [P, 2, D], F32R)
        xt_lo = sb("xt_lo", [P, 2, D], F32R)
        ht_hi = sb("ht_hi", [P, 2, D], F32R)
        ht_lo = sb("ht_lo", [P, 2, D], F32R)
        rows_at = wr_at + 3 * KC * X + 8 * D
        w1_at, w2_at = ARENA - 2 * KC * X * XF, ARENA - KC * X * XF
        sb("rows_room", [P, w1_at - rows_at])
        w1_lo = [sb(f"w1_lo{c}", [P, X * XF], F32R) for c in range(KC)]
        w2_lo = [sb(f"w2_lo{c}", [P, KC, D], F32R) for c in range(4)]

        def at(off, *shape, dt=None):
            n = int(np.prod(shape))
            assert off + n <= ARENA, (off, shape)
            v = arena[:, off:off + n]
            if dt is not None:
                v = v.bitcast(dt)
            if len(shape) == 2:
                v = v.rearrange("p (a b) -> p a b", a=shape[0])
            elif len(shape) == 3:
                v = v.rearrange("p (a b c) -> p a b c", a=shape[0], b=shape[1])
            return v

        t_el = at(0, CL)
        t_pen = at(CL, CL + 1)
        t_run = at(2 * CL + 2, CL)
        q_feat = at(0, 2, NP)
        e_el = at(3 * CL + 4, ET, H)
        o = ph_a
        wv = at(o, KC, D); o += KC * D
        wmv = at(o, KC, D); o += KC * D
        wqk = at(o, KC, D); o += KC * D
        o += 4 * D
        wo = at(ph_a + KC * D, KC, D)
        e_er = at(ph_a, ET, H)
        bv_all = at(o, D); o += D
        wlr = at(o, KC, 2 * H); o += KC * 2 * H
        blr = at(o, 2 * H); o += 2 * H
        at_acc = at(o, KC * HF + 2)
        kvt_acc = at(o, KC, HF); o += KC * HF
        ks_acc = at(o, 2); o += 2
        r_diag = at(o, HF); o += HF
        g_mat = at(o, 2, D); o += 2 * D
        kvt_diag = at(o, KC, P); o += KC * P
        ks_diag = at(o, 2, P); o += 2 * P
        xs_at = o
        xs = at(o, 2, D); o += 2 * D
        xn = at(o, D); o += D
        xt = at(o, 2, D); o += 2 * D
        vs = at(o, 2, D); o += 2 * D
        mv = at(o, D); o += D
        ex = at(o, 2, 2 * P); o += 4 * P
        feat = xt[:, 0, :]
        assert o <= ARENA, o
        o = 0
        s_w = at(o, KC, D); o += KC * D
        s_w2 = at(o, KC, D); o += KC * D
        s_al = at(o, D); o += D
        s_ar = at(o, D); o += D
        s_bs = at(o, D); o += D
        s_bd = at(o, D); o += D
        s_tmp = at(o, KC, D); o += KC * D
        s_wqt = at(o, 8, D); o += 8 * D
        s_cnt = at(o, ST); o += ST
        s_d = at(o, ST); o += ST
        s_io = at(o, ST); o += ST
        s_last = at(o, ET); o += ET
        x4 = at(o, 4, D); o += 4 * D
        assert o <= 3 * CL + 4
        d128 = sb("d128", [P, ST])

        xn2 = [xn, mv]
        xm = at(ph_a, 4, D)
        norm = [ex[:, 0, :], mv[:, 0:2 * P]]
        qn = [feat[:, 0:2 * P].rearrange("p (c t) -> p c t", c=2), ex[:, 1, :].rearrange("p (c t) -> p c t", c=2)]
        o = 0
        vg = at(o, U, D); o += U * D
        pv = at(o, V, D + H); o += V * (D + H)
        hot = at(o, 2, V, P); o += 2 * V * P
        fin = at(o, 2, D + H); o += 2 * (D + H)
        assert o <= 2 * CL
        wr = at(wr_at, KC, X)
        w1 = at(w1_at, KC, X * XF)
        w2 = at(w2_at, 2 * X, D)
        o = rows_at
        da = at(o, 2, D + H); o += 2 * (D + H)
        dx = at(o, 4, D); o += 4 * D
        hs = at(o, 2, D); o += 2 * D
        assert o <= w1_at
        idx = sb("idx", [P, U], I32)
        idx_el = sb("idx_el", [P, 2, CH], I32)
        got_el = sb("got_el", [P, 2, CH, H])
        thr = sb("thr", [P, 1])
        ag2 = sb("ag2", [P, 2, 2])
        inv = sb("inv", [P, 1])
        power = sb("power", [P, 1])
        bn = sb("bn", [P, 6])
        ag = sb("ag", [P, 2])
        den = sb("den", [P, H])
        row = at(ph_a + (ET + NT) * H, 12, P)
        o = ph_a + (ET + NT) * H + 12 * P
        hot_b = at(o, G * P, dt=BF16).rearrange("p (s g n) -> p s g n", s=2, g=G); o += G * P
        hot_t = at(o, G * P, dt=BF16).rearrange("p (s n) -> p s n", s=2); o += G * P
        same = at(0, SG, H * (1 + G)).rearrange("p g (h i) -> p g h i", h=H)
        er_got = at(o, 2, H, 1 + G); o += 2 * H * (1 + G)
        er_run = at(o, 2, H, 1 + G); o += 2 * H * (1 + G)
        assert o <= xs_at
        edge_first = sb("edge_first", [P, 4])
        col = sb("col", [P, 2])
        lg = sb("lg", [P, 8])
        top = sb("top", [P, 8])
        nmax = sb("nmax", [P, 1])
        pr = sb("pr", [P, 8])
        psum_ = sb("psum_", [P, 1])
        ptop = sb("ptop", [P, 8])
        pidx = sb("pidx", [P, 8], U32)
        pidf = sb("pidf", [P, 8])
        ga = sb("ga", [P, 8])
        gb = sb("gb", [P, 8])
        gate = sb("gate", [P, 2, 8])
        e_m = at(2 * CL + 2, ET, H)
        dst_scan = at(2 * CL + 2, CL, dt=I32)
        el_er_flat = el_er[:].rearrange("p t a -> p (t a)")
        er_flat = er_parts[:].rearrange("p t i h -> p (t i h)")
        e_er_flat = at(ph_a, (ET + NT) * H)
        e_el_flat = e_el.rearrange("p k h -> p (k h)")

        bank = [ctx.enter_context(nc.psum_tensor(f"bank{i}", [P, D], F32)) for i in range(7)]
        bank_b = ctx.enter_context(nc.psum_tensor("bank_b", [P, 2 * D], BF16))
        turned_hot = [bank_b, bank[6][:].bitcast(BF16)]
        sems = {}

        def s(name):
            if name not in sems:
                sems[name] = sem(name)
            return sems[name]

        gathered = [sem(f"rows_gathered{j}") for j in range(U)]
        for name in SEMAPHORES:
            s(name)
        block = ctx.enter_context(nc.Block())

        def apart(eng, sem_, value):
            if not isinstance(value, int):
                value = eng.to_reg(value)
                eng.wait_ge(s("p_set"), 1)
            eng.wait_ge(sem_, value)

        def by_chunk(w):
            return w.rearrange("(c p) n -> p c n", p=P)

        def bcast(row_ap):
            return row_ap.broadcast_to([P, row_ap.shape[-1]])

        def by_part(w, n):
            return w[:].unsqueeze(1) if n == 1 else w[:]

        def looked_up(engine, table, t, n, top):
            return nc.values_load_multi_w_load_instructions(
                table[0:1, bass.ds(t, n)], engines=(engine,), min_val=0, max_val=top,
                skip_runtime_bounds_check_because="the tables count edge tiles and node tiles, whatever dst holds")[1]

        @block.sync
        def _(sp):
            for dst, src in ((ends_of[:, 0, :], src_cols), (ends_of[:, 1, :], dst_cols), (s_w, by_chunk(w_src)),
                             (s_w2, by_chunk(w_dst)), (s_al, bcast(attn_l)), (s_ar, bcast(attn_r)),
                             (s_bs, bcast(b_src)), (s_bd, bcast(b_dst)),
                             (s_last[0:NT - 1, :].bitcast(I32), dst_cols[P - 1:P, :].broadcast_to([NT - 1, ET]))):
                sp.dma_start(dst, src).then_inc(s("setup_in"), 16)

            def scores(t, j, r):
                wait_past(sp, s("sc_xn"), t, 4)
                sp.dma_start(x4[:, j, :], rows(x, t)).then_inc(s(f"st_x{j}"), 16)
            turns(sp, scores, NT, 4)
            sp.wait_ge(s("sc_out"), NT)
            sp.dma_start(el_table.rearrange("(t p) h -> p t h", p=P), el_er[:, :, 0:H]).then_inc(s("el_stored"), 16)

            def proj(t, slot, r):
                wait_past(sp, s("pj_xn"), t, 2)
                sp.dma_start(xs[:, slot, :], rows(x, t)).then_inc(s(f"pj_x{slot}"), 16)
                if later(t, 1):
                    sp.wait_ge(s("pj_vout"), t)
                    sp.dma_start(rows(v_table, t - 1), vs[:, 1 - slot, :]).then_inc(s(f"pj_st{1 - slot}"), 16)
            turns(sp, proj)
            sp.wait_ge(s("pj_vout"), NT)
            sp.dma_start(rows(v_table, NT - 1), vs[:, (NT - 1) % 2, :]).then_inc(s("pj_st0"), 16)

            sp.wait_ge(s("pj_q"), NT)
            sp.dma_start(wo, by_chunk(w_out)).then_inc(s("wo_in"), 16)

            def mix_store(t, j):
                sp.wait_ge(s("mx_out"), t + 1)
                sp.dma_start(rows(x_mix, t), xm[:, j, :]).then_inc(s(f"mx_st{j}"), 16)

            def mix(t, j, r):
                if later(t, 4):
                    sp.wait_ge(s(f"mx_st{j}"), r * 16)
                sp.dma_start(xm[:, j, :], rows(x, t)).then_inc(s(f"mx_x{j}"), 16)
                if later(t, 3):
                    mix_store(t - 3, (j + 1) % 4)
            turns(sp, mix, NT, 4)
            for t in range(NT - 3, NT):
                mix_store(t, t % 4)

            for c in range(CH):
                sp.dma_start(dst_scan[c * H:(c + 1) * H, :], dst_rows[c:c + 1, :].broadcast_to([H, CL]))\
                  .then_inc(s("dst_scan_in"), 16)

            for j in range(4):
                sp.wait_ge(s(f"mx_st{j}"), 16 * ((NT - 1 - j) // 4 + 1))
            sp.wait_ge(s("p_ready"), 1)
            w1_by = w1.rearrange("p c (e f) -> p c e f", e=X)
            for c in range(KC):
                sp.dma_start(w1_by[:, c], w_1[:, c * P:(c + 1) * P, :].rearrange("e p f -> p e f")).then_inc(s("experts_in"), 16)
            sp.dma_start(w2, w_2.rearrange("e (c p) n -> p (e c) n", p=P)).then_inc(s("experts_in"), 16)
            sp.dma_start(wr, by_chunk(w_r)).then_inc(s("experts_in"), 16)
            sp.wait_ge(s("fin_st0"), 16 * (NT // 2 + 1))
            sp.wait_ge(s("fin_st1"), 16 * (NT // 2))
            sp.wait_ge(s("step_mm"), ST)

            def store(t, j, r):
                sp.wait_ge(s("ex_out"), t + 1)
                sp.dma_start(rows(out, t), dx[:, j, :]).then_inc(s(f"ex_st{j}"), 16)

            def moe(t, j, r):
                wait_past(sp, s("ex_tp"), t, 2)
                sp.dma_start(da[:, j % 2, :], rows(agg, t)).then_inc(s(f"jn_a{j % 2}"), 16)
                if later(t, 4):
                    sp.wait_ge(s(f"ex_st{j}"), r * 16)
                sp.dma_start(dx[:, j, :], rows(x_mix, t)).then_inc(s(f"jn_b{j}"), 16)
                if later(t, 3):
                    store(t - 3, (j + 1) % 4, r)
            turns(sp, moe, NT, 4)
            for t in range(NT - 3, NT):
                store(t, t % 4, t // 4)
            for j in range(4):
                sp.wait_ge(s(f"ex_st{j}"), 16 * ((NT - 1 - j) // 4 + 1))

        @block.gpsimd
        def _(pool):
            kw = dict(allow_small_or_imprecise_dtypes=True)
            pool.memset(ident[:], 0.0).then_inc(s("p_set"), 1)
            pool.memset(ones[:], 1.0).then_inc(s("p_set"), 1)
            pool.memset(zeros[:], 0.0).then_inc(s("p_set"), 1)
            pool.wait_ge(s("p_set"), 1)
            pool.affine_select(out=ident[:], in_=ident[:], compare_op=ALU.not_equal, fill=1.0, base=0,
                               pattern=[[-1, P]], channel_multiplier=1).then_inc(s("p_set"), 1)
            pool.iota(col_no[:], [[1, P]], base=0, channel_multiplier=0, **kw).then_inc(s("p_set"), 1)
            pool.iota(thr[:], [[0, 1]], base=P, channel_multiplier=P, **kw).then_inc(s("p_set"), 1)
            pool.iota(s_io, [[1, ST]], base=0, channel_multiplier=0, **kw).then_inc(s("p_set"), 1)
            pool.iota(real_row[:], [[P, NT]], base=0, channel_multiplier=1, **kw).then_inc(s("p_row"), 1)
            pool.wait_ge(s("p_row"), 1)
            pool.tensor_scalar(real_row[:], real_row[:], float(N), None, ALU.is_lt).then_inc(s("p_set"), 1)
            pool.memset(r_diag, 0.0).then_inc(s("r_zeroed"), 1)
            pool.memset(kvt_diag, 0.0).then_inc(s("p_set"), 1)
            pool.memset(ks_diag, 0.0).then_inc(s("p_set"), 1)
            pool.memset(at_acc, 0.0).then_inc(s("p_set"), 1)
            pool.memset(power[:], -0.5).then_inc(s("p_row"), 1)
            pool.wait_ge(s("p_row"), 2)

            def deviation(t, slot, r):
                apart(pool, s("st_agg"), t + 1)
                pool.tensor_scalar(ag2[:, slot, 1:2], ag2[:, slot, 1:2], LN_EPS, None, ALU.add).then_inc(s("st_eps"), 1)
                pool.wait_ge(s("st_eps"), t + 1)
                pool.tensor_tensor(ag2[:, slot, 1:2], ag2[:, slot, 1:2], power[:], ALU.pow).then_inc(s("st_inv"), 1)
            turns(pool, deviation)
            pool.wait_ge(s("setup_in"), SETUP_DMAS * 16)
            pool.wait_ge(s("el_stored"), 16)

            def keep(t, slot, r):
                pool.wait_ge(s(f"el_in{slot}"), (r + 1) * (16 * CH))
                pool.tensor_copy(e_el_flat[:, bass.ds(t * P, P)], got_el[:, slot].rearrange("p c h -> p (c h)"))\
                    .then_inc(s("el_kept"), 1)

            def gather(t, slot, r):
                wait_past(pool, s("el_kept"), t, 2)
                pool.tensor_copy(idx_el[:, slot, :], ends_of[:, 0, bass.ds(t * CH, CH)])\
                    .then_inc(s("el_idx"), 1)
                apart(pool, s("el_idx"), t + 1)
                for c in range(CH):
                    pool.indirect_dma_start(got_el[:, slot, c, :], None, el_table,
                                            bass.IndirectOffsetOnAxis(ap=idx_el[:, slot, c:c + 1], axis=0))\
                        .then_inc(s(f"el_in{slot}"), 16)
                if later(t, 1):
                    keep(t - 1, 1 - slot, (r - 1 if slot == 0 else r))
            turns(pool, gather, CJ)
            keep(CJ - 1, (CJ - 1) % 2, (CJ - 1) // 2)

            for name, n in (("pj_st0", NT // 2 + 1), ("pj_st1", NT // 2)):
                pool.wait_ge(s(name), 16 * n)
            pool.wait_ge(s("ends_stepped"), ST // U)
            pool.wait_ge(s("p_ready"), 1)

            def values(t, j, r):
                if j % 8 == 0:
                    wait_past(pool, s("step_pv"), t, 9)
                    pool.tensor_copy(idx[:, j:j + 8], ends_step[:, 0, bass.ds(t, 8)]).then_inc(s("step_idx"), 1)
                    apart(pool, s("step_idx"), r * (U // 8) + (j // 8 + 1))
                if later(t, U):
                    apart(pool, s("step_pv"), t + (1 - U))
                pool.indirect_dma_start(vg[:, j, :], None, v_table,
                                        bass.IndirectOffsetOnAxis(ap=idx[:, j:j + 1], axis=0))\
                    .then_inc(gathered[j], 16)
            turns(pool, values, ST, U)

            def inverse(t, slot, r):
                apart(pool, s("jn_ag"), t + 1)
                wait_past(pool, s("ex_xn"), t, 1)
                pool.tensor_scalar(inv[:], ag[:, 1:2], LN_EPS, None, ALU.add).then_inc(s("jn_eps"), 1)
                pool.wait_ge(s("jn_eps"), t + 1)
                pool.tensor_tensor(inv[:], inv[:], power[:], ALU.pow).then_inc(s("jn_inv"), 1)
            turns(pool, inverse)

        @block.scalar
        def _(act):
            act.wait_ge(s("r_zeroed"), 1)
            for dst, src in ((r_diag[0:HF, 0:HD], r_mat), (r_diag[HF:P, HD:2 * HD], r_mat),
                             (s_wqt, by_chunk(w_qk_t)), (wv, by_chunk(w_val)), (wmv, by_chunk(w_v)),
                             (bv_all, bcast(b_val)), (bo_all[:], bcast(b_out))):
                act.dma_start(dst, src).then_inc(s("weights_in"), 16)
            act.wait_ge(s("fold_mm"), KC)
            for c in range(KC):
                act.activation(wqk[:, c, :], bank[c][:], ACT.Copy).then_inc(s("fold_out"), 1)

            def scores(t, slot, r):
                act.wait_ge(s("sc_tp"), t + 1)
                wait_past(act, s("sc_mm"), t, 2)
                act.activation(xt[:, slot, :], bank[slot][:], ACT.Copy).then_inc(s("sc_xt"), 1)
            turns(act, scores)
            act.wait_ge(s("sc_mm"), NT)

            act.wait_ge(s("sc_xn"), NT)
            for hi, w in ((wv_hi, wv), (wmv_hi, wmv), (wqk_hi, wqk)):
                act.activation(hi[:], w, ACT.Copy).then_inc(s("pw_hi"), 1)

            def proj_hi(t, slot):
                act.wait_ge(s("pj_tp"), t + 1)
                wait_past(act, s("pj_q"), t, 2)
                act.activation(xp_hi[:, slot, :], bank[slot][:], ACT.Copy).then_inc(s("pj_xhi"), 1)

            def features(t):
                act.wait_ge(s("pj_kmin"), t + 1)
                act.activation(ex[:], ex[:], ACT.Exp).then_inc(s("pj_kexp"), 1)

            def keep_q(t):
                act.wait_ge(s("pj_kv"), t + 1)
                act.activation(q_feat[:, :, bass.ds(t * P, P)], bank[5][:, 0:2 * P].rearrange("p (c t) -> p c t", c=2),
                               ACT.Copy).then_inc(s("pj_qf"), 1)

            def proj(t, slot, r):
                if later(t, 1):
                    features(t - 1)
                    keep_q(t - 1)
                act.wait_ge(s("pj_mv"), t + 1)
                act.activation(mv, bank[3][:], ACT.Copy).then_inc(s("pj_mvs"), 1)
                if not_last(t):
                    proj_hi(t + 1, 1 - slot)
                edge_ends(t)

            def edge_ends(t):
                for i, k in enumerate(looked_up(ENGINE.Activation, k_tab, t * U, U, ET - 1)):
                    last = act.activation(ends_step[:, :, bass.ds(t * U + i, 1)], ends_of[:, :, bass.ds(k, 1)], ACT.Copy)
                last.then_inc(s("ends_stepped"), 1)
            act.wait_ge(s("tab_d"), 4)
            act.wait_ge(s("setup_in"), SETUP_DMAS * 16)
            proj_hi(0, 0)
            turns(act, proj)
            for t in range(NT, ST // U):
                edge_ends(t)
            features(NT - 1)
            keep_q(NT - 1)
            act.wait_ge(s("g_mm"), 1)
            for c in range(2):
                act.activation(g_mat[:, c, :], bank[c][:], ACT.Copy).then_inc(s("g_out"), 1)

            def mix(t, slot, r):
                act.wait_ge(s("mx_norm"), t + 1)
                wait_past(act, s("mx_qn"), t, 2)
                act.activation(norm[slot], bank[slot][:, 0:2 * P], ACT.Copy, bias=1e-6).then_inc(s("mx_n1"), 1)
            turns(act, mix)

            def keep_hot(g, slot):
                act.wait_ge(s("er_tp"), g + 1)
                wait_past(act, s("er_mm"), g, 2)
                act.activation(hot_t[:, slot, :], turned_hot[slot][:, 0:G * P], ACT.Copy).then_inc(s("er_hot_t"), 1)

            def keep_er(g, slot, places):
                act.wait_ge(s("er_summed"), g + 1)
                for i, k in enumerate(places):
                    last = act.activation(e_er_flat[:, bass.ds(k * H, H)], er_run[:, slot, :, 1 + i], ACT.Copy)
                last.then_inc(s("er_kept"), 1)

            def places_of(g):
                return looked_up(ENGINE.Activation, keep_tab, g * G, G, ET + NT - 1)

            def expand(g, slot, r):
                if later(g, 1):
                    keep_hot(g - 1, 1 - slot)
                if later(g, 3):
                    keep_er(g - 3, 1 - slot, places_of(g - 3))
            for j in range(4):
                act.wait_ge(s(f"mx_st{j}"), 16 * ((NT - 1 - j) // 4 + 1))
            turns(act, expand, SG, peeled=2)
            keep_hot(SG - 1, 1)
            for g in range(SG - 3, SG):
                keep_er(g, g % 2, places_of(g))

            for g in range(-(-CJ // 4)):
                n = min(4, CJ - 4 * g)
                act.wait_ge(s("tp_el"), g + 1)
                act.activation(t_el[:, g * D:g * D + n * P], bank[g % 4][:, 0:n * P], ACT.Copy).then_inc(s("tp_el_out"), 1)
            act.wait_ge(s("scan_v"), 1)
            act.activation(t_pen[:, 1:CL], t_pen[:, 1:CL], ACT.Copy, scale=-BIG).then_inc(s("pen_ready"), 1)
            m_flat = e_m.rearrange("p k h -> p (k h)")
            for g in range(-(-CJ // 4)):
                n = min(4, CJ - 4 * g)
                act.wait_ge(s("tp_m"), g + 1)
                act.activation(m_flat[:, 4 * g * P:(4 * g + n) * P], bank[g % 4][:, 0:n * P], ACT.Copy).then_inc(s("tp_m_out"), 1)
            act.wait_ge(s("sm_diff"), 1)
            act.activation(e_el, e_el, ACT.Exp).then_inc(s("p_ready"), 1)

            def finish(t, slot, r):
                act.wait_ge(s("tile_sum"), t + 1)
                if later(t, 2):
                    act.wait_ge(s(f"fin_st{slot}"), r * 16)
                for i in range(2):
                    last = act.activation(fin[:, slot, i * HALF:(i + 1) * HALF], bank[i][:, 0:HALF], ACT.Copy)
                last.then_inc(s("tile_out"), 1)
                act.wait_ge(s("tile_out"), t + 1)
                act.dma_start(rows(agg, t), fin[:, slot, :]).then_inc(s(f"fin_st{slot}"), 16)
            turns(act, finish)

            act.wait_ge(s("step_mm"), ST)
            act.wait_ge(s("fin_st0"), 16 * (NT // 2 + 1))
            act.wait_ge(s("fin_st1"), 16 * (NT // 2))
            act.wait_ge(s("experts_in"), EXPERT_DMAS * 16)
            act.activation(wr_r[:, :, 0:X], wr, ACT.Copy).then_inc(s("w_hi"), 1)
            for hi, w in ((w1_hi, w1), (w2_hi, w2)):
                for c in range(4):
                    n = w.shape[1] // 4
                    act.activation(by_part(hi[c], n), w[:, c * n:(c + 1) * n], ACT.Copy).then_inc(s("w_hi"), 1)

            def x_hi(t, slot):
                act.wait_ge(s("ex_tp"), t + 1)
                if later(t, 2):
                    act.wait_ge(s("ex_hmm"), 4 * t - 4)
                act.activation(xt_hi[:, slot, :], bank[slot][:], ACT.Copy).then_inc(s("ex_xhi"), 1)

            def exps(t):
                act.wait_ge(s("ex_nmax"), t + 1)
                act.activation(pr[:], lg[:], ACT.Exp, bias=nmax[:], accum_out=psum_[:]).then_inc(s("ex_exp"), 1)

            def gelu(n, q):
                act.wait_ge(s("ex_hmm"), n + 1)
                wait_past(act, s("ex_htp"), n, 2)
                act.activation(hs[:, q % 2, :], bank[2 + q % 2][:], ACT.Gelu).then_inc(s("ex_gelu"), 1)

            def h_hi(n, q):
                act.wait_ge(s("ex_htp"), n + 1)
                wait_past(act, s("ex_ymm"), n, 2)
                act.activation(ht_hi[:, q % 2, :], bank[4][:], ACT.Copy).then_inc(s("ex_hhi"), 1)
            x_hi(0, 0)
            exps(0)
            gelu(0, 0)
            gelu(1, 1)

            def moe(t, j, r):
                more = not_last(t)
                for q in range(4):
                    h_hi(t * 4 + q, q)
                    if q == 1 and more:
                        x_hi(t + 1, (j + 1) % 2)
                    if q < 2 or more:
                        gelu(t * 4 + (q + 2), q)
                    if q == 2 and more:
                        exps(t + 1)
            turns(act, moe, NT, 4)

        @block.vector
        def _(dve):
            dve.wait_ge(s("p_set"), 11)
            dve.tensor_copy(ident_b[:], ident[:]).then_inc(s("ident_ready"), 1)
            dve.wait_ge(s("setup_in"), SETUP_DMAS * 16)
            R_ = NT - 1
            dve.tensor_copy(s_last[0:R_, :], s_last[0:R_, :].bitcast(I32)).then_inc(s("v_set"), 1)
            dve.wait_ge(s("v_set"), 1)
            dve.tensor_scalar(s_d[0:R_, 0:ET], s_last[0:R_, :], thr[0:R_, :], None, ALU.is_lt).then_inc(s("v_set"), 1)
            dve.wait_ge(s("v_set"), 2)
            dve.tensor_reduce(small[0:R_, 0:1], s_d[0:R_, 0:ET], AX.X, ALU.add).then_inc(s("v_set"), 1)
            dve.wait_ge(s("v_set"), 3)
            dve.scalar_tensor_tensor(small[0:R_, 1:2], thr[0:R_, :], 1.0 / P, small[0:R_, 0:1], ALU.mult, ALU.add)\
                .then_inc(s("v_set"), 1)
            dve.wait_ge(s("v_set"), 4)
            dve.tensor_scalar(s_cnt[0:R_, :], s_io[0:R_, :], small[0:R_, 1:2], None, ALU.is_ge).then_inc(s("tab_begun"), 1)
            n = 0
            for w, a, b, lo in ((s_w, s_al, s_bs, 0), (s_w2, s_ar, s_bd, H)):
                for c in range(KC):
                    dve.tensor_tensor(s_tmp[:, c, :], w[:, c, :], a, ALU.mult).then_inc(s("fold_v"), 1)
                n += KC
                dve.wait_ge(s("fold_v"), n)
                dve.tensor_reduce(wlr[:, :, lo:lo + H], s_tmp.rearrange("p c (h f) -> p c h f", f=HF), AX.X, ALU.add)\
                    .then_inc(s("fold_v"), 1)
                n += 1
                dve.wait_ge(s("fold_v"), n)
                dve.tensor_tensor(s_tmp[:, 0, :], b, a, ALU.mult).then_inc(s("fold_v"), 1)
                n += 1
                dve.wait_ge(s("fold_v"), n)
                dve.tensor_reduce(blr[:, lo:lo + H], s_tmp[:, 0, :].rearrange("p (h f) -> p h f", f=HF), AX.X, ALU.add)\
                    .then_inc(s("fold_v"), 1)
                n += 1
                dve.wait_ge(s("fold_v"), n)
            dve.wait_ge(s("tab_mm"), 1)
            dve.tensor_scalar(d128[:, 0:ST // 2], bank[4][:, 0:ST // 2], float(P), None, ALU.mult)
            dve.tensor_scalar(d128[:, ST // 2:], bank[5][:, 0:ST // 2], float(P), None, ALU.mult)
            dve.tensor_copy(s_d[0:1, 0:ST // 2], bank[4][0:1, 0:ST // 2])
            dve.tensor_copy(s_d[0:1, ST // 2:ST], bank[5][0:1, 0:ST // 2]).then_inc(s("tab_d"), 1)
            dve.wait_ge(s("tab_d"), 1)
            dve.tensor_copy(d_tab[:], s_d[0:1, 0:ST])
            dve.tensor_tensor(s_tmp[0:1, 0:2, :].rearrange("o a b -> o (a b)")[:, 0:ST], s_io[0:1, :], s_d[0:1, 0:ST],
                              ALU.subtract).then_inc(s("tab_k"), 1)
            k_row = s_tmp[0:1, 0:2, :].rearrange("o a b -> o (a b)")[:, 0:ST]
            c_row = s_tmp[0:1, 2:4, :].rearrange("o a b -> o (a b)")[:, 0:ST]
            dve.wait_ge(s("tab_k"), 1)
            dve.tensor_scalar(c_row, k_row, 1.0 / CJ, 0.5 / CJ - 0.5, ALU.mult, ALU.add).then_inc(s("tab_k"), 1)
            dve.wait_ge(s("tab_k"), 2)
            dve.tensor_scalar(c_row, c_row, ROUND, -ROUND, ALU.add, ALU.add).then_inc(s("tab_k"), 1)
            dve.tensor_scalar(k_row, k_row, float(CH), None, ALU.mult).then_inc(s("tab_k"), 1)
            dve.wait_ge(s("tab_k"), 4)
            dve.scalar_tensor_tensor(k_row, c_row, float(1 - CH * CJ), k_row, ALU.mult, ALU.add).then_inc(s("tab_k"), 1)
            dve.tensor_tensor(s_cnt[0:1, 0:ST - 1], s_d[0:1, 1:ST], s_d[0:1, 0:ST - 1], ALU.subtract)
            dve.memset(s_cnt[0:1, ST - 1:ST], 0.0).then_inc(s("tab_d"), 1)
            dve.wait_ge(s("tab_k"), 5)
            dve.wait_ge(s("tab_d"), 2)
            dve.tensor_copy(k_tab[:], k_row)
            dve.scalar_tensor_tensor(c_row, s_d[0:1, 0:ST], float(ET), k_row, ALU.add, ALU.subtract).then_inc(s("tab_k"), 1)
            dve.wait_ge(s("tab_k"), 6)
            dve.tensor_tensor(c_row, c_row, s_cnt[0:1, :], ALU.mult).then_inc(s("tab_k"), 1)
            dve.wait_ge(s("tab_k"), 7)
            dve.tensor_tensor(keep_tab[:], c_row, k_row, ALU.add)
            dve.memset(s_cnt[0:1, ST - 1:ST], 1.0).then_inc(s("tab_d"), 1)
            dve.wait_ge(s("tab_d"), 3)
            dve.scalar_tensor_tensor(turn_tab[:], s_d[0:1, 0:ST], 1.0, s_cnt[0:1, :], ALU.add, ALU.mult)\
                .then_inc(s("tab_d"), 1)

            def normed(out_, in_, t):
                return dve.tensor_scalar(out_, in_, mean_rstd[:, bass.ds(t * 2, 1)], mean_rstd[:, bass.ds(t * 2 + 1, 1)],
                                         ALU.subtract, ALU.mult)

            def score_in(t, j):
                slot = j % 2
                dve.wait_ge(s("st_inv"), t + 1)
                dve.tensor_copy(mean_rstd[:, bass.ds(t * 2, 2)], ag2[:, slot, :])
                wait_past(dve, s("sc_tp"), t, 2)
                dve.tensor_scalar(xn2[slot], x4[:, j, :], ag2[:, slot, 0:1], ag2[:, slot, 1:2], ALU.subtract, ALU.mult)\
                    .then_inc(s("sc_xn"), 1)

            def score_out(t, slot):
                dve.wait_ge(s("sc_mm"), t + 1)
                dve.tensor_tensor(el_er_flat[:, bass.ds(t * 2 * H, 2 * H)], bank[2 + slot][:, 0:2 * H], blr, ALU.add).then_inc(s("sc_out"), 1)

            def scores(t, j, r):
                dve.wait_ge(s(f"st_x{j}"), (r + 1) * 16)
                wait_past(dve, s("st_agg"), t, 1)
                wait_past(dve, s("sc_xn"), t, 2)
                dve.bn_stats(bn[:], x4[:, j, :]).then_inc(s("st_seen"), 1)
                apart(dve, s("st_seen"), t + 1)
                dve.bn_aggr(ag2[:, j % 2, :], bn[:]).then_inc(s("st_agg"), 1)
                if later(t, 1):
                    score_in(t - 1, (j - 1) % 4)
                if later(t, 3):
                    score_out(t - 3, (j - 1) % 2)
            turns(dve, scores, NT, 4)
            score_in(NT - 1, (NT - 1) % 4)
            for t in range(NT - 3, NT):
                score_out(t, t % 2)
            dve.wait_ge(s("weights_in"), WEIGHT_DMAS * 16)

            def kv_add(t):
                dve.wait_ge(s("pj_kv"), t + 1)
                wait_past(dve, s("pj_kva"), t, 1)
                dve.tensor_tensor(at_acc, at_acc, bank[6][:, 0:KC * HF + 2], ALU.add).then_inc(s("pj_kva"), 1)

            def proj_lo(t, slot):
                dve.wait_ge(s("pj_xhi"), t + 1)
                dve.tensor_tensor(xp_lo[:, slot, :], bank[slot][:], xp_hi[:, slot, :].bitcast(F32), ALU.subtract)\
                    .then_inc(s("pj_xt"), 1)

            def below(t):
                dve.wait_ge(s("pj_q"), t + 1)
                wait_past(dve, s("pj_kf"), t, 1)
                dve.tensor_scalar_min(ex_flat, bank[4][:], 0.0).then_inc(s("pj_kmin"), 1)

            def features(t):
                dve.wait_ge(s("pj_kexp"), t + 1)
                wait_past(dve, s("pj_kv"), t, 1)
                dve.scalar_tensor_tensor(feat, bank[4][:], 0.0, ex_flat, ALU.max, ALU.add).then_inc(s("pj_kf"), 1)

            def proj(t, slot, r):
                if later(t, 1):
                    below(t - 1)
                if not_last(t):
                    dve.wait_ge(s(f"pj_x{1 - slot}"), (r + (1 if slot == 0 else 2)) * 16)
                    dve.wait_ge(s("pj_tp"), t + 1)
                    normed(xn, xs[:, 1 - slot, :], t + 1).then_inc(s("pj_xn"), 1)
                if later(t, 1):
                    features(t - 1)
                dve.wait_ge(s("pj_v"), t + 1)
                if later(t, 2):
                    dve.wait_ge(s(f"pj_st{slot}"), r * 16)
                dve.tensor_tensor(vs[:, slot, :], bank[2][:], bv_all, ALU.add).then_inc(s("pj_vout"), 1)
                if later(t, 1):
                    kv_add(t - 1)
                if not_last(t):
                    proj_lo(t + 1, 1 - slot)
            ex_flat = ex.rearrange("p a b -> p (a b)")
            def pw_lo(i, lo, w, hi):
                dve.wait_ge(s("pw_hi"), i + 1)
                dve.tensor_tensor(lo[:], w, hi[:].bitcast(F32), ALU.subtract).then_inc(s("pw_lo"), 1)
            pw_lo(0, wv_lo, wv, wv_hi)
            dve.wait_ge(s("pj_x0"), 16)
            normed(xn, xs[:, 0, :], 0).then_inc(s("pj_xn"), 1)
            pw_lo(1, wmv_lo, wmv, wmv_hi)
            proj_lo(0, 0)
            pw_lo(2, wqk_lo, wqk, wqk_hi)
            dve.wait_ge(s("sc_out"), NT)
            for i in range(3):
                rest = el_er[:, :, H:2 * H] if i == 0 else er_rest[:]
                dve.tensor_copy(er_parts[:, :, i, :], rest).then_inc(s("er_split"), 1)
                dve.wait_ge(s("er_split"), 2 * i + 1)
                if i < 2:
                    dve.tensor_tensor(er_rest[:], rest, er_parts[:, :, i, :], ALU.subtract).then_inc(s("er_split"), 1)
                    dve.wait_ge(s("er_split"), 2 * i + 2)

            turns(dve, proj)
            below(NT - 1)
            features(NT - 1)
            kv_add(NT - 1)
            dve.wait_ge(s("pj_kva"), NT)
            for j in range(KC):
                for i in range(2):
                    b = (2 * j + i) % 4
                    dve.tensor_copy(kvt_diag[i * HF:(i + 1) * HF, j, b * HD:(b + 1) * HD],
                                    kvt_acc[i * HF:(i + 1) * HF, j, i * HD:(i + 1) * HD])
            for c in range(2):
                for b in range(4):
                    r_ = slice(b * HD, (b + 1) * HD)
                    last = dve.tensor_scalar(ks_diag[r_, c, r_], ones[r_, r_], ks_acc[r_, c:c + 1], None, ALU.mult)
            last.then_inc(s("g_in"), 1)

            def mix(t, j, r):
                slot = j % 2
                dve.wait_ge(s("mx_n1"), t + 1)
                dve.reciprocal(norm[slot], norm[slot]).then_inc(s("mx_n2"), 1)
                dve.wait_ge(s("mx_n2"), t + 1)
                wait_past(dve, s("mx_mm"), t, 2)
                dve.tensor_tensor(qn[slot], q_feat[:, :, bass.ds(t * P, P)],
                                  norm[slot].rearrange("p (c t) -> p c t", c=2), ALU.mult).then_inc(s("mx_qn"), 1)
                if later(t, 1):
                    mix_out(t - 1, (j - 1) % 4, (r if j else r - 1))

            def mix_out(t, j, r):
                dve.wait_ge(s(f"mx_x{j}"), (r + 1) * 16)
                dve.wait_ge(s("mx_mm"), t + 1)
                dve.tensor_tensor(xm[:, j, :], xm[:, j, :], bank[2 + j % 2][:], ALU.add).then_inc(s("mx_out"), 1)
            turns(dve, mix, NT, 4)
            mix_out(NT - 1, 0, (NT - 1) // 4)

            by_group = d128[:].rearrange("p (g i) -> p g i", i=G).unsqueeze(2)
            dve.memset(same[:, :, :, 0], 0.0)
            dve.memset(same[:, 0:1, :, 1], 0.0)
            dve.tensor_tensor(same[:, 1:, :, 1], by_group[:, 1:, :, 0].broadcast_to([P, SG - 1, H]),
                              by_group[:, :SG - 1, :, G - 1].broadcast_to([P, SG - 1, H]), ALU.is_gt)
            dve.tensor_tensor(same[:, :, :, 2:], by_group[:, :, :, 1:].broadcast_to([P, SG, H, G - 1]),
                              by_group[:, :, :, :G - 1].broadcast_to([P, SG, H, G - 1]), ALU.is_gt).then_inc(s("v_set"), 1)
            dve.wait_ge(s("v_set"), 5)
            same_flat = same.rearrange("p g h i -> p (g h i)")
            dve.wait_ge(s("ends_stepped"), ST // U)
            dve.tensor_tensor(dst_local[:], ends_step[:, 1, :], d128[:], ALU.subtract).then_inc(s("dst_stepped"), 1)
            dve.wait_ge(s("dst_stepped"), 1)

            def er_sum(g, slot):
                dve.wait_ge(s("er_mm"), g + 1)
                dve.tensor_reduce(er_got[:, slot, :, 1:], bank[slot][:, 0:G * 3 * H].rearrange("p (g i h) -> p h g i", g=G, i=3),
                                  AX.X, ALU.add).then_inc(s("er_got"), 1)
                if later(g, 1):
                    dve.wait_ge(s("er_summed"), g)
                    dve.tensor_copy(er_got[:, slot, :, 0], er_run[:, 1 - slot, :, G]).then_inc(s("er_carried"), 1)
                    dve.wait_ge(s("er_carried"), g)
                dve.wait_ge(s("er_got"), g + 1)
                wait_past(dve, s("er_kept"), g, 2)
                n = H * (1 + G)
                dve.tensor_tensor_scan(er_run[:, slot].rearrange("p h i -> p (h i)"), same_flat[:, bass.ds(g * n, n)],
                                       er_got[:, slot].rearrange("p h i -> p (h i)"), 0.0, ALU.mult, ALU.add).then_inc(s("er_summed"), 1)

            def expand(g, slot, r):
                wait_past(dve, s("er_tp"), g, 2)
                dve.tensor_tensor(hot_b[:, slot], col_no[:].unsqueeze(1).broadcast_to([P, G, P]),
                                  dst_local[:, bass.ds(g * G, G)].unsqueeze(2).broadcast_to([P, G, P]), ALU.is_equal)\
                    .then_inc(s("er_hot"), 1)
                if later(g, 2):
                    er_sum(g - 2, slot)
            turns(dve, expand, SG, peeled=2)
            for g in (SG - 2, SG - 1):
                er_sum(g, g % 2)

            dve.wait_ge(s("dst_scan_in"), 16 * CH)
            dve.wait_ge(s("er_summed"), SG)
            dve.tensor_tensor(t_pen[:, 1:CL], dst_scan[:, 1:CL], dst_scan[:, 0:CL - 1], ALU.not_equal).then_inc(s("scan_v"), 1)
            dve.tensor_copy(edge_first[:, 0:1], dst_scan[:, 0:1])
            dve.tensor_copy(edge_first[:, 1:2], dst_scan[:, CL - 1:CL])
            dve.memset(t_pen[:, 0:1], 0.0)
            dve.memset(t_pen[:, CL:CL + 1], 0.0).then_inc(s("scan_v"), 1)
            dve.wait_ge(s("scan_v"), 2)
            dve.wait_ge(s("er_kept"), SG)
            dve.wait_ge(s("el_kept"), CJ)
            dve.wait_ge(s("tp_el"), -(-CJ // 4))
            dve.tensor_tensor(e_el, e_el, e_er, ALU.add).then_inc(s("sm"), 1)
            dve.wait_ge(s("pen_ready"), 1)
            dve.wait_ge(s("tp_el_out"), -(-CJ // 4))
            dve.tensor_tensor_scan(t_run, t_pen[:, 0:CL], t_el, -BIG, ALU.add, ALU.max).then_inc(s("scan_v"), 1)
            dve.wait_ge(s("scan_v"), 3)
            dve.tensor_copy(edge_first[:, 2:3], t_run[:, CL - 1:CL]).then_inc(s("scan_ends"), 1)

            def R(i):
                return row[0:1, i, :]
            FIRST, LAST, RUN, CONN, WHOLE, PEN_IN, PEN_W, OUT_, IN_, PEN_INB, PEN_WB = range(11)
            hc = lambda a: a.rearrange("o (h c) -> o h c", c=CH)
            n = 0

            def link(ins):
                nonlocal n
                n += 1
                ins.then_inc(s("row_v"), 1)
                dve.wait_ge(s("row_v"), n)
            dve.wait_ge(s("ends_tp"), 1)
            for i in range(3):
                link(dve.tensor_copy(hc(R(i)), bank[5][0:1, i * P:(i + 1) * P].rearrange("o (c h) -> o h c", h=H)))
            link(dve.memset(R(CONN), 0.0))
            link(dve.tensor_tensor(hc(R(CONN))[:, :, 1:CH], hc(R(FIRST))[:, :, 1:CH], hc(R(LAST))[:, :, 0:CH - 1], ALU.is_equal))
            link(dve.tensor_tensor(R(WHOLE), R(FIRST), R(LAST), ALU.is_equal))
            link(dve.tensor_scalar(R(PEN_IN), R(CONN), BIG, -BIG, ALU.mult, ALU.add))
            link(dve.tensor_tensor(R(PEN_W), R(CONN), R(WHOLE), ALU.mult))
            link(dve.tensor_scalar(R(PEN_W), R(PEN_W), BIG, -BIG, ALU.mult, ALU.add))
            link(dve.memset(R(PEN_INB), -BIG))
            link(dve.tensor_copy(hc(R(PEN_INB))[:, :, 0:CH - 1], hc(R(PEN_IN))[:, :, 1:CH]))
            link(dve.tensor_scalar(R(PEN_WB), R(WHOLE), BIG, -BIG, ALU.mult, ALU.add))
            link(dve.tensor_tensor(R(PEN_WB), R(PEN_WB), R(PEN_INB), ALU.min))
            link(dve.tensor_tensor_scan(R(OUT_), R(PEN_W), R(RUN), -BIG, ALU.add, ALU.max))
            link(dve.memset(R(IN_), -BIG))
            link(dve.tensor_tensor(hc(R(IN_))[:, :, 1:CH], hc(R(OUT_))[:, :, 0:CH - 1], hc(R(PEN_IN))[:, :, 1:CH], ALU.add))
            dve.tensor_scalar_max(R(11).rearrange("o (c h) -> o h c", h=H), hc(R(IN_)), -BIG).then_inc(s("row_in"), 1)
            dve.wait_ge(s("row_back"), 1)
            dve.tensor_copy(col[:, 0:1], bank[6][:, 0:1]).then_inc(s("scan_v"), 1)
            dve.wait_ge(s("scan_v"), 4)
            dve.tensor_tensor_scan(t_run, t_pen[:, 0:CL], t_el, col[:, 0:1], ALU.add, ALU.max).then_inc(s("scan_v"), 1)
            dve.wait_ge(s("scan_v"), 5)
            dve.tensor_tensor_scan(t_el[:, ::-1], t_pen[:, 1:CL + 1][:, ::-1], t_run[:, ::-1], -BIG, ALU.add, ALU.max)\
                .then_inc(s("scan_v"), 1)
            dve.wait_ge(s("scan_v"), 6)
            dve.tensor_copy(edge_first[:, 3:4], t_el[:, 0:1]).then_inc(s("scan_ends"), 1)
            dve.wait_ge(s("ends_tp"), 2)
            link(dve.tensor_copy(hc(R(RUN)), bank[5][0:1, 0:P].rearrange("o (c h) -> o h c", h=H)))
            link(dve.tensor_tensor_scan(R(OUT_)[:, ::-1], R(PEN_WB)[:, ::-1], R(RUN)[:, ::-1], -BIG, ALU.add, ALU.max))
            link(dve.memset(R(IN_), -BIG))
            link(dve.tensor_tensor(hc(R(IN_))[:, :, 0:CH - 1], hc(R(OUT_))[:, :, 1:CH], hc(R(PEN_INB))[:, :, 0:CH - 1], ALU.add))
            dve.tensor_scalar_max(R(11).rearrange("o (c h) -> o h c", h=H), hc(R(IN_)), -BIG).then_inc(s("row_in"), 1)
            dve.wait_ge(s("row_back"), 2)
            dve.tensor_copy(col[:, 1:2], bank[6][:, 0:1]).then_inc(s("scan_v"), 1)
            dve.wait_ge(s("scan_v"), 7)
            dve.tensor_tensor_scan(t_el[:, ::-1], t_pen[:, 1:CL + 1][:, ::-1], t_run[:, ::-1], col[:, 1:2], ALU.add, ALU.max)\
                .then_inc(s("scan_done"), 1)

            dve.wait_ge(s("sm"), 1)
            dve.scalar_tensor_tensor(e_el, e_el, NEG_SLOPE, e_el, ALU.mult, ALU.max).then_inc(s("sm"), 1)
            dve.wait_ge(s("tp_m_out"), -(-CJ // 4))
            dve.tensor_tensor(e_m, e_m, e_er, ALU.add).then_inc(s("sm"), 1)
            dve.wait_ge(s("sm"), 3)
            dve.scalar_tensor_tensor(e_m, e_m, NEG_SLOPE, e_m, ALU.mult, ALU.max).then_inc(s("sm"), 1)
            dve.wait_ge(s("sm"), 4)
            dve.tensor_tensor(e_el, e_el, e_m, ALU.subtract).then_inc(s("sm_diff"), 1)
            dve.wait_ge(s("p_ready"), 1)

            places = []
            def step(t, j, r):
                if j % V == 0:
                    wait_past(dve, s("step_mm"), t, V + 1)
                    dve.tensor_tensor(hot[:, j // V % 2], col_no[:].unsqueeze(1).broadcast_to([P, V, P]),
                                      dst_local[:, bass.ds(t, V)].unsqueeze(2).broadcast_to([P, V, P]), ALU.is_equal)
                if j % V == 0:
                    places[:] = looked_up(ENGINE.DVE, k_tab, t, V, ET - 1)
                k, b = places[j % V], j % V
                wait_past(dve, s("step_mm"), t, V)
                dve.tensor_copy(pv[:, b, D:D + H], e_el_flat[:, bass.ds(k * H, H)])
                dve.wait_ge(gathered[j], (r + 1) * 16)
                dve.tensor_tensor(pv[:, b, 0:D].rearrange("p (h f) -> p h f", h=H),
                                  vg[:, j, :].rearrange("p (h f) -> p h f", h=H),
                                  e_el_flat[:, bass.ds(k * H, H)].unsqueeze(2).broadcast_to([P, H, HF]),
                                  ALU.mult).then_inc(s("step_pv"), 1)
            turns(dve, step, ST, U)

            def w_lo(lo, w, hi, c, n):
                dve.wait_ge(s("w_hi"), n)
                m = w.shape[1] // 4
                dve.tensor_tensor(by_part(lo[c], m), w[:, c * m:(c + 1) * m], by_part(hi[c], m).bitcast(F32), ALU.subtract)\
                    .then_inc(s("w_lo"), 1)

            def join(t, j, r):
                slot = j % 2
                dve.wait_ge(s(f"jn_a{slot}"), r * 32 + 16 * (j // 2 + 1))
                if later(t, 1):
                    dve.wait_ge(s("jn_n"), t * 4)
                dve.tensor_scalar_max(den[:], da[:, slot, D:D + H], 1e-16).then_inc(s("jn_n"), 1)
                dve.wait_ge(s(f"jn_b{j}"), (r + 1) * 16)
                dve.tensor_tensor(dx[:, j, :], dx[:, j, :], bo_all[:], ALU.add).then_inc(s("jn_n"), 1)
                dve.wait_ge(s("jn_n"), t * 4 + 1)
                dve.reciprocal(den[:], den[:]).then_inc(s("jn_n"), 1)
                dve.wait_ge(s("jn_n"), t * 4 + 3)
                by_head = da[:, slot, 0:D].rearrange("p (h f) -> p h f", h=H)
                dve.tensor_tensor(by_head, by_head, den[:].unsqueeze(2).broadcast_to([P, H, HF]), ALU.mult).then_inc(s("jn_n"), 1)
                dve.wait_ge(s("jn_n"), t * 4 + 4)
                dve.tensor_tensor(dx[:, j, :], da[:, slot, 0:D], dx[:, j, :], ALU.add).then_inc(s("jn_x"), 1)
                wait_past(dve, s("jn_ag"), t, 1)
                dve.wait_ge(s("jn_x"), t + 1)
                dve.bn_stats(bn[:], dx[:, j, :]).then_inc(s("jn_bn"), 1)
                apart(dve, s("jn_bn"), t + 1)
                wait_past(dve, s("ex_xn"), t, 1)
                dve.bn_aggr(ag[:], bn[:]).then_inc(s("jn_ag"), 1)
                dve.wait_ge(s("jn_inv"), t + 1)
                dve.tensor_scalar(da[:, slot, 0:D], dx[:, j, :], ag[:, 0:1], inv[:], ALU.subtract, ALU.mult)\
                    .then_inc(s("ex_xn"), 1)

            def x_lo(t, slot):
                dve.wait_ge(s("ex_xhi"), t + 1)
                dve.tensor_tensor(xt_lo[:, slot, :], bank[slot][:], xt_hi[:, slot, :].bitcast(F32), ALU.subtract)\
                    .then_inc(s("ex_xt"), 1)

            def gates(t, slot):
                n = 0

                def link(ins):
                    nonlocal n
                    n += 1
                    ins.then_inc(s("ex_g"), 1)
                    apart(dve, s("ex_g"), t * 10 + n)
                dve.wait_ge(s("ex_lg"), t + 1)
                link(dve.tensor_copy(lg[:], bank[6][:, 0:X]))
                link(dve.tensor_tensor(lg[:], lg[:], bank[6][:, X:2 * X], ALU.add))
                link(dve.max(top[:], lg[:]))
                dve.tensor_scalar(nmax[:], top[:, 0:1], -1.0, None, ALU.mult).then_inc(s("ex_nmax"), 1)
                dve.wait_ge(s("ex_exp"), t + 1)
                link(dve.reciprocal(psum_[:], psum_[:]))
                link(dve.tensor_scalar(pr[:], pr[:], psum_[:], None, ALU.mult))
                link(dve.max(ptop[:], pr[:]))
                link(dve.max_index(pidx[:], ptop[:], pr[:]))
                link(dve.tensor_copy(pidf[:], pidx[:]))
                dve.scalar_tensor_tensor(ga[:], col_no[:, 0:X], pidf[:, 0:1], pr[:], ALU.is_equal, ALU.mult)
                link(dve.scalar_tensor_tensor(gb[:], col_no[:, 0:X], pidf[:, 1:2], pr[:], ALU.is_equal, ALU.mult))
                link(dve.tensor_tensor(gate[:, slot, :], ga[:], gb[:], ALU.add))

            def gated(n, q, slot):
                dve.wait_ge(s("ex_gelu"), n + 1)
                by_expert = hs[:, q % 2, :].rearrange("p (e f) -> p e f", e=2)
                dve.tensor_tensor(by_expert, by_expert, gate[:, slot, 2 * q:2 * q + 2].unsqueeze(2).broadcast_to([P, 2, XF]),
                                  ALU.mult).then_inc(s("ex_hs"), 1)

            def h_lo(n, q):
                dve.wait_ge(s("ex_hhi"), n + 1)
                dve.tensor_tensor(ht_lo[:, q % 2, :], bank[4][:], ht_hi[:, q % 2, :].bitcast(F32), ALU.subtract)\
                    .then_inc(s("ex_ht"), 1)

            def output(t, j):
                dve.wait_ge(s("ex_ymm"), 4 * t + 4)
                dve.tensor_tensor(dx[:, j, :], dx[:, j, :], bank[5][:], ALU.add).then_inc(s("ex_out"), 1)
            dve.wait_ge(s("experts_in"), EXPERT_DMAS * 16)
            dve.wait_ge(s("w_hi"), 1)
            dve.tensor_tensor(wr_r[:, :, X:2 * X], wr, wr_r[:, :, 0:X].bitcast(F32), ALU.subtract).then_inc(s("w_lo"), 1)
            w_lo(w1_lo, w1, w1_hi, 0, 2)
            w_lo(w1_lo, w1, w1_hi, 1, 3)
            join(0, 0, 0)
            w_lo(w1_lo, w1, w1_hi, 2, 4)
            w_lo(w1_lo, w1, w1_hi, 3, 5)
            x_lo(0, 0)
            gates(0, 0)
            gated(0, 0, 0)
            w_lo(w2_lo, w2, w2_hi, 0, 6)

            def moe(t, j, r):
                more = not_last(t)
                slot, nslot = j % 2, (j + 1) % 2
                for q in range(4):
                    h_lo(t * 4 + q, q)
                    if q < 3 and not later(t, 1):
                        w_lo(w2_lo, w2, w2_hi, q + 1, 7 + q)
                    if q == 0:
                        if later(t, 1):
                            output(t - 1, (j - 1) % 4)
                    if q == 1 and more:
                        x_lo(t + 1, nslot)
                    if q < 3:
                        gated(t * 4 + (q + 1), q + 1, slot)
                    elif more:
                        gated(t * 4 + 4, 0, nslot)
                    if q == 0 and more:
                        join(t + 1, (j + 1) % 4, (r if j < 3 else r + 1))
                    if q == 2 and more:
                        gates(t + 1, nslot)
            turns(dve, moe, NT, 4)
            output(NT - 1, (NT - 1) % 4)

        @block.tensor
        def _(pe):
            def product(dst, pairs, opened=True, closed=True):
                n = len(pairs)
                for i, (a, b) in enumerate(pairs):
                    last = pe.matmul(dst, a, b, start=(opened and i == 0), stop=(closed and i == n - 1))
                return last

            def transposed(dst, src, n=KC):
                for c in range(n):
                    last = pe.transpose(dst[:, c * P:(c + 1) * P], src[:, c * P:(c + 1) * P], ident[:])
                return last

            def split_product(dst, parts, opened=True, closed=True):
                return product(dst, [pair for a, a_lo, b, b_lo in parts for pair in ((a, b), (a, b_lo), (a_lo, b))],
                               opened, closed)

            pe.wait_ge(s("ident_ready"), 1)
            pe.wait_ge(s("tab_begun"), 1)
            for i in range(2):
                last = product(bank[4 + i][:, 0:ST // 2], [(ones[0:NT - 1, :], s_cnt[0:NT - 1, i * (ST // 2):(i + 1) * (ST // 2)])])
            last.then_inc(s("tab_mm"), 1)
            pe.wait_ge(s("weights_in"), WEIGHT_DMAS * 16)
            for c in range(KC):
                for j in range(8):
                    last = product(bank[c][:, j * HF:(j + 1) * HF], [(s_wqt[:, j, c * P:(c + 1) * P], r_diag)])
                last.then_inc(s("fold_mm"), 1)
            pe.wait_ge(s("fold_out"), KC)
            pe.wait_ge(s("fold_v"), 14)

            def score(t, slot):
                pe.wait_ge(s("sc_xt"), t + 1)
                wait_past(pe, s("sc_out"), t, 2)
                product(bank[2 + slot][:, 0:2 * H], [(xt[:, slot, c * P:(c + 1) * P], wlr[:, c, :]) for c in range(KC)])\
                    .then_inc(s("sc_mm"), 1)

            def scores(t, slot, r):
                pe.wait_ge(s("sc_xn"), t + 1)
                wait_past(pe, s("sc_xt"), t, 2)
                transposed(bank[slot], xn2[slot]).then_inc(s("sc_tp"), 1)
                if later(t, 1):
                    score(t - 1, 1 - slot)
            turns(pe, scores, peeled=2)
            score(NT - 1, 0)
            pe.wait_ge(s("sc_out"), NT)

            def x_chunk(slot, c):
                return xp_hi[:, slot, c * P:(c + 1) * P], xp_lo[:, slot, c * P:(c + 1) * P]

            def projected(dst, slot, hi, lo, t, n):
                if not later(t, 1):
                    pe.wait_ge(s("pw_lo"), n)
                return split_product(dst, [(*x_chunk(slot, c), hi[:, c, :], lo[:, c, :]) for c in range(KC)])

            def kv(t):
                pe.wait_ge(s("pj_mvs"), t + 1)
                pe.wait_ge(s("pj_kf"), t + 1)
                wait_past(pe, s("pj_kva"), t, 1)
                wait_past(pe, s("pj_qf"), t, 1)
                transposed(bank[5], feat, 2)
                kf = feat[:, 2 * P:4 * P]
                for j in range(KC):
                    product(bank[6][:, j * HF:(j + 1) * HF], [(mv[:, j * P:(j + 1) * P], kf[:, j * HF:(j + 1) * HF])])
                for c in range(2):
                    last = product(bank[6][:, KC * HF + c:KC * HF + c + 1],
                                   [(kf[:, c * P:(c + 1) * P], real_row[:, bass.ds(t, 1)])])
                last.then_inc(s("pj_kv"), 1)

            def turn_over(t, slot):
                pe.wait_ge(s("pj_xn"), t + 1)
                wait_past(pe, s("pj_xt"), t, 2)
                transposed(bank[slot], xn).then_inc(s("pj_tp"), 1)

            def proj(t, slot, r):
                pe.wait_ge(s("pj_xt"), t + 1)
                wait_past(pe, s("pj_vout"), t, 1)
                projected(bank[2][:], slot, wv_hi, wv_lo, t, 1).then_inc(s("pj_v"), 1)
                if later(t, 1):
                    kv(t - 1)
                projected(bank[3][:], slot, wmv_hi, wmv_lo, t, 2).then_inc(s("pj_mv"), 1)
                if not_last(t):
                    turn_over(t + 1, 1 - slot)
                projected(bank[4][:], slot, wqk_hi, wqk_lo, t, 3).then_inc(s("pj_q"), 1)
            turn_over(0, 0)
            turns(pe, proj)
            kv(NT - 1)

            pe.wait_ge(s("g_in"), 1)
            pe.wait_ge(s("wo_in"), 16)
            for c in range(2):
                last = product(bank[c][:], [(kvt_diag[:, j, :], wo[:, j, :]) for j in (2 * c, 2 * c + 1)])
            last.then_inc(s("g_mm"), 1)
            pe.wait_ge(s("g_out"), 2)

            def mixed(t, slot):
                pe.wait_ge(s("mx_qn"), t + 1)
                wait_past(pe, s("mx_out"), t, 2)
                product(bank[2 + slot][:], [(qn[slot][:, c, :], g_mat[:, c, :]) for c in range(2)]).then_inc(s("mx_mm"), 1)

            def mix(t, slot, r):
                wait_past(pe, s("mx_n1"), t, 2)
                for c in range(2):
                    last = product(bank[slot][:, c * P:(c + 1) * P], [(ks_diag[:, c, :], q_feat[:, c, bass.ds(t * P, P)])])
                last.then_inc(s("mx_norm"), 1)
                if later(t, 1):
                    mixed(t - 1, 1 - slot)
            turns(pe, mix, peeled=2)
            mixed(NT - 1, 0)

            def er_of(g, slot):
                pe.wait_ge(s("er_hot_t"), g + 1)
                wait_past(pe, s("er_got"), g, 2)
                for i, d in enumerate(looked_up(ENGINE.PE, d_tab, g * G, G, NT - 1)):
                    last = product(bank[slot][:, i * 3 * H:(i + 1) * 3 * H],
                                   [(hot_t[:, slot, i * P:(i + 1) * P], er_flat[:, bass.ds(d * 3 * H, 3 * H)])])
                last.then_inc(s("er_mm"), 1)

            def expand(g, slot, r):
                pe.wait_ge(s("er_hot"), g + 1)
                wait_past(pe, s("er_hot_t"), g, 2)
                for i in range(G):
                    last = pe.transpose(turned_hot[slot][:, i * P:(i + 1) * P], hot_b[:, slot, i, :], ident_b[:])
                last.then_inc(s("er_tp"), 1)
                if later(g, 1):
                    er_of(g - 1, 1 - slot)
            pe.wait_ge(s("mx_out"), NT)
            turns(pe, expand, SG, peeled=2)
            er_of(SG - 1, 1)
            pe.wait_ge(s("er_summed"), SG)

            pe.wait_ge(s("el_kept"), CJ)
            for g in range(-(-CJ // 4)):
                if g >= 4:
                    pe.wait_ge(s("tp_el_out"), g - 3)
                for i in range(min(4, CJ - 4 * g)):
                    last = pe.transpose(bank[g % 4][:, i * P:(i + 1) * P], e_el_flat[:, (4 * g + i) * P:(4 * g + i + 1) * P], ident[:])
                last.then_inc(s("tp_el"), 1)
            pe.wait_ge(s("scan_ends"), 1)
            for i in range(3):
                last = pe.transpose(bank[5][0:1, i * P:(i + 1) * P], edge_first[:, i:i + 1], ident[:])
            last.then_inc(s("ends_tp"), 1)
            in_row = row[0:1, 11, :]
            pe.wait_ge(s("row_in"), 1)
            product(bank[6][:, 0:1], [(in_row, ones[0:1, 0:1])]).then_inc(s("row_back"), 1)
            pe.wait_ge(s("scan_ends"), 2)
            pe.transpose(bank[5][0:1, 0:P], edge_first[:, 3:4], ident[:]).then_inc(s("ends_tp"), 1)
            pe.wait_ge(s("row_in"), 2)
            product(bank[6][:, 0:1], [(in_row, ones[0:1, 0:1])]).then_inc(s("row_back"), 1)
            pe.wait_ge(s("scan_done"), 1)
            pe.wait_ge(s("tp_el_out"), -(-CJ // 4))
            for g in range(-(-CJ // 4)):
                if g >= 4:
                    pe.wait_ge(s("tp_m_out"), g - 3)
                for i in range(min(4, CJ - 4 * g)):
                    last = pe.transpose(bank[g % 4][:, i * P:(i + 1) * P], t_el[:, (4 * g + i) * P:(4 * g + i + 1) * P], ident[:])
                last.then_inc(s("tp_m"), 1)
            pe.wait_ge(s("tp_m_out"), -(-CJ // 4))

            def empty(opened, closed):
                for i in range(2):
                    last = pe.matmul(bank[i][:, 0:HALF], zeros[0:1, 0:P], zeros[0:1, 0:HALF], start=opened, stop=closed)
                return last

            ends = []

            def step(t, j, r):
                if j % V == 0:
                    ends[:] = looked_up(ENGINE.PE, turn_tab, t, V, NT)
                turn = ends[j % V]
                pe.wait_ge(s("step_pv"), t + 1)
                for i in range(2):
                    last = pe.matmul(bank[i][:, 0:HALF], hot[:, j // V % 2, j % V, :], pv[:, j % V, i * HALF:(i + 1) * HALF],
                                     start=False, stop=False)
                last.then_inc(s("step_mm"), 1)
                with pe.If(turn):
                    empty(False, True).then_inc(s("tile_sum"), 1)
                    pe.wait_ge(s("tile_out"), turn)
                    empty(True, False)
            empty(True, False)
            turns(pe, step, ST, U)
            empty(False, True)

            def turn_x(t, slot):
                pe.wait_ge(s("ex_xn"), t + 1)
                wait_past(pe, s("ex_xt"), t, 2)
                transposed(bank[slot], da[:, slot, 0:D]).then_inc(s("ex_tp"), 1)

            def x_parts(slot, c):
                return xt_hi[:, slot, c * P:(c + 1) * P], xt_lo[:, slot, c * P:(c + 1) * P]

            def logits(t, slot):
                if later(t, 1):
                    pe.wait_ge(s("ex_g"), (t - 1) * 10 + 2)
                product(bank[6][:, 0:2 * X], [(part, wr_r[:, c, :]) for c in range(KC) for part in x_parts(slot, c)])\
                    .then_inc(s("ex_lg"), 1)

            def hidden(n, q, slot):
                wait_past(pe, s("ex_gelu"), n, 2)
                cols = slice(q * D, (q + 1) * D)
                split_product(bank[2 + q % 2][:], [(*x_parts(slot, c), w1_hi[c][:, cols], w1_lo[c][:, cols]) for c in range(KC)])\
                    .then_inc(s("ex_hmm"), 1)

            def turned(n, q):
                pe.wait_ge(s("ex_hs"), n + 1)
                wait_past(pe, s("ex_ht"), n, 1)
                transposed(bank[4], hs[:, q % 2, :]).then_inc(s("ex_htp"), 1)

            def summed(n, q, t):
                pe.wait_ge(s("ex_ht"), n + 1)
                if not later(t, 1):
                    pe.wait_ge(s("w_lo"), 6 + q)
                if q == 0:
                    wait_past(pe, s("ex_out"), t, 1)
                split_product(bank[5][:], [(ht_hi[:, q % 2, c * P:(c + 1) * P], ht_lo[:, q % 2, c * P:(c + 1) * P],
                                            w2_hi[q][:, c, :], w2_lo[q][:, c, :]) for c in range(KC)],
                              opened=(q == 0), closed=(q == 3)).then_inc(s("ex_ymm"), 1)
            turn_x(0, 0)
            pe.wait_ge(s("ex_xt"), 1)
            pe.wait_ge(s("w_lo"), 5)
            logits(0, 0)
            hidden(0, 0, 0)
            hidden(1, 1, 0)
            turned(0, 0)

            def moe(t, j, r):
                more = not_last(t)
                slot, nslot = j % 2, (j + 1) % 2
                for q in range(4):
                    n = t * 4 + q
                    if q == 2 and more:
                        pe.wait_ge(s("ex_xt"), t + 2)
                    if q < 2 or more:
                        hidden(t * 4 + (q + 2), (q + 2) % 4, slot if q < 2 else nslot)
                    if q == 1 and more:
                        turn_x(t + 1, nslot)
                    if q == 2 and more:
                        logits(t + 1, nslot)
                    summed(n, q, t)
                    if q < 3 or more:
                        turned(t * 4 + (q + 1), (q + 1) % 4)
            turns(pe, moe, NT, 4)


_OUT = (NP, D)


def kernel(**inputs):
    import numpy as _np
    import concourse.bacc as _bacc
    from concourse import mybir as _mybir
    from concourse.bass_utils import run_bass_kernel_spmd as _run

    def padded(a, n):
        b = _np.zeros((n,) + a.shape[1:], a.dtype)
        b[:a.shape[0]] = a
        return b

    a = {k: _np.ascontiguousarray(v) for k, v in inputs.items()}
    def columns(edges):
        return edges.reshape(CH, CJ, P).transpose(2, 1, 0).reshape(P, ET)

    src = padded(a["src"], EP)
    dst = _np.full((EP,), 2 * NP, a["dst"].dtype)
    dst[:E] = a["dst"]
    w_qkv = a["L0_mix_W_qkv"]
    laid = {
        "x": padded(a["x"], NP),
        "src_cols": columns(src), "dst_cols": columns(dst), "dst_rows": dst.reshape(CH, CL),
        "w_src": a["L0_gnn_W_src"], "b_src": a["L0_gnn_b_src"].reshape(1, D),
        "w_dst": a["L0_gnn_W_dst"], "b_dst": a["L0_gnn_b_dst"].reshape(1, D),
        "w_val": a["L0_gnn_W_val"], "b_val": a["L0_gnn_b_val"].reshape(1, D),
        "attn_l": a["L0_gnn_attn_l"].reshape(1, D), "attn_r": a["L0_gnn_attn_r"].reshape(1, D),
        "w_qk_t": w_qkv[:, :2 * D].T, "w_v": w_qkv[:, 2 * D:],
        "r_mat": a["L0_mix_random_matrix"], "w_out": a["L0_mix_W_out"],
        "b_out": a["L0_mix_b_out"].reshape(1, D), "w_r": a["L0_ffn_Wr"],
        "w_1": a["L0_ffn_W1"], "w_2": a["L0_ffn_W2"],
    }
    nc = _bacc.Bacc("TRN2", target_bir_lowering=False, num_devices=1)
    arrays, args = {}, {}
    for name, v in laid.items():
        v = _np.ascontiguousarray(v)
        arrays[f"in_{name}"] = v
        args[name] = nc.dram_tensor(f"in_{name}", v.shape, _mybir.dt.from_np(v.dtype), kind="ExternalInput").ap()
    args["out"] = nc.dram_tensor("out_0", _OUT, _mybir.dt.float32, kind="ExternalOutput").ap()
    gps_layer(nc, **args)
    r = _run(nc, [arrays], core_ids=[0])
    return r.results[0]["out_0"][:N]
```
